# Optimizing a Trainium2 kernel written in Bass

```python
import numpy as np
import jax
import jax.numpy as jnp

def _softmax(x, axis=-1):
    return jax.nn.softmax(x, axis=axis)

def _gelu(x):
    return jax.nn.gelu(x, approximate=True)

def _silu(x):
    return jax.nn.silu(x)

def _sigmoid(x):
    return jax.nn.sigmoid(x)

def _layernorm(x, axis=-1, eps=1e-05):
    m = jnp.mean(x, axis=axis, keepdims=True)
    v = jnp.var(x, axis=axis, keepdims=True)
    return (x - m) / jnp.sqrt(v + eps)

def _scatter_add(tgt, idx, src, axis=0):
    return tgt.at[idx].add(src)

def _segment_sum(src, seg, n):
    return jax.ops.segment_sum(src, seg, n)
kernel_name = 'mk_vit_tower_d2_tok_img512_r4_c2bea9'

def setup_inputs(seed: int=0):
    np.random.seed(seed)
    _w = jnp.asarray

    def _rec_inputs():
        import jax
        import jax.numpy as jnp
        _rk = jax.random.key(seed)
        x = -0.000356955 + 1 * jax.random.normal(jax.random.fold_in(_rk, 1), (32, 3, 96, 96), jnp.float32)
        return x
    x = _rec_inputs()

    def _L0_tok_setup():
        import jax, jax.numpy as jnp
        import numpy as np
        P = 16
        SHIFT = P // 2
        EPS = 1e-05

        def _shift2d(img, dy, dx):
            H, W = (img.shape[2], img.shape[3])
            pad = ((0, 0), (0, 0), (max(dy, 0), max(-dy, 0)), (max(dx, 0), max(-dx, 0)))
            z = jnp.pad(img, pad)
            return z[:, :, max(-dy, 0):max(-dy, 0) + H, max(-dx, 0):max(-dx, 0) + W]

        def _patchify(img):
            B, C, H, W = img.shape
            nH, nW = (H // P, W // P)
            t = img.reshape(B, C, nH, P, nW, P).transpose(0, 2, 4, 1, 3, 5)
            return t.reshape(B, nH * nW, C * P * P)
        key = jax.random.key(seed)
        ks = jax.random.split(key, 8)
        B, C, H, Wd = (128, 3, 224, 224)
        embed_dim = 128
        d_main = embed_dim // 2
        d_shift = embed_dim // 8
        fan_in = C * P * P
        std = 0.02
        x = jax.random.normal(ks[0], (B, C, H, Wd), dtype=jnp.float32)
        W_main = jax.random.normal(ks[1], (d_main, fan_in), dtype=jnp.float32) * std
        b_main = jnp.zeros((d_main,), dtype=jnp.float32)
        W_sx = jax.random.normal(ks[2], (d_shift, fan_in), dtype=jnp.float32) * std
        b_sx = jnp.zeros((d_shift,), dtype=jnp.float32)
        W_sy = jax.random.normal(ks[3], (d_shift, fan_in), dtype=jnp.float32) * std
        b_sy = jnp.zeros((d_shift,), dtype=jnp.float32)
        ln_g = jnp.ones((embed_dim,), dtype=jnp.float32)
        ln_b = jnp.zeros((embed_dim,), dtype=jnp.float32)
        return {'x': x, 'W_main': W_main, 'b_main': b_main, 'W_sx': W_sx, 'b_sx': b_sx, 'W_sy': W_sy, 'b_sy': b_sy, 'ln_g': ln_g, 'ln_b': ln_b}
    _L0_tok_all = _L0_tok_setup()
    _L0_tok_in = {k: v for k, v in _L0_tok_all.items() if k in ('W_main', 'b_main', 'W_sx', 'b_sx', 'W_sy', 'b_sy', 'ln_g', 'ln_b')}
    del _L0_tok_all

    def _L0_attn_setup():
        import jax, jax.numpy as jnp
        import numpy as np
        D_MODEL = 128
        NHEAD = 8
        D_FF = 512
        EPS = 1e-05

        def _layernorm(x, gamma, beta):
            mu = jnp.mean(x, axis=-1, keepdims=True)
            var = jnp.mean(jnp.square(x - mu), axis=-1, keepdims=True)
            return (x - mu) * jax.lax.rsqrt(var + EPS) * gamma + beta

        def _rope(x, cos, sin):
            d = x.shape[-1]
            x1, x2 = (x[..., :d // 2], x[..., d // 2:])
            return jnp.concatenate([x1 * cos - x2 * sin, x2 * cos + x1 * sin], axis=-1)
        key = jax.random.key(seed)
        ks = jax.random.split(key, 12)
        B, S = (2, 1024)
        s = 0.02
        inp = {'src': jax.random.normal(ks[0], (B, S, D_MODEL), dtype=jnp.float32), 'Wq': jax.random.normal(ks[1], (D_MODEL, D_MODEL), dtype=jnp.float32) * s, 'Wk': jax.random.normal(ks[2], (D_MODEL, D_MODEL), dtype=jnp.float32) * s, 'Wv': jax.random.normal(ks[3], (D_MODEL, D_MODEL), dtype=jnp.float32) * s, 'Wo': jax.random.normal(ks[4], (D_MODEL, D_MODEL), dtype=jnp.float32) * s, 'W1': jax.random.normal(ks[5], (D_FF, D_MODEL), dtype=jnp.float32) * s, 'b1': jnp.zeros((D_FF,), dtype=jnp.float32), 'W2': jax.random.normal(ks[6], (D_MODEL, D_FF), dtype=jnp.float32) * s, 'b2': jnp.zeros((D_MODEL,), dtype=jnp.float32), 'g1': jnp.ones((D_MODEL,), dtype=jnp.float32), 'be1': jnp.zeros((D_MODEL,), dtype=jnp.float32), 'g2': jnp.ones((D_MODEL,), dtype=jnp.float32), 'be2': jnp.zeros((D_MODEL,), dtype=jnp.float32)}
        return inp
    _L0_attn_all = _L0_attn_setup()
    _L0_attn_in = {k: v for k, v in _L0_attn_all.items() if k in ('Wq', 'Wk', 'Wv', 'Wo', 'W1', 'b1', 'W2', 'b2', 'g1', 'be1', 'g2', 'be2')}
    del _L0_attn_all

    def _L0_ffn_setup():
        import jax, jax.numpy as jnp
        import numpy as np
        T = 128
        B = 64
        C = 256

        def _triu_apply(x, W, b):
            Wm = jnp.tril(W)
            return jnp.einsum('bct,st->bcs', x, Wm) + b
        key = jax.random.key(seed)
        ks = jax.random.split(key, 5)
        x = jax.random.normal(ks[0], (B, C, T), dtype=jnp.float32)
        scale = 1.0 / jnp.sqrt(jnp.arange(1, T + 1, dtype=jnp.float32))[:, None]
        W1 = jax.random.uniform(ks[1], (T, T), jnp.float32, -1.0, 1.0) * scale
        b1 = jax.random.uniform(ks[2], (T,), jnp.float32, -1.0, 1.0) * scale[:, 0]
        W2 = jax.random.uniform(ks[3], (T, T), jnp.float32, -1.0, 1.0) * scale
        b2 = jax.random.uniform(ks[4], (T,), jnp.float32, -1.0, 1.0) * scale[:, 0]
        return {'x': x, 'W1': W1, 'b1': b1, 'W2': W2, 'b2': b2}
    _L0_ffn_all = _L0_ffn_setup()
    _L0_ffn_in = {k: v for k, v in _L0_ffn_all.items() if k in ('W1', 'b1', 'W2', 'b2')}
    del _L0_ffn_all

    def _L1_attn_setup():
        import jax, jax.numpy as jnp
        import numpy as np
        B, S, D = (2, 512, 128)
        H = 8
        G = 4
        LAMBDA_INIT = 0.2
        EPS = 1e-05
        key = jax.random.key(seed)
        ks = jax.random.split(key, 16)
        n = jax.random.normal
        return {'x': n(ks[0], (B, S, D), jnp.float32), 'K1_w': n(ks[1], (D, D), jnp.float32) * 0.02, 'K1_b': n(ks[2], (D,), jnp.float32) * 0.02, 'Q1_w': n(ks[3], (D, D), jnp.float32) * 0.02, 'K2_w': n(ks[4], (D, D), jnp.float32) * 0.02, 'K2_b': n(ks[5], (D,), jnp.float32) * 0.02, 'Q2_w': n(ks[6], (D, D), jnp.float32) * 0.02, 'V_w': n(ks[7], (D, D), jnp.float32) * 0.02, 'lambda_q1': n(ks[8], (H, 1), jnp.float32), 'lambda_k1': n(ks[9], (H, 1), jnp.float32), 'lambda_q2': n(ks[10], (H, 1), jnp.float32), 'lambda_k2': n(ks[11], (H, 1), jnp.float32), 'gn_w': jnp.ones((D,), jnp.float32), 'gn_b': jnp.zeros((D,), jnp.float32), 'out_w': n(ks[12], (D, D), jnp.float32) * 0.02, 'out_b': n(ks[13], (D,), jnp.float32) * 0.02}
    _L1_attn_all = _L1_attn_setup()
    _L1_attn_in = {k: v for k, v in _L1_attn_all.items() if k in ('K1_w', 'K1_b', 'Q1_w', 'K2_w', 'K2_b', 'Q2_w', 'V_w', 'lambda_q1', 'lambda_k1', 'lambda_q2', 'lambda_k2', 'gn_w', 'gn_b', 'out_w', 'out_b')}
    del _L1_attn_all

    def _L1_ffn_setup():
        import jax, jax.numpy as jnp
        import numpy as np
        EPS = 1e-05
        NUM_HEADS = 8
        TOP_K = 2
        CAP_FACTOR = 2

        def layernorm(x, g, b):
            m = jnp.mean(x, axis=-1, keepdims=True)
            v = jnp.var(x, axis=-1, keepdims=True)
            return (x - m) * jax.lax.rsqrt(v + EPS) * g + b
        key = jax.random.key(seed)
        ks = jax.random.split(key, 16)
        B, S, H, E, F = (2, 512, 128, 64, 512)
        s = 0.02
        return {'x': jax.random.normal(ks[0], (B, S, H), jnp.float32), 'ln1_g': jnp.ones((H,), jnp.float32), 'ln1_b': jnp.zeros((H,), jnp.float32), 'wq': jax.random.normal(ks[1], (H, H), jnp.float32) * s, 'wk': jax.random.normal(ks[2], (H, H), jnp.float32) * s, 'wv': jax.random.normal(ks[3], (H, H), jnp.float32) * s, 'wo': jax.random.normal(ks[4], (H, H), jnp.float32) * s, 'ln2_g': jnp.ones((H,), jnp.float32), 'ln2_b': jnp.zeros((H,), jnp.float32), 'wr': jax.random.normal(ks[5], (H, E), jnp.float32) * s, 'w1': jax.random.normal(ks[6], (E, H, F), jnp.float32) * s, 'b1': jnp.zeros((E, F), jnp.float32), 'w2': jax.random.normal(ks[7], (E, F, H), jnp.float32) * s, 'b2': jnp.zeros((E, H), jnp.float32)}
    _L1_ffn_all = _L1_ffn_setup()
    _L1_ffn_in = {k: v for k, v in _L1_ffn_all.items() if k in ('ln1_g', 'ln1_b', 'wq', 'wk', 'wv', 'wo', 'ln2_g', 'ln2_b', 'wr', 'w1', 'b1', 'w2', 'b2')}
    del _L1_ffn_all
    return {'x': x, 'L0_tok_W_main': _L0_tok_in['W_main'], 'L0_tok_b_main': _L0_tok_in['b_main'], 'L0_tok_W_sx': _L0_tok_in['W_sx'], 'L0_tok_b_sx': _L0_tok_in['b_sx'], 'L0_tok_W_sy': _L0_tok_in['W_sy'], 'L0_tok_b_sy': _L0_tok_in['b_sy'], 'L0_tok_ln_g': _L0_tok_in['ln_g'], 'L0_tok_ln_b': _L0_tok_in['ln_b'], 'L0_attn_Wq': _L0_attn_in['Wq'], 'L0_attn_Wk': _L0_attn_in['Wk'], 'L0_attn_Wv': _L0_attn_in['Wv'], 'L0_attn_Wo': _L0_attn_in['Wo'], 'L0_attn_W1': _L0_attn_in['W1'], 'L0_attn_b1': _L0_attn_in['b1'], 'L0_attn_W2': _L0_attn_in['W2'], 'L0_attn_b2': _L0_attn_in['b2'], 'L0_attn_g1': _L0_attn_in['g1'], 'L0_attn_be1': _L0_attn_in['be1'], 'L0_attn_g2': _L0_attn_in['g2'], 'L0_attn_be2': _L0_attn_in['be2'], 'L0_ffn_W1': _L0_ffn_in['W1'], 'L0_ffn_b1': _L0_ffn_in['b1'], 'L0_ffn_W2': _L0_ffn_in['W2'], 'L0_ffn_b2': _L0_ffn_in['b2'], 'L1_attn_K1_w': _L1_attn_in['K1_w'], 'L1_attn_K1_b': _L1_attn_in['K1_b'], 'L1_attn_Q1_w': _L1_attn_in['Q1_w'], 'L1_attn_K2_w': _L1_attn_in['K2_w'], 'L1_attn_K2_b': _L1_attn_in['K2_b'], 'L1_attn_Q2_w': _L1_attn_in['Q2_w'], 'L1_attn_V_w': _L1_attn_in['V_w'], 'L1_attn_lambda_q1': _L1_attn_in['lambda_q1'], 'L1_attn_lambda_k1': _L1_attn_in['lambda_k1'], 'L1_attn_lambda_q2': _L1_attn_in['lambda_q2'], 'L1_attn_lambda_k2': _L1_attn_in['lambda_k2'], 'L1_attn_gn_w': _L1_attn_in['gn_w'], 'L1_attn_gn_b': _L1_attn_in['gn_b'], 'L1_attn_out_w': _L1_attn_in['out_w'], 'L1_attn_out_b': _L1_attn_in['out_b'], 'L1_ffn_ln1_g': _L1_ffn_in['ln1_g'], 'L1_ffn_ln1_b': _L1_ffn_in['ln1_b'], 'L1_ffn_wq': _L1_ffn_in['wq'], 'L1_ffn_wk': _L1_ffn_in['wk'], 'L1_ffn_wv': _L1_ffn_in['wv'], 'L1_ffn_wo': _L1_ffn_in['wo'], 'L1_ffn_ln2_g': _L1_ffn_in['ln2_g'], 'L1_ffn_ln2_b': _L1_ffn_in['ln2_b'], 'L1_ffn_wr': _L1_ffn_in['wr'], 'L1_ffn_w1': _L1_ffn_in['w1'], 'L1_ffn_b1': _L1_ffn_in['b1'], 'L1_ffn_w2': _L1_ffn_in['w2'], 'L1_ffn_b2': _L1_ffn_in['b2']}

def reference(x, L0_tok_W_main, L0_tok_b_main, L0_tok_W_sx, L0_tok_b_sx, L0_tok_W_sy, L0_tok_b_sy, L0_tok_ln_g, L0_tok_ln_b, L0_attn_Wq, L0_attn_Wk, L0_attn_Wv, L0_attn_Wo, L0_attn_W1, L0_attn_b1, L0_attn_W2, L0_attn_b2, L0_attn_g1, L0_attn_be1, L0_attn_g2, L0_attn_be2, L0_ffn_W1, L0_ffn_b1, L0_ffn_W2, L0_ffn_b2, L1_attn_K1_w, L1_attn_K1_b, L1_attn_Q1_w, L1_attn_K2_w, L1_attn_K2_b, L1_attn_Q2_w, L1_attn_V_w, L1_attn_lambda_q1, L1_attn_lambda_k1, L1_attn_lambda_q2, L1_attn_lambda_k2, L1_attn_gn_w, L1_attn_gn_b, L1_attn_out_w, L1_attn_out_b, L1_ffn_ln1_g, L1_ffn_ln1_b, L1_ffn_wq, L1_ffn_wk, L1_ffn_wv, L1_ffn_wo, L1_ffn_ln2_g, L1_ffn_ln2_b, L1_ffn_wr, L1_ffn_w1, L1_ffn_b1, L1_ffn_w2, L1_ffn_b2):
    import jax
    import jax.numpy as jnp

    def _L0_tok_ref(x, W_main, b_main, W_sx, b_sx, W_sy, b_sy, ln_g, ln_b):
        import jax, jax.numpy as jnp
        import numpy as np
        P = 16
        SHIFT = P // 2
        EPS = 1e-05

        def _shift2d(img, dy, dx):
            H, W = (img.shape[2], img.shape[3])
            pad = ((0, 0), (0, 0), (max(dy, 0), max(-dy, 0)), (max(dx, 0), max(-dx, 0)))
            z = jnp.pad(img, pad)
            return z[:, :, max(-dy, 0):max(-dy, 0) + H, max(-dx, 0):max(-dx, 0) + W]

        def _patchify(img):
            B, C, H, W = img.shape
            nH, nW = (H // P, W // P)
            t = img.reshape(B, C, nH, P, nW, P).transpose(0, 2, 4, 1, 3, 5)
            return t.reshape(B, nH * nW, C * P * P)

        def proj(img, W, b):
            return jnp.einsum('bnf,of->bno', _patchify(img), W) + b
        main = proj(x, W_main, b_main)
        xl = proj(_shift2d(x, 0, -SHIFT), W_sx, b_sx)
        xr = proj(_shift2d(x, 0, SHIFT), W_sx, b_sx)
        yu = proj(_shift2d(x, -SHIFT, 0), W_sy, b_sy)
        yd = proj(_shift2d(x, SHIFT, 0), W_sy, b_sy)
        tok = jnp.concatenate([main, xl, xr, yu, yd], axis=-1)
        mu = jnp.mean(tok, axis=-1, keepdims=True)
        var = jnp.mean(jnp.square(tok - mu), axis=-1, keepdims=True)
        return (tok - mu) * jax.lax.rsqrt(var + EPS) * ln_g + ln_b

    def _L0_attn_ref(src, Wq, Wk, Wv, Wo, W1, b1, W2, b2, g1, be1, g2, be2):
        import jax, jax.numpy as jnp
        import numpy as np
        D_MODEL = 128
        NHEAD = 8
        D_FF = 512
        EPS = 1e-05

        def _layernorm(x, gamma, beta):
            mu = jnp.mean(x, axis=-1, keepdims=True)
            var = jnp.mean(jnp.square(x - mu), axis=-1, keepdims=True)
            return (x - mu) * jax.lax.rsqrt(var + EPS) * gamma + beta

        def _rope(x, cos, sin):
            d = x.shape[-1]
            x1, x2 = (x[..., :d // 2], x[..., d // 2:])
            return jnp.concatenate([x1 * cos - x2 * sin, x2 * cos + x1 * sin], axis=-1)
        B, S, D = src.shape
        H = NHEAD
        hd = D // H
        q = (src @ Wq.T).reshape(B, S, H, hd)
        k = (src @ Wk.T).reshape(B, S, H, hd)
        v = (src @ Wv.T).reshape(B, S, H, hd)
        inv_freq = 1.0 / 10000.0 ** (jnp.arange(0, hd, 2, dtype=jnp.float32) / hd)
        t = jnp.arange(S, dtype=jnp.float32)
        freqs = t[:, None] * inv_freq[None, :]
        cos = jnp.cos(freqs)[None, :, None, :]
        sin = jnp.sin(freqs)[None, :, None, :]
        q = _rope(q, cos, sin)
        k = _rope(k, cos, sin)
        scale = 1.0 / jnp.sqrt(jnp.float32(hd))
        scores = jnp.einsum('bqhd,bkhd->bhqk', q, k) * scale
        attn = jax.nn.softmax(scores, axis=-1)
        ctx = jnp.einsum('bhqk,bkhd->bqhd', attn, v).reshape(B, S, D)
        attn_out = ctx @ Wo.T
        x = _layernorm(src + attn_out, g1, be1)
        ffn = jax.nn.relu(x @ W1.T + b1) @ W2.T + b2
        x = _layernorm(x + ffn, g2, be2)
        return x

    def _L0_ffn_ref(x, W1, b1, W2, b2):
        import jax, jax.numpy as jnp
        import numpy as np
        T = 128
        B = 64
        C = 256

        def _triu_apply(x, W, b):
            Wm = jnp.tril(W)
            return jnp.einsum('bct,st->bcs', x, Wm) + b
        h = _triu_apply(x, W1, b1)
        h = jax.nn.gelu(h, approximate=False)
        return _triu_apply(h, W2, b2)

    def _L1_attn_ref(x, K1_w, K1_b, Q1_w, K2_w, K2_b, Q2_w, V_w, lambda_q1, lambda_k1, lambda_q2, lambda_k2, gn_w, gn_b, out_w, out_b):
        import jax, jax.numpy as jnp
        import numpy as np
        B, S, D = (2, 512, 128)
        H = 8
        G = 4
        LAMBDA_INIT = 0.2
        EPS = 1e-05
        b, s, d = x.shape
        hd = d // H

        def heads(t):
            return t.reshape(b, s, H, hd).transpose(0, 2, 1, 3)
        q1 = heads(x @ Q1_w.T)
        k1 = heads(x @ K1_w.T + K1_b)
        q2 = heads(x @ Q2_w.T)
        k2 = heads(x @ K2_w.T + K2_b)
        v = heads(x @ V_w.T)
        scale = hd ** 0.5
        a1 = jax.nn.softmax(jnp.einsum('bhqd,bhkd->bhqk', q1, k1) / scale, axis=-1)
        a2 = jax.nn.softmax(jnp.einsum('bhqd,bhkd->bhqk', q2, k2) / scale, axis=-1)
        lam = jnp.exp(lambda_q1 * lambda_k1) - jnp.exp(lambda_q2 * lambda_k2) + LAMBDA_INIT
        attn = a1 - lam.reshape(1, H, 1, 1) * a2
        o = jnp.einsum('bhqk,bhkd->bhqd', attn, v)
        o = o.transpose(0, 2, 1, 3).reshape(b, s, d)
        xc = o.transpose(0, 2, 1).reshape(b, G, d // G, s)
        mu = xc.mean(axis=(2, 3), keepdims=True)
        var = xc.var(axis=(2, 3), keepdims=True)
        xn = ((xc - mu) * jax.lax.rsqrt(var + EPS)).reshape(b, d, s)
        xn = xn * gn_w[None, :, None] + gn_b[None, :, None]
        y = xn.transpose(0, 2, 1) @ out_w.T + out_b
        return y

    def _L1_ffn_ref(x, ln1_g, ln1_b, wq, wk, wv, wo, ln2_g, ln2_b, wr, w1, b1, w2, b2):
        import jax, jax.numpy as jnp
        import numpy as np
        EPS = 1e-05
        NUM_HEADS = 8
        TOP_K = 2
        CAP_FACTOR = 2

        def layernorm(x, g, b):
            m = jnp.mean(x, axis=-1, keepdims=True)
            v = jnp.var(x, axis=-1, keepdims=True)
            return (x - m) * jax.lax.rsqrt(v + EPS) * g + b
        B, S, H = x.shape
        NH = NUM_HEADS
        dh = H // NH
        x1 = layernorm(x, ln1_g, ln1_b)
        q = (x1 @ wq).reshape(B, S, NH, dh)
        k = (x1 @ wk).reshape(B, S, NH, dh)
        v = (x1 @ wv).reshape(B, S, NH, dh)
        scores = jnp.einsum('bqhd,bkhd->bhqk', q, k) * dh ** (-0.5)
        p = jax.nn.softmax(scores, axis=-1)
        attn_out = jnp.einsum('bhqk,bkhd->bqhd', p, v).reshape(B, S, H) @ wo
        x = x + attn_out
        x2 = layernorm(x, ln2_g, ln2_b).reshape(B * S, H)
        T = B * S
        E = wr.shape[1]
        C = CAP_FACTOR * (T * TOP_K // E)
        probs = jax.nn.softmax(x2 @ wr, axis=-1)
        gate_v, gate_i = jax.lax.top_k(probs, TOP_K)
        gate_v = gate_v / jnp.sum(gate_v, axis=-1, keepdims=True)
        ef = gate_i.reshape(-1)
        gf = gate_v.reshape(-1)
        oh = jax.nn.one_hot(ef, E, dtype=x2.dtype)
        pos = jnp.sum((jnp.cumsum(oh, axis=0) - oh) * oh, axis=1).astype(jnp.int32)
        keep = (pos < C).astype(x2.dtype)
        posc = jnp.minimum(pos, C - 1)
        tok = jnp.repeat(x2, TOP_K, axis=0) * keep[:, None]
        buf = jnp.zeros((E, C, H), x2.dtype).at[ef, posc].add(tok)
        h = jax.nn.gelu(jnp.einsum('ech,ehf->ecf', buf, w1) + b1[:, None, :])
        y = jnp.einsum('ecf,efh->ech', h, w2) + b2[:, None, :]
        ys = y[ef, posc] * (gf * keep)[:, None]
        moe_out = ys.reshape(T, TOP_K, H).sum(axis=1).reshape(B, S, H)
        return x + moe_out
    h = _L0_tok_ref(x, L0_tok_W_main, L0_tok_b_main, L0_tok_W_sx, L0_tok_b_sx, L0_tok_W_sy, L0_tok_b_sy, L0_tok_ln_g, L0_tok_ln_b)
    h = h + _L0_attn_ref(_layernorm(h, axis=-1), L0_attn_Wq, L0_attn_Wk, L0_attn_Wv, L0_attn_Wo, L0_attn_W1, L0_attn_b1, L0_attn_W2, L0_attn_b2, L0_attn_g1, L0_attn_be1, L0_attn_g2, L0_attn_be2)
    h = h + _L0_ffn_ref(_layernorm(h, axis=-1), L0_ffn_W1, L0_ffn_b1, L0_ffn_W2, L0_ffn_b2)
    h = h + _L1_attn_ref(_layernorm(h, axis=-1), L1_attn_K1_w, L1_attn_K1_b, L1_attn_Q1_w, L1_attn_K2_w, L1_attn_K2_b, L1_attn_Q2_w, L1_attn_V_w, L1_attn_lambda_q1, L1_attn_lambda_k1, L1_attn_lambda_q2, L1_attn_lambda_k2, L1_attn_gn_w, L1_attn_gn_b, L1_attn_out_w, L1_attn_out_b)
    h = h + _L1_ffn_ref(_layernorm(h, axis=-1), L1_ffn_ln1_g, L1_ffn_ln1_b, L1_ffn_wq, L1_ffn_wk, L1_ffn_wv, L1_ffn_wo, L1_ffn_ln2_g, L1_ffn_ln2_b, L1_ffn_wr, L1_ffn_w1, L1_ffn_b1, L1_ffn_w2, L1_ffn_b2)
    return h

_drawn_inputs = setup_inputs


def setup_inputs(seed=0):
    import zlib

    import numpy as np

    out = dict(_drawn_inputs(seed))
    spreads = {'L0_tok_b_main': (0.0, 0.1),
     'L0_tok_b_sx': (0.0, 0.1),
     'L0_tok_b_sy': (0.0, 0.1),
     'L0_tok_ln_g': (1.0, 0.2),
     'L0_tok_ln_b': (0.0, 0.1),
     'L0_attn_b1': (0.0, 0.526),
     'L0_attn_b2': (0.0, 0.1),
     'L0_attn_g1': (1.0, 0.2),
     'L0_attn_be1': (0.0, 0.1),
     'L0_attn_g2': (1.0, 0.2),
     'L0_attn_be2': (0.0, 0.1),
     'L1_attn_gn_w': (1.0, 0.6),
     'L1_attn_gn_b': (0.0, 0.688),
     'L1_ffn_ln1_g': (1.0, 0.6),
     'L1_ffn_ln1_b': (0.0, 0.8),
     'L1_ffn_ln2_g': (1.0, 0.6),
     'L1_ffn_ln2_b': (0.0, 0.637),
     'L1_ffn_b1': (0.0, 0.8),
     'L1_ffn_b2': (0.0, 0.355)}
    factors = {'L0_attn_Wq': 8.0,
     'L0_attn_Wk': 8.0,
     'L0_attn_Wv': 6.312,
     'L0_attn_Wo': 7.457,
     'L1_attn_K1_w': 8.0,
     'L1_attn_K1_b': 8.0,
     'L1_attn_Q1_w': 8.0,
     'L1_attn_K2_w': 8.0,
     'L1_attn_K2_b': 8.0,
     'L1_attn_Q2_w': 8.0,
     'L1_attn_lambda_q2': 4.51,
     'L1_attn_out_b': 5.319,
     'L1_ffn_wq': 8.0,
     'L1_ffn_wk': 8.0,
     'L1_ffn_wv': 7.743,
     'L1_ffn_wo': 7.63,
     'L1_ffn_w1': 4.581,
     'L1_ffn_w2': 4.14}
    for name, (base, spread) in spreads.items():
        noise = np.random.default_rng([zlib.crc32(name.encode()), seed]).standard_normal(out[name].shape)
        drawn = base * np.exp(spread * noise) if base else spread * noise
        out[name] = jnp.asarray(drawn.astype(out[name].dtype))
    for name, factor in factors.items():
        out[name] = (out[name] * factor).astype(out[name].dtype)
    return out
```

```python
from contextlib import ExitStack

import numpy as np

import concourse.bass as bass
from concourse import mybir

ALU = mybir.AluOpType
ACT = mybir.ActivationFunctionType
F32 = mybir.dt.float32
BF16 = mybir.dt.bfloat16
U32 = mybir.dt.uint32
AX_X = mybir.AxisListType.X

D = 128
H = 8
HD = D // H
QUADS = 4
IMG = 32
CH, PX, GRID = 3, 16, 6
SIDE = PX * GRID
SEQ = GRID * GRID
T = IMG * SEQ
NB = 4
IB = IMG // NB
TB = T // NB
TP = 96
TPB = TB // TP
NT = T // TP
PAIRS = IB // 2
HALF = 64
SROWS = HALF + SEQ
F0 = 512
FC = F0 // D
E, FF = 64, 512
CAP = 2 * (T * 2 // E)
SLOTS = E * CAP
ST = SLOTS // D
WIN = 96
RING = 13
LENT = 9
NG = 6
WORK = 17088
EPS = 1e-5
NOWHERE = 1.0e6
GSIZE = D // 4 * SEQ

CONST = {}
_at = 0
for _name, _n in (("ident", D), ("swap", D), ("order", D), ("group", D), ("parity", 2), ("cos", SEQ), ("sin", SEQ),
                  ("iota_e", E), ("iota_lo", D), ("iota_hi", ST), ("before", TP), ("ids", 2 * NT)):
    CONST[_name] = (_at, _n)
    _at += _n
CONST_COLS = _at

BLOCKS = {}
_at = 0
for _name, _n in (("tok", 6), ("L0_attn_Wq", 1), ("L0_attn_Wk", 1), ("L0_attn_Wv", 1), ("L0_attn_Wo", 1),
                  ("L0_attn_W1", FC), ("L0_attn_W2", FC), ("L0_ffn_W1", 1), ("L0_ffn_W2", 1),
                  ("L1_attn_Q1_w", 1), ("L1_attn_K1_w", 1), ("L1_attn_Q2_w", 1), ("L1_attn_K2_w", 1),
                  ("L1_attn_V_w", 1), ("L1_attn_out_w", 1)):
    BLOCKS[_name] = (_at, _n)
    _at += _n
NBLOCKS = _at
DIRECT = ["L1_ffn_wq", "L1_ffn_wk", "L1_ffn_wv", "L1_ffn_wo"]
ROWS = ["L0_tok_ln_g", "L0_tok_ln_b", "L0_attn_g1", "L0_attn_be1", "L0_attn_b2", "L0_attn_g2", "L0_attn_be2",
        "L0_ffn_b2", "L1_attn_out_b", "L1_ffn_ln2_g", "L1_ffn_ln2_b"]
COLS = ["L0_attn_g1", "L0_attn_be1", "L0_ffn_b1", "L1_attn_K1_b", "L1_attn_K2_b", "L1_attn_gn_w", "L1_attn_gn_b",
        "L1_ffn_ln1_g", "L1_ffn_ln1_b", "L1_ffn_ln2_g", "L1_ffn_ln2_b"]
NCOLS = len(COLS) + FC + 1
LAMBDAS = ["L1_attn_lambda_q1", "L1_attn_lambda_k1", "L1_attn_lambda_q2", "L1_attn_lambda_k2"]


def constants():
    c = np.zeros((D, CONST_COLS), np.float32)

    def put(name, value):
        a, n = CONST[name]
        value = np.asarray(value, np.float32)
        c[:value.shape[0], a:a + n] = value

    put("ident", np.eye(D))
    f = np.arange(D)
    q, r = f // 32, f % 32
    partner = np.where(r < 16, f ^ 32, -1)
    swap = np.zeros((D, D))
    swap[partner[r < 16], f[r < 16]] = 1
    put("swap", swap)
    order = np.zeros((D, D))
    order[f, np.where(r < 16, 64 + 16 * q + r, 16 * q + r - 16)] = 1
    put("order", order)
    put("group", (f[:, None] // 32 == f[None, :] // 32))
    put("parity", np.stack([(f // HD) % 2 == 0, (f // HD) % 2 == 1], 1))
    half = HD // 2
    inv = (np.float32(1.0) / np.float32(10000.0) ** (np.arange(0, HD, 2, dtype=np.float32) / np.float32(HD)))
    angle = (np.arange(SEQ, dtype=np.float32)[:, None] * inv.astype(np.float32)[None, :]).astype(np.float32)
    d = f % HD
    put("cos", np.cos(angle)[:, d % half].T)
    put("sin", (np.sin(angle)[:, d % half] * np.where(d < half, -1.0, 1.0)).T)
    put("iota_e", np.tile(np.arange(E), (D, 1)))
    put("iota_lo", np.tile(np.arange(D), (D, 1)))
    put("iota_hi", np.tile(np.arange(ST), (D, 1)))
    t = np.arange(TP)
    put("before", t[:, None] < t[None, :])
    ids = np.zeros((TP, NT, 2))
    for k in range(2):
        ids[:, :, k] = 2 * (np.arange(NT)[None, :] * TP + t[:, None]) + k + 1
    put("ids", ids.reshape(TP, -1))
    return c


def plan():
    order = []

    def each(*stages, skew=0):
        for i in range(NB + skew * (len(stages) - 1)):
            for n, s in reversed(list(enumerate(stages))):
                b = i - skew * n
                if 0 <= b < NB:
                    order.extend((part, b) for part in s.split())

    order.append(("prepare", 0))
    order.extend([("patches", 0), ("patches", 1)])
    each("tok_z", "tok_shift", "tok_turn tok_norm_a", "tok_norm_b", "src_norm_a", "src_norm_b", skew=1)
    each("src_turn", "rope_qk", "rope_v", "rope_scores", "rope_flip", "rope_out", "x1_norm_a", "x1_norm_b", skew=1)
    each("x1_turn", "net_in", "net_out", "x2_norm_a", "x2_norm_b", "mix_norm_a", "mix_norm_b", skew=1)
    each("mix_turn", "mix_in", "mix_out", "dif_norm_a", "dif_norm_b", skew=1)
    each("dif_turn", "dif_qk", "dif_v", "dif_scores", "dif_flip", "gn_mean", "gn_var", "dif_out", "moe_norm_a", "moe_norm_b", skew=1)
    each("moe_turn", "moe_qk", "moe_v", "moe_scores", "moe_flip", "moe_out", "rt_norm_a", "rt_norm_b", "rt_turn", "rt_logits",
         "rt_count", "rt_map", skew=1)
    return order


JOBS = {"prepare": (NBLOCKS + 4 + 3) // 4, "patches": 12, "tok_z": 1, "tok_shift": 1, "tok_turn": 1,
        "src_turn": 1, "rope_qk": 4, "rope_v": 2, "rope_flip": PAIRS + 1, "rope_out": 1,
        "x1_turn": 1, "net_in": FC, "net_out": 1, "mix_turn": 1, "mix_in": 1, "mix_out": 1,
        "dif_turn": 1, "dif_qk": 4, "dif_v": 2, "dif_flip": PAIRS + 1, "gn_mean": 1, "gn_var": 1, "dif_out": 1,
        "moe_turn": 1, "moe_qk": 2, "moe_v": 2, "moe_flip": PAIRS + 1, "moe_out": 1,
        "rt_turn": 1, "rt_logits": 1, "rt_count": 1}


def build(nc, ins, out):
    ORDER = plan()
    job_number = {}
    for stage, b in ORDER:
        for i in range(JOBS.get(stage, 0)):
            job_number[stage, b, i] = len(job_number)
    moe_order = []
    turned = 0
    returned = 0
    for e in range(E + 1):
        if e < E:
            need = min(ST, (min(e + 3, E - 1) * CAP + WIN - 1) // D + 1)
            while turned < need:
                moe_order.append(("take", turned))
                turned += 1
            moe_order.append(("hidden", e))
        if e >= 1:
            moe_order.append(("expert", e - 1))
            while (returned + 1) * D <= (e - 1) * CAP:
                moe_order.append(("give", returned))
                returned += 1
        if 8 <= e < 8 + NB:
            moe_order.append(("bias_turn", e - 8))
            moe_order.append(("bias", e - 8))
    while returned < ST:
        moe_order.append(("give", returned))
        returned += 1
    for kind, i in moe_order:
        job_number[kind, i, 0] = len(job_number)

    jobs = list(job_number)
    turned_parts = ("src", "x1", "mix", "dif", "moe", "rt")
    out_count_stages = ("rope_out", "net_out", "mix_out", "dif_out", "moe_out")

    def counts(names):
        found = {}
        for stage, b in ORDER:
            if stage in names:
                found[stage, b] = len(found) + 1
        return found

    normed_count = {(s.split("_")[0], b): n for (s, b), n in counts([p + "_norm_b" for p in turned_parts]).items()}
    turned_count = {(s.split("_")[0], b): n for (s, b), n in counts([p + "_turn" for p in turned_parts]).items()}
    rstd_count = {(s.split("_")[0], b): n for (s, b), n in counts({s for s, _ in ORDER if s.endswith("norm_a")}).items()}
    out_count = counts(out_count_stages)
    square_n = counts(("gn_mean", "gn_var"))

    ctx = ExitStack()
    with ctx:
        def sb(name, shape, dt=F32):
            return ctx.enter_context(nc.sbuf_tensor(name, shape, dt))

        def sem(name):
            return ctx.enter_context(nc.semaphore(name))

        scores = ctx.enter_context(nc.psum_tensor("scores", [D, QUADS, 512], F32))
        banks = [ctx.enter_context(nc.psum_tensor(f"bank{i}", [D, 512], F32)) for i in range(4)]
        bank_full = [sem(f"bank{i}_full") for i in range(4)]

        ring = sb("ring", [D, RING, 1024])
        xs = ring[:, RING - LENT:, :].rearrange("p a b -> p (a b)")[:, 0:2 * CH * PX * SIDE].rearrange(
            "p (h c y x) -> p h c y x", h=2, c=CH, y=PX)
        cst = sb("cst", [D, CONST_COLS])

        def const(name, rows=D):
            a, n = CONST[name]
            return cst[0:rows, a:a + n]

        SC = PAIRS * 2 * SEQ
        PW = QUADS * PAIRS * 2 * HALF
        work = sb("work", [D, WORK])

        class Share:
            def __init__(self):
                self.at = 0

            def take(self, shape, dt=F32):
                n = int(np.prod(shape))
                a = work[:, self.at:self.at + n]
                self.at += n
                assert self.at <= WORK, self.at
                names = "abcdef"[:len(shape)]
                return a.rearrange(f"p ({' '.join(names)}) -> p {' '.join(names)}", **dict(zip(names, shape)))

        first = Share()
        wnat = first.take([NBLOCKS, D])
        wshift = first.take([6 * D])
        b1nat = first.take([FF])[0:E, :]
        zraw = first.take([T])
        tokT = first.take([T])
        patchT = first.take([6, T])
        piece = first.take([2, GRID, PX, PX])
        second = Share()
        qT = second.take([2, 2, TB])
        kT = second.take([2, TB])
        rot_a = second.take([2, TB])
        rot_b = second.take([2, TB])
        kM = second.take([2, 2, 2, TB])
        ex = second.take([2, QUADS, SC])
        pT = second.take([QUADS, PAIRS, 2, SEQ])
        hid = ex.rearrange("p a b c -> p (a b c)").rearrange("p (m a t) -> p m a t", m=FC, a=2)
        ctxT = second.take([T])
        vd = second.take([2, IB, D])
        probs = second.take([2, QUADS, PAIRS, 2, HALF])
        third = Share()
        xe = third.take([SLOTS + WIN])
        yT = third.take([SLOTS])
        hT = third.take([3, FC, WIN])
        got = third.take([NG, D])
        ys = third.take([4, D])
        gmT = third.take([NB, TB])[0:E]

        wT = sb("wT", [D, NBLOCKS, D])
        wdir = sb("wdir", [D, len(DIRECT), D])
        wrot = sb("wrot", [D, 2, D])
        wr = sb("wr", [D, E])
        rows = sb("rows", [TP, len(ROWS), D])
        crows = sb("crows", [NCOLS, D])
        cols = sb("cols", [D, NCOLS])
        tok_bias = cols[:, NCOLS - 1:NCOLS]
        net_bias = cols[:, len(COLS):len(COLS) + FC]
        masked_bias = sb("masked_bias", [D, 2, 2])
        lambdas = sb("lambdas", [SROWS, 4, H])
        lam = sb("lam", [SROWS, H])
        mh = sb("mh", [D, TPB])
        b1T = sb("b1T", [D, FC, E])
        b2nat = sb("b2nat", [E, D])

        h = sb("h", [TP, NT, D])
        src = sb("src", [TP, NT, D])
        mid = sb("mid", [TP, NT, D])
        norm = sb("norm", [TP, NT, D])
        xT = sb("xT", [D, 2, TB])
        xTp = sb("xTp", [D, 2, IB + 1, HALF])
        res = norm
        stats = sb("stats", [TP, 2, TPB, 6])
        mv = sb("mv", [TP, NT, 2])
        rstd = sb("rstd", [TP, NT, 2])
        mx = sb("mx", [SROWS, 2, QUADS * PAIRS * 2])
        sm = sb("sm", [SROWS, 2, QUADS * PAIRS * 2])
        gn_s = sb("gn_s", [D, 4, IMG])
        gn_q = sb("gn_q", [D, 2, TB])
        lg = sb("lg", [TP, NT, E])
        top = sb("top", [TP, NT, 8])
        top_i = sb("top_i", [TP, NT, 8], U32)
        top_f = sb("top_f", [TP, NT, 2])
        gate = sb("gate", [TP, NT, 4])
        oh = sb("oh", [TP, 2, NT, E])
        oh_both = sb("oh_both", [TP, NT, E], BF16)
        run = sb("run", [TP, NT + 1, E], BF16)
        before16 = sb("before16", [TP, TP], BF16)
        ones16 = sb("ones16", [TP, TP], BF16)
        cum = sb("cum", [TP, TPB, E])
        pos = sb("pos", [TP, NT, 2])
        flat = sb("flat", [TP, NT, 2])
        flat_u = sb("flat_u", [TP, 3, NT, 2], U32)
        flat_f = sb("flat_f", [TP, 2, NT, 2])
        kept = sb("kept", [TP, NT, 2])
        lo1 = sb("lo1", [TP, 2, TPB, D])
        hi1 = sb("hi1", [TP, 2, TPB, ST])
        pay = sb("pay", [TP, 2, TPB, 2 * ST])
        gm = sb("gm", [TP, NT, E])
        smap = sb("smap", [D, 2 * ST])
        smap2 = sb("smap2", [D, 2, ST])
        put_u = sb("put_u", [D, ST], U32)
        get_u = sb("get_u", [D, 2, ST], U32)

        x2d = nc.dram_tensor("x2_rows", [T, D], F32, kind="Internal").ap()
        ytok = nc.dram_tensor("expert_rows", [2 * T, D], F32, kind="Internal").ap()

        names = """piece_ready w_in x_in0 x_in1 small_in zero_in zeros16 pads_zero scores_zero w_made blocks_turned b1_turned
            tri_made rot_made patches_turned patches_turned2 z_raw z_biased tok_added h_norm var rstd_ready
            normed x_turned rot_parts q_ready k_full k_ready v_ready s_full exp_in exp_done sums_ready
            probs_ready flip_ready ctx_ready gn_stat gn_back gn_ready out_added affine_ready hid_ready
            mask_ready x2_stored logits_ready picked mapped map_full map_ready xe_ready h_full yT_ready ys_ready
            back_in stored gm_ready gmT_ready bias_added lam_ready square_ready pT_ready gn_mean_back gn_centred
            gn_scaled logits_back placed gate_exp dve_step act_step pool_step final_ready
           """.split()
        S = {n: sem(n) for n in names}
        w_here = [sem(f"expert_here{i}") for i in range(RING)]
        got_here = [sem(f"got{i}") for i in range(NG)]
        ys_gone = [sem(f"ys_gone{i}") for i in range(4)]

        def bank(job):
            n = job_number[job]
            return banks[n % 4]

        def fill(pe, job):
            n = job_number[job]
            if n >= 4:
                name, count = taken(jobs[n - 4])
                pe.wait_ge(S[name], count)
            return banks[n % 4]

        def filled(job):
            return bank_full[job_number[job] % 4]

        def read(eng, job):
            n = job_number[job]
            eng.wait_ge(bank_full[n % 4], n // 4 + 1)
            return banks[n % 4]

        def taken(job):
            stage, b, i = job
            part = stage.split("_")[0]
            at = {"rope": 0, "dif": 1, "moe": 2}.get(part, 0) * NB + b
            if stage == "prepare":
                return ("b1_turned", 1) if i == JOBS[stage] - 1 else ("blocks_turned", i + 1)
            if stage == "patches":
                return ("patches_turned2" if i % 2 else "patches_turned"), 6 * b + i // 2 + 1
            if stage.endswith("_turn") and part in turned_parts:
                return "x_turned", turned_count[part, b]
            if stage in ("rope_v", "dif_v", "moe_v"):
                return "v_ready", 4 * at + 2 * i + 2
            if stage in ("rope_flip", "dif_flip", "moe_flip"):
                return ("pT_ready", PAIRS * at + i + 1) if i < PAIRS else ("ctx_ready", at + 1)
            if stage in out_count_stages:
                return "out_added", out_count[stage, b]
            return {
                "tok_z": ("z_biased", b + 1), "tok_shift": ("tok_added", b + 1), "tok_turn": ("h_norm", b + 1),
                "rope_qk": ("rot_parts", 4 * b + i + 1),
                "net_in": ("hid_ready", FC * b + i + 1), "mix_in": ("hid_ready", FC * NB + b + 1),
                "dif_qk": ("k_ready", 2 * NB + 4 * b + i + 1) if i % 2 else ("q_ready", NB + 2 * b + i // 2 + 1),
                "moe_qk": ("k_ready", 6 * NB + 2 * b + 2) if i % 2 else ("q_ready", 3 * NB + b + 1),
                "gn_mean": ("gn_mean_back", b + 1), "gn_var": ("gn_back", b + 1),
                "rt_logits": ("logits_back", b + 1), "rt_count": ("placed", b + 1),
                "take": ("xe_ready", b + 1), "hidden": ("h_full", b + 1), "expert": ("yT_ready", b + 1),
                "give": ("ys_ready", b + 1), "bias_turn": ("gmT_ready", b + 1), "bias": ("bias_added", b + 1),
            }[stage]

        class Steps:

            def __init__(self, eng, s):
                self.eng, self.s, self.n = eng, s, 0

            def step(self, ins):
                ins.then_inc(self.s, 1)
                self.n += 1

            def link(self, ins):
                self.step(ins)
                self.eng.wait_ge(self.s, self.n)

            def settle(self):
                self.eng.wait_ge(self.s, self.n)

        def block_of(name, i=0):
            return wT[:, BLOCKS[name][0] + i, :]

        def row(name):
            return rows[:, ROWS.index(name), :].unsqueeze(1).broadcast_to([TP, TPB, D])

        def col(name):
            i = COLS.index(name)
            return cols[:, i:i + 1]

        def tiles(t, b):
            return t[:, TPB * b:TPB * b + TPB, :]

        def grid(ap):
            return ap.rearrange("p (i r c) -> p i r c", r=GRID, c=GRID)

        NDMA = {}
        def back_of(b):
            return ring[0:TP, b, 0:TPB * 2 * D].rearrange("p (n c) -> p n c", n=TPB)

        block = ctx.enter_context(nc.Block())

        def load_small(eng, s):
            n = 0

            def go(dst, source):
                nonlocal n
                eng.dma_start(dst, source).then_inc(s, 16)
                n += 16

            go(cst[:, :], ins["const"])
            for name in ("L0_attn_Wq", "L0_attn_Wk", "L0_attn_Wv", "L0_attn_Wo", "L0_ffn_W1", "L0_ffn_W2", "L1_attn_Q1_w",
                         "L1_attn_K1_w", "L1_attn_Q2_w", "L1_attn_K2_w", "L1_attn_V_w", "L1_attn_out_w"):
                go(wnat[:, BLOCKS[name][0], :], ins[name])
            a = BLOCKS["L0_attn_W1"][0]
            go(wnat[:, a:a + FC, :], ins["L0_attn_W1"].rearrange("(m p) i -> p m i", p=D))
            a = BLOCKS["L0_attn_W2"][0]
            go(wnat[:, a:a + FC, :], ins["L0_attn_W2"].rearrange("o (m f) -> o m f", f=D))
            for i, name in enumerate(DIRECT):
                go(wdir[:, i, :], ins[name])
            go(wr[:, :], ins["L1_ffn_wr"])
            for i, name in enumerate(ROWS):
                go(rows[:, i, :], ins[name].partition_broadcast(TP))
            for i, name in enumerate(COLS):
                go(crows[i:i + 1, :], ins[name].rearrange("(a p) -> a p", a=1))
            go(crows[len(COLS):len(COLS) + FC, :], ins["L0_attn_b1"].rearrange("(m p) -> m p", p=D))
            for i, name in enumerate(LAMBDAS):
                go(lambdas[:, i, :], ins[name].rearrange("h a -> (h a)").partition_broadcast(SROWS))
            go(b1nat[:, :], ins["L1_ffn_b1"])
            go(b2nat[:, :], ins["L1_ffn_b2"])
            return n

        SMALL = 16 * (1 + 12 + 2 + 4 + 1 + len(ROWS) + len(COLS) + 1 + 4 + 2)

        @block.sync
        def _(sp):
            for i in range(IMG):
                half, at = i // (IMG // 2), GRID * (i % (IMG // 2))
                eng = sp
                eng.dma_start(xs[at:at + GRID, half, :, :, :].rearrange("p c y x -> p c (y x)"),
                              ins["x"][i].rearrange("c (r y) x -> r c (y x)", y=PX)).then_inc(S[f"x_in{half}"], 16)
            assert load_small(sp, S["small_in"]) == SMALL
            for e in range(E):
                s = e % RING
                if e == RING - LENT:
                    sp.wait_ge(S["patches_turned"], 12)
                    sp.wait_ge(S["patches_turned2"], 12)
                if e >= RING:
                    sp.wait_ge(S["yT_ready"], e - RING + 1)
                sp.dma_start(ring[:, s, 0:FF], ins["L1_ffn_w1"][e]).then_inc(w_here[s], 16)
                sp.dma_start(ring[:, s, FF:2 * FF].rearrange("p (c n) -> p c n", n=D),
                             ins["L1_ffn_w2"][e].rearrange("(c p) n -> p c n", p=D)).then_inc(w_here[s], 16)
            sp.wait_ge(S["yT_ready"], E)
            for i in range(4):
                sp.wait_ge(ys_gone[i], 16 * (ST // 4))
            for b in range(NB):
                sp.dma_start(back_of(b), ytok.rearrange("(n p k) c -> p n (k c)", p=TP, k=2)[:, TPB * b:TPB * b + TPB, :]
                             ).then_inc(S["back_in"], 16)
            for b in range(NB):
                sp.wait_ge(S["final_ready"], b + 1)
                sp.dma_start(out.rearrange("i s c -> (i s) c").rearrange("(n p) c -> p n c", p=TP)[:, TPB * b:TPB * b + TPB, :],
                             tiles(res, b)).then_inc(S["stored"], 16)
            sp.wait_ge(S["stored"], 16 * NB)

        @block.gpsimd
        def _(pool):
            st = Steps(pool, S["pool_step"])
            pool.memset(wnat[:, 0:6, :], 0.0).then_inc(S["zeros16"], 1)
            pool.wait_ge(S["zeros16"], 1)
            wn = wnat[:, 0:6, :].rearrange("p k f -> p (k f)")
            for q in range(QUADS):
                pool.dma_start(wn[32 * q + 16:32 * q + 32, :], ins["L0_tok_W_main"][16 * q:16 * q + 16, :]).then_inc(S["w_in"], 16)
                pool.dma_start(crows[NCOLS - 1:NCOLS, 32 * q + 16:32 * q + 32],
                               ins["L0_tok_b_main"][16 * q:16 * q + 16].rearrange("(a p) -> a p", a=1)).then_inc(S["w_in"], 16)
                side = "sx" if q < 2 else "sy"
                pool.dma_start(wshift[32 * q:32 * q + 16, :], ins[f"L0_tok_W_{side}"]).then_inc(S["w_in"], 16)
                pool.dma_start(crows[NCOLS - 1:NCOLS, 32 * q:32 * q + 16],
                               ins[f"L0_tok_b_{side}"].rearrange("(a p) -> a p", a=1)).then_inc(S["w_in"], 16)
            st.step(pool.memset(mh[:, :], -0.5))
            st.step(pool.memset(xTp[:, :, :, :], 0.0))
            st.step(pool.memset(run[:, 0, :], 0.0))
            st.step(pool.memset(ones16[:, :], 1.0))
            st.link(pool.memset(mid[:, :, :], 0.0))
            for k in range(2):
                pool.dma_start(ytok.rearrange("(k p n) c -> k p (n c)", k=2, p=TP)[k], mid[:, :, :].rearrange("p n c -> p (n c)")
                               ).then_inc(S["zero_in"], 16)
            pool.wait_ge(S["zero_in"], 32)
            pool.wait_ge(S["w_in"], 16 * 4 * QUADS)
            w5 = wn.rearrange("p (c y x) -> p c y x", c=CH, y=PX)
            s5 = wshift[:, :].rearrange("p (c y x) -> p c y x", c=CH, y=PX)
            hp = PX // 2
            pool.tensor_copy(w5[0:16, :, :, hp:PX], s5[0:16, :, :, 0:hp]).then_inc(S["w_made"], 1)
            pool.tensor_copy(w5[32:48, :, :, 0:hp], s5[32:48, :, :, hp:PX]).then_inc(S["w_made"], 1)
            pool.tensor_copy(w5[64:80, :, hp:PX, :], s5[64:80, :, 0:hp, :]).then_inc(S["w_made"], 1)
            pool.tensor_copy(w5[96:112, :, 0:hp, :], s5[96:112, :, hp:PX, :]).then_inc(S["w_made"], 1)
            pool.wait_ge(S["w_made"], 4)
            pool.wait_ge(S["small_in"], SMALL)
            pool.tensor_copy(before16[:, :], const("before", TP)).then_inc(S["tri_made"], 1)
            pool.wait_ge(S["b1_turned"], 1)
            for n, name in enumerate(("L1_attn_K1_b", "L1_attn_K2_b")):
                for a in range(2):
                    pool.tensor_tensor(masked_bias[:, n, a:a + 1], col(name), const("parity")[:, a:a + 1], ALU.mult
                                       ).then_inc(S["mask_ready"], 1)
            pool.wait_ge(S["blocks_turned"], (NBLOCKS + 3) // 4)
            for name in ("L0_ffn_W1", "L0_ffn_W2"):
                w = block_of(name)
                pool.affine_select(out=w, in_=w, compare_op=ALU.is_ge, fill=0.0, base=0, pattern=[[1, D]],
                                   channel_multiplier=-1).then_inc(S["tri_made"], 1)
            for n, name in enumerate(("L0_attn_Wq", "L0_attn_Wk")):
                w = block_of(name).rearrange("p (h a d) -> p h a d", h=H, a=2)
                r = wrot[:, n, :].rearrange("p (h a d) -> p h a d", h=H, a=2)
                for a in range(2):
                    pool.tensor_copy(r[:, :, a, :], w[:, :, 1 - a, :]).then_inc(S["rot_made"], 1)

            var_n = 0

            def rsqrt(b, twice=False):
                nonlocal var_n
                var_n += 1
                pool.wait_ge(S["var"], var_n)
                v = mv[:, TPB * b:TPB * b + TPB, 1]
                r = rstd[:, TPB * b:TPB * b + TPB, 0]
                r2 = rstd[:, TPB * b:TPB * b + TPB, 1]
                st.link(pool.tensor_scalar(r2, v, EPS, None, ALU.add))
                if not twice:
                    pool.tensor_tensor(r, r2, mh[0:TP, 0:TPB], ALU.pow).then_inc(S["rstd_ready"], 1)
                    return
                st.link(pool.tensor_tensor(r, r2, mh[0:TP, 0:TPB], ALU.pow))
                st.link(pool.tensor_tensor(r2, r, r, ALU.mult))
                st.link(pool.tensor_tensor(r2, r2, v, ALU.mult))
                st.link(pool.tensor_scalar(r2, r2, EPS, None, ALU.add))
                pool.tensor_tensor(r2, r2, mh[0:TP, 0:TPB], ALU.pow).then_inc(S["rstd_ready"], 1)

            soft_n = sums_n = flips = pieces = 0
            for stage, b in ORDER:
                tok = slice(TB * b, TB * b + TB)
                if stage == "patches":
                    pool.wait_ge(S[f"x_in{b}"], 16 * IMG // 2)
                    for c in range(CH):
                        if pieces >= 2:
                            pool.wait_ge(S["patches_turned"], 2 * (pieces - 1))
                            pool.wait_ge(S["patches_turned2"], 2 * (pieces - 1))
                        for y in range(0, PX, PX // 2):
                            last = pool.tensor_copy(piece[0:TP, pieces % 2, :, y:y + PX // 2, :],
                                                    xs[0:TP, b, c, y:y + PX // 2, :].rearrange("p y (w x) -> p w y x", x=PX))
                            last.then_inc(S["piece_ready"], 1)
                        pieces += 1
                if stage == "src_turn" and b == 0:
                    pool.wait_ge(S["z_biased"], NB)
                    st.step(pool.memset(probs[:, :, :, :, :, :], 0.0))
                    pool.memset(vd[:, :, :, :], 0.0).then_inc(S["pads_zero"], 1)
                if stage.endswith("norm_a"):
                    rsqrt(b, twice=stage.startswith("moe"))
                if stage == "rope_qk":
                    pool.wait_ge(S["rot_parts"], 4 * b + 2)
                    pool.tensor_tensor(qT[:, b % 2, 0, :], rot_a[:, 0, :], rot_b[:, 0, :], ALU.add).then_inc(S["q_ready"], 1)
                    pool.wait_ge(S["rot_parts"], 4 * b + 4)
                    pool.tensor_tensor(kT[:, b % 2, :], rot_a[:, 1, :], rot_b[:, 1, :], ALU.add).then_inc(S["k_full"], 1)
                if stage in ("rope_scores", "moe_scores"):
                    soft_n += 1
                    sums_n += 1
                    pool.wait_ge(S["sums_ready"], sums_n)
                    if flips >= 2:
                        pool.wait_ge(S["pT_ready"], PAIRS * (flips - 1))
                    s = (soft_n - 1) % 2
                    for q in range(QUADS):
                        ins_ = pool.tensor_tensor(
                            probs[0:SROWS, flips % 2, q, :, :, 0:SEQ].rearrange("p a b k -> p (a b) k"),
                            ex[0:SROWS, s, q, :].rearrange("p (a k) -> p a k", k=SEQ),
                            sm[:, s, 2 * PAIRS * q:2 * PAIRS * (q + 1)].unsqueeze(2).broadcast_to([SROWS, 2 * PAIRS, SEQ]), ALU.mult)
                    ins_.then_inc(S["probs_ready"], 1)
                    flips += 1
                if stage == "dif_scores":
                    soft_n += 2
                    sums_n += 1
                    pool.wait_ge(S["sums_ready"], sums_n)
                    s = (soft_n - 2) % 2
                    for q in range(QUADS):
                        v = ex[0:SROWS, s, q, :].rearrange("p (a k) -> p a k", k=SEQ)
                        ins_ = pool.tensor_tensor(
                            v, v, sm[:, s, 2 * PAIRS * q:2 * PAIRS * (q + 1)].unsqueeze(2).broadcast_to([SROWS, 2 * PAIRS, SEQ]), ALU.mult)
                    ins_.then_inc(S["flip_ready"], 1)
                    flips += 1
                if stage == "gn_var":
                    pool.wait_ge(S["gn_back"], b + 1)
                    im = slice(IB * b, IB * b + IB)
                    st.link(pool.tensor_scalar(gn_s[:, 3, im], gn_s[:, 3, im], EPS, None, ALU.add))
                    st.link(pool.tensor_tensor(gn_s[:, 3, im], gn_s[:, 3, im], mh[:, 0:1].broadcast_to([D, IB]), ALU.pow))
                    pool.tensor_scalar(gn_s[:, 3, im], gn_s[:, 3, im], col("L1_attn_gn_w"), 0.0, ALU.mult, ALU.add
                                       ).then_inc(S["gn_ready"], 1)
                if stage == "x1_norm_b":
                    pool.wait_ge(S["normed"], normed_count["x1", b])
                    st.link(pool.tensor_tensor(tiles(mid, b), tiles(norm, b), row("L0_attn_g1"), ALU.mult))
                    st.link(pool.tensor_tensor(tiles(mid, b), tiles(mid, b), row("L0_attn_be1"), ALU.add))
                    pool.tensor_tensor(tiles(mid, b), tiles(mid, b), row("L0_attn_b2"), ALU.add).then_inc(S["affine_ready"], 1)
                if stage == "rt_norm_b":
                    pool.wait_ge(S["normed"], normed_count["rt", b])
                    st.link(pool.tensor_tensor(tiles(mid, b), tiles(norm, b), row("L1_ffn_ln2_g"), ALU.mult))
                    st.link(pool.tensor_tensor(tiles(mid, b), tiles(mid, b), row("L1_ffn_ln2_b"), ALU.add))
                    pool.dma_start(x2d.rearrange("(n p) c -> p n c", p=TP)[:, TPB * b:TPB * b + TPB, :], tiles(mid, b)
                                   ).then_inc(S["x2_stored"], 16)

            pool.wait_ge(S["map_ready"], 1)
            pool.wait_ge(S["x2_stored"], 16 * NB)
            gathered = 0

            def gather(i):
                if i >= NG:
                    pool.wait_ge(S["xe_ready"], i - NG + 1)
                pool.indirect_dma_start(out=got[:, i % NG, :], out_offset=None, in_=x2d[:, :],
                                        in_offset=bass.IndirectOffsetOnAxis(ap=get_u[:, 1, i:i + 1], axis=0)
                                        ).then_inc(got_here[i % NG], 16)

            for kind, i in moe_order:
                if kind == "take":
                    while gathered < min(ST, i + 3):
                        gather(gathered)
                        gathered += 1
                if kind == "give":
                    pool.wait_ge(S["ys_ready"], i + 1)
                    pool.indirect_dma_start(out=ytok[:, :], out_offset=bass.IndirectOffsetOnAxis(ap=put_u[:, i:i + 1], axis=0),
                                            in_=ys[:, i % 4, :], in_offset=None, bounds_check=2 * T - 1, oob_is_err=False
                                            ).then_inc(ys_gone[i % 4], 16)

        @block.tensor
        def _(pe):
            def mm(o, a, b, start=True, stop=True):
                return nc.tensor.matmul(o, a, b, start=start, stop=stop)

            x_turned = {"n": 0}

            def turn(stage, b):
                job = (stage, b, 0)
                o = fill(pe, job)
                source = src if stage == "src_turn" else norm
                pe.wait_ge(S["normed"], normed_count[stage.split("_")[0], b])
                for i in range(TPB):
                    last = nc.tensor.transpose(o[:, TP * i:TP * i + TP], source[:, TPB * b + i, :], const("ident")[0:TP, 0:TP])
                last.then_inc(filled(job), 1)

            def features(job, w, b, n=None):
                o = fill(pe, job)
                x = xT[:, b % 2, :] if job[0] in ("net_in", "mix_in") else xTp[:, b % 2, 0:IB, 0:SEQ]
                mm(o[:, 0:TB], w, x).then_inc(filled(job), 1)

            def tokens(job, lhs, rhs_list, width=D):
                o = fill(pe, job)
                for i in range(TPB):
                    for k, rhs in enumerate(rhs_list):
                        last = mm(o[0:TP, width * i:width * i + width], lhs(k, i), rhs, start=(k == 0), stop=(k == len(rhs_list) - 1))
                last.then_inc(filled(job), 1)

            def values(stage, b, w):
                for half in range(2):
                    job = (stage, b, half)
                    o = fill(pe, job)
                    for i in range(IB // 2):
                        at = IB // 2 * half + i
                        last = mm(o[:, D * i:D * i + D], xTp[:, b % 2, at:at + 2, :].rearrange("p i s -> p (i s)"), w)
                    last.then_inc(filled(job), 1)

            def score(n, b, s):
                if n >= 1:
                    pe.wait_ge(S["exp_in"], n)
                else:
                    pe.wait_ge(S["scores_zero"], 1)
                for p in range(PAIRS):
                    for a in range(2):
                        t = SEQ * (2 * p + a)
                        for q in range(QUADS):
                            last = mm(scores[HALF * a:HALF * a + SEQ, q, 2 * SEQ * p:2 * SEQ * (p + 1)],
                                      qT[32 * q:32 * q + 32, b % 2, s, t:t + SEQ], kM[32 * q:32 * q + 32, b % 2, s, :, t:t + SEQ])
                last.then_inc(S["s_full"], 1)

            def flip(stage, b, n):
                pe.wait_ge(S["probs_ready"], n + 1)
                for p in range(PAIRS):
                    job = (stage, b, p)
                    o = fill(pe, job)
                    for q in range(QUADS):
                        last = nc.tensor.transpose(o[:, SROWS * q:SROWS * (q + 1)],
                                                   probs[0:SROWS, n % 2, q, p, :, :].rearrange("p a k -> p (a k)"),
                                                   const("ident")[0:SROWS, 0:SROWS])
                    last.then_inc(filled(job), 1)
                job = (stage, b, PAIRS)
                o = fill(pe, job)
                pe.wait_ge(S["v_ready"], 4 * (n + 1))
                pe.wait_ge(S["pT_ready"], PAIRS * (n + 1))
                for p in range(PAIRS):
                    for a in range(2):
                        i = 2 * p + a
                        for q in range(QUADS):
                            last = mm(o[32 * q:32 * q + 32, SEQ * i:SEQ * i + SEQ], vd[:, b % 2, i, 32 * q:32 * q + 32],
                                      pT[:, q, p, a, :])
                last.then_inc(filled(job), 1)

            score_n = 0
            flip_n = 0
            turn_n = 0
            pe.wait_ge(S["small_in"], SMALL)
            for stage, b in ORDER:
                def ctx_tile(k, i):
                    return ctxT[:, TB * b + TP * i:TB * b + TP * i + TP]

                if stage == "prepare":
                    pe.wait_ge(S["w_made"], 4)
                    for j in range(JOBS["prepare"] - 1):
                        o = fill(pe, (stage, 0, j))
                        for i in range(4 * j, min(4 * j + 4, NBLOCKS)):
                            last = nc.tensor.transpose(o[:, D * (i % 4):D * (i % 4) + D], wnat[:, i, :], const("ident"))
                        last.then_inc(filled((stage, 0, j)), 1)
                    job = (stage, 0, JOBS["prepare"] - 1)
                    o = fill(pe, job)
                    for c in range(FC):
                        last = nc.tensor.transpose(o[:, E * c:E * c + E], b1nat[:, D * c:D * c + D], const("ident")[0:E, 0:E])
                    pe.wait_ge(S["w_in"], 16 * 4 * QUADS)
                    last = nc.tensor.transpose(o[:, FC * E:FC * E + NCOLS], crows[:, :], const("ident")[0:NCOLS, 0:NCOLS])
                    last.then_inc(filled(job), 1)
                elif stage == "patches":
                    for k in range(6):
                        pe.wait_ge(S["piece_ready"], 6 * b + k + 1)
                        for g in range(2):
                            job = (stage, b, 2 * k + g)
                            o = fill(pe, job)
                            for w in range(3):
                                last = nc.tensor.transpose(o[:, TP * w:TP * w + TP],
                                                           piece[0:TP, (CH * b + k // 2) % 2, 3 * g + w, 8 * (k % 2):8 * (k % 2) + 8, :]
                                                           .rearrange("p y x -> p (y x)"),
                                                           const("ident")[0:TP, 0:TP])
                            last.then_inc(filled(job), 1)
                elif stage == "tok_z":
                    pe.wait_ge(S["patches_turned"], 6 * (b // 2 + 1))
                    pe.wait_ge(S["patches_turned2"], 6 * (b // 2 + 1))
                    if b == 0:
                        pe.wait_ge(S["blocks_turned"], (NBLOCKS + 3) // 4)
                    job = (stage, b, 0)
                    o = fill(pe, job)
                    for k in range(6):
                        last = mm(o[:, 0:TB], wT[:, k, :], patchT[:, k, TB * b:TB * b + TB], start=(k == 0), stop=(k == 5))
                    last.then_inc(filled(job), 1)
                elif stage == "tok_shift":
                    pe.wait_ge(S["z_raw"], b + 1)
                    job = (stage, b, 0)
                    o = fill(pe, job)
                    mm(o[:, 0:TB], const("swap"), zraw[:, TB * b:TB * b + TB]).then_inc(filled(job), 1)
                elif stage == "tok_turn":
                    pe.wait_ge(S["tok_added"], b + 1)
                    tokens((stage, b, 0), lambda k, i: tokT[:, TB * b + TP * i:TB * b + TP * i + TP], [const("order")])
                elif stage in ("src_turn", "x1_turn", "mix_turn", "dif_turn", "moe_turn", "rt_turn"):
                    turn(stage, b)
                elif stage == "rope_qk":
                    pe.wait_ge(S["x_turned"], turned_count["src", b])
                    if b == 0:
                        pe.wait_ge(S["rot_made"], 4)
                    for j, w in enumerate((block_of("L0_attn_Wq"), wrot[:, 0, :], block_of("L0_attn_Wk"), wrot[:, 1, :])):
                        features((stage, b, j), w, b)
                elif stage == "rope_v":
                    if b == 0:
                        pe.wait_ge(S["pads_zero"], 1)
                    values(stage, b, block_of("L0_attn_Wv"))
                elif stage == "rope_scores":
                    pe.wait_ge(S["q_ready"], b + 1)
                    pe.wait_ge(S["k_ready"], 2 * (b + 1))
                    score(score_n, b, 0)
                    score_n += 1
                elif stage in ("rope_flip", "dif_flip", "moe_flip"):
                    flip(stage, b, flip_n)
                    flip_n += 1
                elif stage in ("rope_out", "moe_out"):
                    pe.wait_ge(S["ctx_ready"], NB * (2 if stage == "moe_out" else 0) + b + 1)
                    tokens((stage, b, 0), ctx_tile, [block_of("L0_attn_Wo") if stage == "rope_out" else wdir[:, 3, :]])
                elif stage == "net_in":
                    pe.wait_ge(S["x_turned"], turned_count["x1", b])
                    for m in range(FC):
                        features((stage, b, m), block_of("L0_attn_W1", m), b)
                elif stage == "net_out":
                    pe.wait_ge(S["hid_ready"], 4 * (b + 1))
                    tokens((stage, b, 0), lambda k, i: hid[:, k, b % 2, TP * i:TP * i + TP],
                           [block_of("L0_attn_W2", m) for m in range(FC)])
                elif stage == "mix_in":
                    pe.wait_ge(S["x_turned"], turned_count["mix", b])
                    if b == 0:
                        pe.wait_ge(S["tri_made"], 3)
                    features((stage, b, 0), block_of("L0_ffn_W1"), b)
                elif stage == "mix_out":
                    pe.wait_ge(S["hid_ready"], 4 * NB + b + 1)
                    tokens((stage, b, 0), lambda k, i: hid[:, 0, b % 2, TP * i:TP * i + TP], [block_of("L0_ffn_W2")])
                elif stage == "dif_qk":
                    pe.wait_ge(S["x_turned"], turned_count["dif", b])
                    for j, w in enumerate(("L1_attn_Q1_w", "L1_attn_K1_w", "L1_attn_Q2_w", "L1_attn_K2_w")):
                        features((stage, b, j), block_of(w), b)
                elif stage == "dif_v":
                    values(stage, b, block_of("L1_attn_V_w"))
                elif stage == "dif_scores":
                    pe.wait_ge(S["q_ready"], NB + 2 * (b + 1))
                    pe.wait_ge(S["k_ready"], 2 * NB + 4 * (b + 1))
                    score(score_n, b, 0)
                    score(score_n + 1, b, 1)
                    score_n += 2
                elif stage == "gn_mean":
                    job = (stage, b, 0)
                    o = fill(pe, job)
                    pe.wait_ge(S["gn_stat"], square_n[stage, b])
                    mm(o[:, 0:IB], const("group"), gn_s[:, 0, IB * b:IB * b + IB]).then_inc(filled(job), 1)
                elif stage == "gn_var":
                    job = (stage, b, 0)
                    o = fill(pe, job)
                    pe.wait_ge(S["gn_stat"], square_n[stage, b])
                    mm(o[:, 0:IB], const("group"), gn_s[:, 2, IB * b:IB * b + IB]).then_inc(filled(job), 1)
                elif stage == "dif_out":
                    pe.wait_ge(S["square_ready"], square_n["gn_var", b])
                    tokens((stage, b, 0), ctx_tile, [block_of("L1_attn_out_w")])
                elif stage == "moe_qk":
                    pe.wait_ge(S["x_turned"], turned_count["moe", b])
                    for j in range(2):
                        features((stage, b, j), wdir[:, j, :], b)
                elif stage == "moe_v":
                    values(stage, b, wdir[:, 2, :])
                elif stage == "moe_scores":
                    pe.wait_ge(S["q_ready"], 3 * NB + b + 1)
                    pe.wait_ge(S["k_ready"], 6 * NB + 2 * (b + 1))
                    score(score_n, b, 0)
                    score_n += 1
                elif stage == "rt_logits":
                    pe.wait_ge(S["x_turned"], turned_count["rt", b])
                    tokens((stage, b, 0), lambda k, i: xT[:, b % 2, TP * i:TP * i + TP], [wr[:, :]], width=E)
                elif stage == "rt_count":
                    pe.wait_ge(S["picked"], b + 1)
                    job = (stage, b, 0)
                    o = fill(pe, job)
                    for i in range(TPB):
                        g = TPB * b + i
                        mm(o[0:TP, E * i:E * i + E], before16[:, :], oh_both[:, g, :], start=True, stop=False)
                        last = mm(o[0:TP, E * i:E * i + E], ones16[:, :], run[:, g, :], start=False, stop=True)
                    last.then_inc(filled(job), 1)
                elif stage == "rt_map":
                    pe.wait_ge(S["mapped"], b + 1)
                    if b == 0:
                        pe.wait_ge(S["exp_in"], 4 * NB)
                    for i in range(TPB):
                        for k in range(2):
                            last = mm(scores[:, 0, 0:2 * ST], lo1[:, k, i, :], pay[:, k, i, :],
                                      start=(b == 0 and i == 0 and k == 0), stop=(b == NB - 1 and i == TPB - 1 and k == 1))
                    last.then_inc(S["map_full"], 1)

            for kind, i in moe_order:
                job = (kind, i, 0)
                o = fill(pe, job)
                if kind == "take":
                    pe.wait_ge(got_here[i % NG], 16 * (i // NG + 1))
                    nc.tensor.transpose(o[:, 0:D], got[:, i % NG, :], const("ident")).then_inc(filled(job), 1)
                elif kind == "hidden":
                    e, s = i, i % RING
                    pe.wait_ge(S["xe_ready"], min(ST, (e * CAP + WIN - 1) // D + 1))
                    pe.wait_ge(w_here[s], 32 * (e // RING + 1))
                    for c in range(FC):
                        last = mm(o[:, WIN * c:WIN * c + WIN], ring[:, s, D * c:D * c + D], xe[:, CAP * e:CAP * e + WIN])
                    last.then_inc(filled(job), 1)
                elif kind == "expert":
                    e, s = i, i % RING
                    pe.wait_ge(S["h_full"], e + 1)
                    for c in range(FC):
                        last = mm(o[:, 0:WIN], ring[:, s, FF + D * c:FF + D * c + D], hT[:, e % 3, c, :], start=(c == 0), stop=(c == FC - 1))
                    last.then_inc(filled(job), 1)
                elif kind == "give":
                    pe.wait_ge(S["yT_ready"], min(E, -(-(i + 1) * D // CAP)))
                    nc.tensor.transpose(o[:, 0:D], yT[:, D * i:D * i + D], const("ident")).then_inc(filled(job), 1)
                elif kind == "bias_turn":
                    pe.wait_ge(S["gm_ready"], NB)
                    for t in range(TPB):
                        last = nc.tensor.transpose(o[0:E, TP * t:TP * t + TP], gm[:, TPB * i + t, :], const("ident")[0:TP, 0:TP])
                    last.then_inc(filled(job), 1)
                elif kind == "bias":
                    pe.wait_ge(S["gmT_ready"], i + 1)
                    for t in range(TPB):
                        last = mm(o[0:TP, D * t:D * t + D], gmT[:, i, TP * t:TP * t + TP], b2nat[:, :])
                    last.then_inc(filled(job), 1)

        @block.scalar
        def _(act):
            def go(o, i, f=ACT.Copy, **kw):
                return nc.scalar.activation(o, i, f, **kw)

            flip_n = 0
            soft_n = 0
            v_n = 0
            st = Steps(act, S["act_step"])
            for stage, b in ORDER:
                tok = slice(TB * b, TB * b + TB)
                if stage == "prepare":
                    for j in range(JOBS["prepare"] - 1):
                        n = min(4 * j + 4, NBLOCKS) - 4 * j
                        o = read(act, (stage, 0, j))
                        go(wT[:, 4 * j:4 * j + n, :], o[:, 0:D * n].rearrange("p (k f) -> p k f", f=D)).then_inc(S["blocks_turned"], 1)
                    job = (stage, 0, JOBS["prepare"] - 1)
                    o = read(act, job)
                    go(cols[:, :], o[:, FC * E:FC * E + NCOLS])
                    go(b1T[:, :, :], o[:, 0:FC * E].rearrange("p (c e) -> p c e", e=E)).then_inc(S["b1_turned"], 1)
                    act.wait_ge(S["lam_ready"], 1)
                    go(lambdas[:, 0:2, :], lambdas[:, 0:2, :], ACT.Exp).then_inc(S["lam_ready"], 1)
                elif stage == "patches":
                    for k in range(6):
                        job = (stage, b, 2 * k)
                        o = read(act, job)
                        dst = patchT[:, k, T // 2 * b:T // 2 * (b + 1)].rearrange("p (r w) -> p w r", w=GRID)[:, 0:3, :]
                        go(dst, o[:, 0:3 * TP].rearrange("p (w r) -> p w r", w=3)).then_inc(S["patches_turned"], 1)
                elif stage == "tok_z":
                    if b == 0:
                        act.wait_ge(S["b1_turned"], 1)
                    job = (stage, b, 0)
                    o = read(act, job)
                    go(zraw[:, tok], o[:, 0:TB]).then_inc(S["z_raw"], 1)
                    go(tokT[:, tok], o[:, 0:TB], ACT.Identity, bias=tok_bias[:, 0:1]).then_inc(S["z_biased"], 1)
                elif stage in ("src_turn", "mix_turn", "dif_turn"):
                    job = (stage, b, 0)
                    o = read(act, job)
                    dst, again, u = xT[:, b % 2, :], None, o[:, 0:TB]
                    if stage != "mix_turn":
                        dst, again, u = xTp[:, b % 2, 0:IB, 0:SEQ], xTp[:, b % 2, IB, 0:SEQ], u.rearrange("p (i s) -> p i s", s=SEQ)
                        go(again, o[:, 0:SEQ])
                    go(dst, u).then_inc(S["x_turned"], 1)
                elif stage in ("x1_turn", "moe_turn", "rt_turn"):
                    g, be = {"x1": ("L0_attn_g1", "L0_attn_be1"), "moe": ("L1_ffn_ln1_g", "L1_ffn_ln1_b"),
                             "rt": ("L1_ffn_ln2_g", "L1_ffn_ln2_b")}[stage.split("_")[0]]
                    job = (stage, b, 0)
                    o = read(act, job)
                    dst, u = xT[:, b % 2, :], o[:, 0:TB]
                    if stage == "moe_turn":
                        dst, u = xTp[:, b % 2, 0:IB, 0:SEQ], u.rearrange("p (i s) -> p i s", s=SEQ)
                        go(xTp[:, b % 2, IB, 0:SEQ], o[:, 0:SEQ], ACT.Identity, bias=col(be), scale=col(g))
                    go(dst, u, ACT.Identity, bias=col(be), scale=col(g)).then_inc(S["x_turned"], 1)
                elif stage == "rope_qk":
                    act.wait_ge(S["k_full"], b + 1)
                    for a in range(2):
                        go(kM[:, b % 2, 0, a, :], kT[:, b % 2, :], ACT.Identity, scale=const("parity")[:, a:a + 1]).then_inc(S["k_ready"], 1)
                elif stage in ("rope_v", "dif_v", "moe_v"):
                    if v_n == 0:
                        act.wait_ge(S["pads_zero"], 1)
                    for half in range(2):
                        job = (stage, b, half)
                        o = read(act, job)
                        i0 = IB // 2 * half
                        for a in range(2):
                            r = slice(HALF * a, HALF * a + HALF)
                            v5 = vd[r, b % 2, :, :].rearrange("p i (q a d) -> p i q a d", q=QUADS, a=2)[:, :, :, a, :]
                            o5 = o[r, :].rearrange("p (i q a d) -> p i q a d", i=IB // 2, q=QUADS, a=2)[:, :, :, a, :]
                            n = IB // 2 - (1 if a and half else 0)
                            ins_ = go(v5[:, i0 + a:i0 + a + n], o5[:, 0:n])
                            if a and half:
                                ins_ = go(v5[:, 0], o5[:, n])
                            ins_.then_inc(S["v_ready"], 1)
                            v_n += 1
                elif stage in ("dif_qk", "moe_qk"):
                    for j in range(JOBS[stage]):
                        job = (stage, b, j)
                        o = read(act, job)
                        s = j // 2
                        if j % 2 == 0:
                            ins_ = go(qT[:, b % 2, s, :], o[:, 0:TB])
                            ins_.then_inc(S["q_ready"], 1)
                        else:
                            for a in range(2):
                                if stage == "dif_qk":
                                    ins_ = go(kM[:, b % 2, s, a, :], o[:, 0:TB], ACT.Identity, scale=const("parity")[:, a:a + 1],
                                              bias=masked_bias[:, s, a:a + 1])
                                else:
                                    ins_ = go(kM[:, b % 2, s, a, :], o[:, 0:TB], ACT.Identity, scale=const("parity")[:, a:a + 1])
                                ins_.then_inc(S["k_ready"], 1)
                elif stage in ("rope_scores", "dif_scores", "moe_scores"):
                    for s in range(2 if stage == "dif_scores" else 1):
                        act.wait_ge(S["exp_in"], soft_n + 1)
                        v = ex[0:SROWS, soft_n % 2, :, :]
                        go(v, v, ACT.Exp, scale=HD ** -0.5).then_inc(S["exp_done"], 1)
                        soft_n += 1
                elif stage in ("rope_flip", "dif_flip", "moe_flip"):
                    for p in range(PAIRS):
                        job = (stage, b, p)
                        o = read(act, job)
                        ins_ = go(pT[:, :, p, :, :],
                                  o[:, 0:SROWS * QUADS].rearrange("p (q r) -> p q r", q=QUADS)
                                  if False else bass.AP(o[:, :].tensor, o[:, :].offset,
                                                        [list(o[:, :].ap[0]), [SROWS, QUADS], [HALF, 2], [1, SEQ]]))
                        ins_.then_inc(S["pT_ready"], 1)
                    flip_n += 1
                    job = (stage, b, PAIRS)
                    o = read(act, job)
                    go(ctxT[:, tok], o[:, 0:TB]).then_inc(S["ctx_ready"], 1)
                elif stage == "gn_mean":
                    act.wait_ge(S["gn_centred"], b + 1)
                    go(gn_q[:, b % 2, :], ctxT[:, tok], ACT.Square).then_inc(S["square_ready"], 1)
                elif stage == "gn_var":
                    act.wait_ge(S["gn_scaled"], b + 1)
                    go(ctxT[:, tok], ctxT[:, tok], ACT.Identity, bias=col("L1_attn_gn_b")).then_inc(S["square_ready"], 1)
                elif stage == "net_in":
                    for m in range(0, FC):
                        job = (stage, b, m)
                        o = read(act, job)
                        go(hid[:, m, b % 2, :], o[:, 0:TB], ACT.Relu, bias=net_bias[:, m:m + 1]).then_inc(S["hid_ready"], 1)
                elif stage == "mix_in":
                    job = (stage, b, 0)
                    o = read(act, job)
                    go(hid[:, 0, b % 2, :], o[:, 0:TB], ACT.Gelu, bias=col("L0_ffn_b1")).then_inc(S["hid_ready"], 1)
                elif stage == "rt_logits":
                    act.wait_ge(S["logits_ready"], b + 1)
                    t = slice(TPB * b, TPB * b + TPB)
                    go(gate[:, t, 2], gate[:, t, 3], ACT.Exp).then_inc(S["gate_exp"], 1)

            for kind, i in moe_order:
                job = (kind, i, 0)
                if kind == "hidden":
                    if i >= 3:
                        act.wait_ge(S["yT_ready"], i - 2)
                    o = read(act, job)
                    for c in range(FC):
                        ins_ = go(hT[:, i % 3, c, 0:CAP], o[:, WIN * c:WIN * c + CAP], ACT.Gelu_apprx_tanh, bias=b1T[:, c, i:i + 1])
                    ins_.then_inc(S["h_full"], 1)
                elif kind == "give":
                    if i >= 4:
                        act.wait_ge(ys_gone[i % 4], 16 * (i // 4))
                    o = read(act, job)
                    go(ys[:, i % 4, :], o[:, 0:D], ACT.Identity, scale=smap[:, ST + i:ST + i + 1]).then_inc(S["ys_ready"], 1)

        @block.vector
        def _(dve):
            v = nc.vector
            st = Steps(dve, S["dve_step"])
            v.memset(scores[:, :, :], 0.0).then_inc(S["scores_zero"], 1)
            dve.wait_ge(S["small_in"], SMALL)
            st.step(v.tensor_tensor(lambdas[:, 0, :], lambdas[:, 0, :], lambdas[:, 1, :], ALU.mult))
            st.settle()
            v.tensor_tensor(lambdas[:, 1, :], lambdas[:, 2, :], lambdas[:, 3, :], ALU.mult).then_inc(S["lam_ready"], 1)

            def moments(b, source):
                for i in range(TPB):
                    st.step(v.bn_stats(stats[:, b % 2, i, :], source(i)))
                st.settle()
                for i in range(TPB):
                    last = v.bn_aggr(mv[:, TPB * b + i, :], stats[:, b % 2, i, :])
                return last

            def normalise(name, b, dst, source):
                dve.wait_ge(S["rstd_ready"], rstd_count[name, b])
                for i in range(TPB):
                    g = TPB * b + i
                    last = v.tensor_scalar(dst[:, g, :], source(i), mv[:, g, 0:1], rstd[:, g, 0:1], ALU.subtract, ALU.mult)
                return last

            def of(t, b):
                return lambda i: t[:, TPB * b + i, :]

            soft_n = 0
            flip_n = 0
            dif_n = 0
            flip_of = []
            for stage, b in ORDER:
                tok = slice(TB * b, TB * b + TB)
                name = stage.split("_")[0]
                t = slice(TPB * b, TPB * b + TPB)
                if stage == "patches":
                    for k in range(6):
                        job = (stage, b, 2 * k + 1)
                        o = read(dve, job)
                        dst = patchT[:, k, T // 2 * b:T // 2 * (b + 1)].rearrange("p (r w) -> p w r", w=GRID)[:, 3:6, :]
                        v.tensor_copy(dst, o[:, 0:3 * TP].rearrange("p (w r) -> p w r", w=3)).then_inc(S["patches_turned2"], 1)
                elif stage == "tok_shift":
                    job = (stage, b, 0)
                    dve.wait_ge(S["z_biased"], b + 1)
                    o = read(dve, job)
                    z, x = grid(o[:, 0:TB]), grid(tokT[:, tok])
                    n = GRID - 1
                    for q, (to, frm) in enumerate((((slice(0, GRID), slice(0, n)), (slice(0, GRID), slice(1, GRID))),
                                                   ((slice(0, GRID), slice(1, GRID)), (slice(0, GRID), slice(0, n))),
                                                   ((slice(0, n), slice(0, GRID)), (slice(1, GRID), slice(0, GRID))),
                                                   ((slice(1, GRID), slice(0, GRID)), (slice(0, n), slice(0, GRID))))):
                        p = slice(32 * q, 32 * q + 16)
                        last = v.tensor_tensor(x[p, :, to[0], to[1]], x[p, :, to[0], to[1]], z[p, :, frm[0], frm[1]], ALU.add)
                    last.then_inc(S["tok_added"], 1)
                elif stage == "tok_norm_a":
                    o = read(dve, ("tok_turn", b, 0))
                    moments(b, lambda i: o[0:TP, D * i:D * i + D]).then_inc(S["var"], 1)
                elif stage == "tok_norm_b":
                    job = ("tok_turn", b, 0)
                    o = bank(job)
                    normalise("tok", b, h, lambda i: o[0:TP, D * i:D * i + D]).then_inc(S["h_norm"], 1)
                    dve.wait_ge(S["h_norm"], b + 1)
                    st.link(v.tensor_tensor(h[:, t, :], h[:, t, :], row("L0_tok_ln_g"), ALU.mult))
                    st.link(v.tensor_tensor(h[:, t, :], h[:, t, :], row("L0_tok_ln_b"), ALU.add))
                elif stage == "src_norm_a":
                    moments(b, of(h, b)).then_inc(S["var"], 1)
                elif stage == "src_norm_b":
                    normalise(name, b, src, of(h, b)).then_inc(S["normed"], 1)
                elif stage == "rope_qk":
                    if b >= 1:
                        dve.wait_ge(S["q_ready"], b)
                        dve.wait_ge(S["k_full"], b)
                    for n in range(2):
                        for dst, table, j in ((rot_a, "cos", 2 * n), (rot_b, "sin", 2 * n + 1)):
                            job = (stage, b, j)
                            o = read(dve, job)
                            v.tensor_tensor(dst[:, n, :].rearrange("p (i s) -> p i s", s=SEQ), o[:, 0:TB].rearrange("p (i s) -> p i s", s=SEQ),
                                            const(table).unsqueeze(1).broadcast_to([D, IB, SEQ]), ALU.mult).then_inc(S["rot_parts"], 1)
                elif stage in ("rope_scores", "dif_scores", "moe_scores"):
                    for s in range(2 if stage == "dif_scores" else 1):
                        u = soft_n % 2
                        dve.wait_ge(S["s_full"], soft_n + 1)
                        sc = scores[0:SROWS, :, 0:SC].rearrange("p q (a k) -> p q a k", k=SEQ)
                        m3 = mx[:, u, :].rearrange("p (q a) -> p q a", q=QUADS)
                        st.link(v.tensor_reduce(m3, sc, AX_X, ALU.max))
                        if soft_n >= 2:
                            dve.wait_ge(S["probs_ready"], flip_of[-2] + 1)
                        e4 = ex[0:SROWS, u, :, :].rearrange("p q (a k) -> p q a k", k=SEQ)
                        v.tensor_tensor(e4, sc, m3.unsqueeze(3).broadcast_to([SROWS, QUADS, 2 * PAIRS, SEQ]), ALU.subtract
                                        ).then_inc(S["exp_in"], 1)
                        dve.wait_ge(S["exp_done"], soft_n + 1)
                        s3 = sm[:, u, :].rearrange("p (q a) -> p q a", q=QUADS)
                        st.link(v.tensor_reduce(s3, e4, AX_X, ALU.add))
                        if stage == "dif_scores" and s == 1:
                            st.link(v.reciprocal(s3, s3))
                            s4 = sm[:, u, :].rearrange("p (q i a) -> p q i a", q=QUADS, a=2)
                            l4 = lam[:, :].rearrange("p (q a) -> p q a", a=2).unsqueeze(2).broadcast_to([SROWS, QUADS, PAIRS, 2])
                            st.link(v.tensor_tensor(s4, s4, l4, ALU.mult))
                            st.link(v.tensor_tensor(e4, e4, s3.unsqueeze(3).broadcast_to([SROWS, QUADS, 2 * PAIRS, SEQ]), ALU.mult))
                            dve.wait_ge(S["flip_ready"], dif_n + 1)
                            if flip_n >= 2:
                                dve.wait_ge(S["pT_ready"], PAIRS * (flip_n - 1))
                            for q in range(QUADS):
                                last = v.tensor_tensor(probs[0:SROWS, flip_n % 2, q, :, :, 0:SEQ].rearrange("p a b k -> p (a b) k"),
                                                       ex[0:SROWS, 1 - u, q, :].rearrange("p (a k) -> p a k", k=SEQ),
                                                       ex[0:SROWS, u, q, :].rearrange("p (a k) -> p a k", k=SEQ), ALU.subtract)
                            last.then_inc(S["probs_ready"], 1)
                            dif_n += 1
                        else:
                            v.reciprocal(s3, s3).then_inc(S["sums_ready"], 1)
                        soft_n += 1
                        flip_of.append(flip_n)
                    flip_n += 1
                    if stage == "rope_scores" and b == 0:
                        dve.wait_ge(S["lam_ready"], 2)
                        st.link(v.tensor_tensor(lam[:, :], lambdas[:, 0, :], lambdas[:, 1, :], ALU.subtract))
                        st.link(v.tensor_scalar(lam[:, :], lam[:, :], 0.2, None, ALU.add))
                elif stage in ("rope_out", "net_out", "mix_out", "dif_out", "moe_out"):
                    job = (stage, b, 0)
                    if stage == "net_out":
                        dve.wait_ge(S["affine_ready"], b + 1)
                    o = read(dve, job)
                    base = {"rope": src, "net": mid, "mix": h, "dif": h, "moe": src}[name]
                    dst = {"rope": src, "net": src, "mix": h, "dif": h, "moe": src}[name]
                    last = v.tensor_tensor(dst[:, t, :], o[0:TP, 0:TPB * D].rearrange("p (n c) -> p n c", c=D), base[:, t, :], ALU.add)
                    last.then_inc(S["out_added"], 1)
                    dve.wait_ge(S["out_added"], out_count[stage, b])
                    if stage in ("mix_out", "dif_out"):
                        st.link(v.tensor_tensor(h[:, t, :], h[:, t, :], row("L0_ffn_b2" if name == "mix" else "L1_attn_out_b"), ALU.add))
                    if stage == "moe_out":
                        st.link(v.tensor_tensor(h[:, t, :], h[:, t, :], src[:, t, :], ALU.add))
                elif stage in ("x1_norm_a", "x2_norm_a", "rt_norm_a"):
                    moments(b, of(src, b)).then_inc(S["var"], 1)
                elif stage in ("mix_norm_a", "dif_norm_a", "moe_norm_a"):
                    moments(b, of(h, b)).then_inc(S["var"], 1)
                elif stage in ("x1_norm_b", "rt_norm_b"):
                    normalise(name, b, norm, of(src, b)).then_inc(S["normed"], 1)
                elif stage in ("mix_norm_b", "dif_norm_b"):
                    normalise(name, b, norm, of(h, b)).then_inc(S["normed"], 1)
                elif stage == "x2_norm_b":
                    st.step(normalise(name, b, norm, of(src, b)))
                    st.settle()
                    st.link(v.tensor_tensor(norm[:, t, :], norm[:, t, :], row("L0_attn_g2"), ALU.mult))
                    st.link(v.tensor_tensor(norm[:, t, :], norm[:, t, :], row("L0_attn_be2"), ALU.add))
                    st.link(v.tensor_tensor(h[:, t, :], h[:, t, :], norm[:, t, :], ALU.add))
                elif stage == "moe_norm_b":
                    st.step(normalise(name, b, src, of(h, b)))
                    st.settle()
                    for i in range(TPB):
                        g = TPB * b + i
                        last = v.tensor_scalar(norm[:, g, :], src[:, g, :], rstd[:, g, 1:2], None, ALU.mult)
                    last.then_inc(S["normed"], 1)
                elif stage == "gn_mean":
                    im = slice(IB * b, IB * b + IB)
                    dve.wait_ge(S["ctx_ready"], NB + b + 1)
                    c3 = ctxT[:, tok].rearrange("p (i s) -> p i s", s=SEQ)
                    v.tensor_reduce(gn_s[:, 0, im], c3, AX_X, ALU.add).then_inc(S["gn_stat"], 1)
                    job = (stage, b, 0)
                    o = read(dve, job)
                    v.tensor_scalar(gn_s[:, 1, im], o[:, 0:IB], 1.0 / GSIZE, None, ALU.mult).then_inc(S["gn_mean_back"], 1)
                    dve.wait_ge(S["gn_mean_back"], b + 1)
                    v.tensor_tensor(c3, c3, gn_s[:, 1, im].unsqueeze(2).broadcast_to([D, IB, SEQ]), ALU.subtract
                                    ).then_inc(S["gn_centred"], 1)
                elif stage == "gn_var":
                    im = slice(IB * b, IB * b + IB)
                    dve.wait_ge(S["square_ready"], square_n["gn_mean", b])
                    v.tensor_reduce(gn_s[:, 2, im], gn_q[:, b % 2, :].rearrange("p (i s) -> p i s", s=SEQ), AX_X, ALU.add
                                    ).then_inc(S["gn_stat"], 1)
                    job = (stage, b, 0)
                    o = read(dve, job)
                    v.tensor_scalar(gn_s[:, 3, im], o[:, 0:IB], 1.0 / GSIZE, None, ALU.mult).then_inc(S["gn_back"], 1)
                    dve.wait_ge(S["gn_ready"], b + 1)
                    c3 = ctxT[:, tok].rearrange("p (i s) -> p i s", s=SEQ)
                    v.tensor_tensor(c3, c3, gn_s[:, 3, im].unsqueeze(2).broadcast_to([D, IB, SEQ]), ALU.mult
                                    ).then_inc(S["gn_scaled"], 1)
                elif stage == "rt_logits":
                    job = (stage, b, 0)
                    o = read(dve, job)
                    v.tensor_copy(lg[:, t, :], o[0:TP, 0:TPB * E].rearrange("p (n e) -> p n e", e=E)).then_inc(S["logits_back"], 1)
                    dve.wait_ge(S["logits_back"], b + 1)
                    for g in range(TPB * b, TPB * b + TPB):
                        st.step(v.max(top[:, g, :], lg[:, g, :]))
                    st.settle()
                    for g in range(TPB * b, TPB * b + TPB):
                        st.step(v.max_index(top_i[:, g, :], top[:, g, :], lg[:, g, :]))
                    v.tensor_tensor(gate[:, t, 3], top[:, t, 1], top[:, t, 0], ALU.subtract).then_inc(S["logits_ready"], 1)
                    st.settle()
                    st.link(v.tensor_copy(top_f[:, t, :], top_i[:, t, 0:2]))
                    for k in range(2):
                        st.step(v.tensor_tensor(oh[:, k, t, :], const("iota_e", TP).unsqueeze(1).broadcast_to([TP, TPB, E]),
                                                top_f[:, t, k:k + 1].broadcast_to([TP, TPB, E]), ALU.is_equal))
                    st.settle()
                    st.link(v.tensor_tensor(oh_both[:, t, :], oh[:, 0, t, :], oh[:, 1, t, :], ALU.add))
                    for g in range(TPB * b, TPB * b + TPB):
                        last = v.tensor_tensor(run[:, g + 1, :], run[:, g, :], oh_both[:, g, :], ALU.add)
                        if g < TPB * b + TPB - 1:
                            st.link(last)
                    last.then_inc(S["picked"], 1)
                    dve.wait_ge(S["picked"], b + 1)
                elif stage == "rt_count":
                    dve.wait_ge(S["gate_exp"], b + 1)
                    st.link(v.tensor_scalar(gate[:, t, 3], gate[:, t, 2], 1.0, None, ALU.add))
                    st.link(v.reciprocal(gate[:, t, 0], gate[:, t, 3]))
                    st.link(v.tensor_tensor(gate[:, t, 1], gate[:, t, 2], gate[:, t, 0], ALU.mult))
                    job = (stage, b, 0)
                    o = read(dve, job)
                    cnt = o[0:TP, 0:TPB * E].rearrange("p (n e) -> p n e", e=E)
                    for k in range(2):
                        st.link(v.tensor_tensor(cum[:, :, :], cnt, oh[:, k, t, :], ALU.mult))
                        last = v.tensor_reduce(pos[:, t, k], cum[:, :, :], AX_X, ALU.add)
                        if k == 0:
                            st.link(last)
                    last.then_inc(S["placed"], 1)
                    dve.wait_ge(S["placed"], b + 1)
                    st.step(v.tensor_scalar(kept[:, t, :], pos[:, t, :], float(CAP), None, ALU.is_lt))
                    st.step(v.tensor_scalar(flat[:, t, :], top_f[:, t, :], float(CAP), None, ALU.mult))
                    st.settle()
                    st.link(v.tensor_tensor(flat[:, t, :], flat[:, t, :], pos[:, t, :], ALU.add))
                    st.step(v.tensor_copy(flat_u[:, 0, t, :], flat[:, t, :]))
                    st.step(v.tensor_tensor(gate[:, t, 0:2], gate[:, t, 0:2], kept[:, t, :], ALU.mult))
                    st.settle()
                    st.step(v.tensor_scalar(flat_u[:, 1, t, :], flat_u[:, 0, t, :], 127, None, ALU.bitwise_and))
                    st.step(v.tensor_scalar(flat_u[:, 2, t, :], flat_u[:, 0, t, :], 7, None, ALU.logical_shift_right))
                    st.settle()
                    for n in range(2):
                        st.step(v.tensor_copy(flat_f[:, n, t, :], flat_u[:, 1 + n, t, :]))
                    st.settle()
                    if b >= 1:
                        dve.wait_ge(S["map_full"], b)
                    for k in range(2):
                        st.step(v.tensor_tensor(lo1[:, k, :, :], const("iota_lo", TP).unsqueeze(1).broadcast_to([TP, TPB, D]),
                                                flat_f[:, 0, t, k:k + 1].broadcast_to([TP, TPB, D]), ALU.is_equal))
                        st.step(v.tensor_tensor(hi1[:, k, :, :], const("iota_hi", TP).unsqueeze(1).broadcast_to([TP, TPB, ST]),
                                                flat_f[:, 1, t, k:k + 1].broadcast_to([TP, TPB, ST]), ALU.is_equal))
                        st.settle()
                        st.link(v.tensor_tensor(hi1[:, k, :, :], hi1[:, k, :, :], kept[:, t, k:k + 1].broadcast_to([TP, TPB, ST]), ALU.mult))
                        ids = const("ids", TP).rearrange("p (n k) -> p n k", k=2)[:, t, k:k + 1].broadcast_to([TP, TPB, ST])
                        st.step(v.tensor_tensor(pay[:, k, :, 0:ST], hi1[:, k, :, :], ids, ALU.mult))
                        last = v.tensor_tensor(pay[:, k, :, ST:2 * ST], hi1[:, k, :, :], gate[:, t, k:k + 1].broadcast_to([TP, TPB, ST]), ALU.mult)
                        if k == 1:
                            last.then_inc(S["mapped"], 1)
                        else:
                            st.step(last)
                elif stage == "rt_map":
                    st.step(v.tensor_tensor(oh[:, 0, t, :], oh[:, 0, t, :], gate[:, t, 0:1].broadcast_to([TP, TPB, E]), ALU.mult))
                    st.step(v.tensor_tensor(oh[:, 1, t, :], oh[:, 1, t, :], gate[:, t, 1:2].broadcast_to([TP, TPB, E]), ALU.mult))
                    st.settle()
                    v.tensor_tensor(gm[:, t, :], oh[:, 0, t, :], oh[:, 1, t, :], ALU.add).then_inc(S["gm_ready"], 1)

            dve.wait_ge(S["map_full"], NB)
            st.step(v.memset(xe[:, SLOTS:SLOTS + WIN], 0.0))
            st.step(v.memset(hT[:, :, :, CAP:WIN], 0.0))
            st.link(v.tensor_copy(smap[:, :], scores[:, 0, 0:2 * ST]))
            st.step(v.tensor_scalar(smap2[:, 0, :], smap[:, 0:ST], 0.0, NOWHERE, ALU.is_equal, ALU.mult))
            st.step(v.tensor_scalar(get_u[:, 0, :], smap[:, 0:ST], 1.0, 1.0, ALU.max, ALU.subtract))
            st.settle()
            st.step(v.tensor_tensor(smap2[:, 1, :], smap2[:, 0, :], smap[:, 0:ST], ALU.add))
            st.step(v.tensor_scalar(get_u[:, 1, :], get_u[:, 0, :], 1, None, ALU.logical_shift_right))
            st.settle()
            v.tensor_scalar(put_u[:, :], smap2[:, 1, :], 1.0, None, ALU.subtract).then_inc(S["map_ready"], 1)
            for kind, i in moe_order:
                job = (kind, i, 0)
                if kind == "take":
                    o = read(dve, job)
                    v.tensor_copy(xe[:, D * i:D * i + D], o[:, 0:D]).then_inc(S["xe_ready"], 1)
                elif kind == "expert":
                    o = read(dve, job)
                    v.tensor_copy(yT[:, CAP * i:CAP * i + CAP], o[:, 0:CAP]).then_inc(S["yT_ready"], 1)
                elif kind == "bias_turn":
                    o = read(dve, job)
                    v.tensor_copy(gmT[:, i, :], o[0:E, 0:TB]).then_inc(S["gmT_ready"], 1)
                elif kind == "bias":
                    o = read(dve, job)
                    t = slice(TPB * i, TPB * i + TPB)
                    v.tensor_tensor(h[:, t, :], o[0:TP, 0:TPB * D].rearrange("p (n c) -> p n c", c=D), h[:, t, :], ALU.add
                                    ).then_inc(S["bias_added"], 1)
            for b in range(NB):
                t = slice(TPB * b, TPB * b + TPB)
                dve.wait_ge(S["back_in"], 16 * NB)
                y = back_of(b)
                st.link(v.tensor_tensor(res[:, t, :], h[:, t, :], y[:, :, 0:D], ALU.add))
                v.tensor_tensor(res[:, t, :], res[:, t, :], y[:, :, D:2 * D], ALU.add).then_inc(S["final_ready"], 1)


def kernel(**inputs):
    import numpy as _np
    import concourse.bacc as _bacc
    from concourse import mybir as _mybir
    from concourse.bass_utils import run_bass_kernel_spmd as _run

    nc = _bacc.Bacc("TRN2", target_bir_lowering=False, num_devices=1)
    arrays, args = {}, {}
    for name, value in list(inputs.items()) + [("const", constants())]:
        a = _np.ascontiguousarray(value)
        arrays[f"in_{name}"] = a
        args[name] = nc.dram_tensor(f"in_{name}", a.shape, _mybir.dt.from_np(a.dtype), kind="ExternalInput").ap()
    out = nc.dram_tensor("out_0", (IMG, SEQ, D), F32, kind="ExternalOutput").ap()
    build(nc, args, out)
    r = _run(nc, [arrays], core_ids=[0])
    return r.results[0]["out_0"]
```

```python
from contextlib import ExitStack

import numpy as np

import concourse.bass as bass
from concourse import mybir

ALU = mybir.AluOpType
ACT = mybir.ActivationFunctionType
F32 = mybir.dt.float32
BF16 = mybir.dt.bfloat16
U32 = mybir.dt.uint32
AX_X = mybir.AxisListType.X

D = 128
H = 8
HD = D // H
QUADS = 4
IMG = 32
CH, PX, GRID = 3, 16, 6
SIDE = PX * GRID
SEQ = GRID * GRID
T = IMG * SEQ
NB = 4
IB = IMG // NB
TB = T // NB
TP = 96
TPB = TB // TP
NT = T // TP
PAIRS = IB // 2
HALF = 64
SROWS = HALF + SEQ
F0 = 512
FC = F0 // D
E, FF = 64, 512
CAP = 2 * (T * 2 // E)
SLOTS = E * CAP
ST = SLOTS // D
WIN = 96
IDLE = 0.5
AGE = 500
RING = 10
LENT = 9
NG = 6
WORK = 17536
EPS = 1e-5
BEYOND = 8192.0
NOWHERE = 1.0e6
GSIZE = D // 4 * SEQ

CONST = {}
_at = 0
for _name, _n in (("ident", D), ("swap", D), ("order", D), ("group", D), ("parity", 2), ("cos", SEQ), ("sin", SEQ),
                  ("iota_e", E), ("iota_lo", D), ("iota_hi", ST), ("before", TP), ("ids", 2 * NT)):
    CONST[_name] = (_at, _n)
    _at += _n
CONST_COLS = _at

BLOCKS = {}
_at = 0
for _name, _n in (("tok", 6), ("L0_attn_Wq", 1), ("L0_attn_Wk", 1), ("L0_attn_Wv", 1), ("L0_attn_Wo", 1),
                  ("L0_attn_W1", FC), ("L0_attn_W2", FC), ("L0_ffn_W1", 1), ("L0_ffn_W2", 1),
                  ("L1_attn_Q1_w", 1), ("L1_attn_K1_w", 1), ("L1_attn_Q2_w", 1), ("L1_attn_K2_w", 1),
                  ("L1_attn_V_w", 1), ("L1_attn_out_w", 1)):
    BLOCKS[_name] = (_at, _n)
    _at += _n
NBLOCKS = _at
DIRECT = ["L1_ffn_wq", "L1_ffn_wk", "L1_ffn_wv", "L1_ffn_wo"]
ROWS = ["L0_tok_ln_g", "L0_tok_ln_b", "L0_attn_g1", "L0_attn_be1", "L0_attn_b2", "L0_attn_g2", "L0_attn_be2",
        "L0_ffn_b2", "L1_attn_out_b", "L1_ffn_ln2_g", "L1_ffn_ln2_b"]
COLS = ["L0_attn_g1", "L0_attn_be1", "L0_ffn_b1", "L1_attn_K1_b", "L1_attn_K2_b", "L1_attn_gn_w", "L1_attn_gn_b",
        "L1_ffn_ln1_g", "L1_ffn_ln1_b", "L1_ffn_ln2_g", "L1_ffn_ln2_b"]
NCOLS = len(COLS) + FC + 1
LAMBDAS = ["L1_attn_lambda_q1", "L1_attn_lambda_k1", "L1_attn_lambda_q2", "L1_attn_lambda_k2"]


def constants():
    c = np.zeros((D, CONST_COLS), np.float32)

    def put(name, value):
        a, n = CONST[name]
        value = np.asarray(value, np.float32)
        c[:value.shape[0], a:a + n] = value

    put("ident", np.eye(D))
    f = np.arange(D)
    q, r = f // 32, f % 32
    partner = np.where(r < 16, f ^ 32, -1)
    swap = np.zeros((D, D))
    swap[partner[r < 16], f[r < 16]] = 1
    put("swap", swap)
    order = np.zeros((D, D))
    order[f, np.where(r < 16, 64 + 16 * q + r, 16 * q + r - 16)] = 1
    put("order", order)
    put("group", (f[:, None] // 32 == f[None, :] // 32))
    put("parity", np.stack([(f // HD) % 2 == 0, (f // HD) % 2 == 1], 1))
    half = HD // 2
    inv = (np.float32(1.0) / np.float32(10000.0) ** (np.arange(0, HD, 2, dtype=np.float32) / np.float32(HD)))
    angle = (np.arange(SEQ, dtype=np.float32)[:, None] * inv.astype(np.float32)[None, :]).astype(np.float32)
    d = f % HD
    put("cos", np.cos(angle)[:, d % half].T)
    put("sin", (np.sin(angle)[:, d % half] * np.where(d < half, -1.0, 1.0)).T)
    put("iota_e", np.tile(np.arange(E), (D, 1)))
    put("iota_lo", np.tile(np.arange(D), (D, 1)))
    put("iota_hi", np.tile(np.arange(ST), (D, 1)))
    t = np.arange(TP)
    put("before", t[:, None] < t[None, :])
    ids = np.zeros((TP, NT, 2))
    for k in range(2):
        ids[:, :, k] = 2 * (np.arange(NT)[None, :] * TP + t[:, None]) + k + 1
    put("ids", ids.reshape(TP, -1))
    return c


STAGES = """
    tok_z        PE 2985 ACT 699
    tok_shift    PE 560 DVE 1399
    tok_turn     PE 729 ACT 499
    tok_norm_a   DVE 999 POOL 1699
    tok_norm_b   ACT 1199 POOL 2100
    src_norm_a   DVE 1000 POOL 1699
    src_norm_b   ACT 1300
    src_turn     PE 374 ACT 399
    rope_qk      PE 3075 DVE 1600 POOL 1600 ACT 899
    rope_v       PE 2364 ACT 1199
    rope_scores  PE 2740 DVE 2700 ACT 1100
    rope_sums    DVE 1799 POOL 2600
    rope_flip    PE 1698 ACT 1199
    rope_pv      PE 1162 ACT 299
    rope_out     PE 810 DVE 499
    x1_norm_a    DVE 999 POOL 1699
    x1_norm_b    ACT 1199 POOL 3100
    x1_turn      PE 374 ACT 500
    net_in       PE 2625 ACT 1600
    net_out      PE 2994 DVE 499
    x2_norm_a    DVE 1000 POOL 1699
    x2_norm_b    ACT 1199 POOL 2100 DVE 500
    mix_norm_a   DVE 999 POOL 1699
    mix_norm_b   ACT 1199
    mix_turn     PE 375 ACT 399
    mix_in       PE 765 ACT 500
    mix_out      PE 810 DVE 500
    dif_norm_a   DVE 999 POOL 1699
    dif_norm_b   ACT 1299
    dif_turn     PE 374 ACT 400
    dif_qk       PE 2780 ACT 2600
    dif_v        PE 2345 ACT 1399
    dif_scores   PE 2740 DVE 2699 ACT 1100
    dif_scores2  PE 3532 DVE 2699 ACT 1100
    dif_sums     DVE 1699 POOL 2600
    dif_sums2    DVE 1999 POOL 2600
    dif_mix      DVE 1600
    dif_flip     PE 2043 ACT 1199
    dif_pv       PE 1395 ACT 399
    gn_sum       DVE 499 PE 139
    gn_center    DVE 600 ACT 400
    gn_var       DVE 400 PE 168
    gn_rstd      DVE 100 POOL 2299
    gn_apply     DVE 400 ACT 499
    dif_out      PE 1089 DVE 500
    moe_norm_a   DVE 999 POOL 3299
    moe_norm_b   ACT 2199
    moe_turn     PE 585 ACT 799
    moe_qk       PE 2014 ACT 1799
    moe_v        PE 2728 ACT 1200
    moe_scores   PE 2765 DVE 2699 ACT 1100
    moe_sums     DVE 1799 POOL 2600
    moe_flip     PE 2423 ACT 1299
    moe_pv       PE 1389 ACT 400
    moe_out      PE 1009 DVE 499
    rt_norm_a    DVE 1000 POOL 1699
    rt_norm_b    ACT 1200 POOL 4699
    rt_turn      PE 489 ACT 600
    rt_logits    PE 804 ACT 299 DVE 2299
    rt_gate      POOL 1100 ACT 199 DVE 600
    rt_count     PE 490 DVE 3400 POOL 1100
    rt_map       PE 1779 DVE 200 POOL 1799
"""


ORDER_FOUND = """
    tok_z:0 tok_shift:0 tok_z:1 tok_turn:0 tok_norm_a:0 tok_norm_b:0 tok_shift:1 tok_z:2 tok_turn:1 tok_norm_a:1
    tok_z:3 src_norm_a:0 tok_shift:2 tok_shift:3 tok_norm_b:1 src_norm_b:0 src_norm_a:1 tok_turn:2 tok_norm_a:2
    src_turn:0 src_norm_b:1 rope_qk:0 src_turn:1 tok_norm_b:2 tok_turn:3 tok_norm_a:3 rope_v:0 src_norm_a:2
    src_norm_b:2 rope_qk:1 tok_norm_b:3 rope_scores:0 rope_sums:0 src_turn:2 rope_v:1 rope_qk:2 src_norm_a:3
    rope_flip:0 src_norm_b:3 rope_scores:1 rope_pv:0 rope_sums:1 src_turn:3 rope_v:2 rope_out:0 rope_qk:3
    x1_norm_a:0 rope_flip:1 x1_norm_b:0 rope_scores:2 rope_pv:1 rope_v:3 rope_sums:2 rope_out:1 x1_turn:0
    x1_norm_a:1 x1_norm_b:1 rope_scores:3 rope_flip:2 rope_sums:3 net_in:0 rope_pv:2 rope_out:2 x1_norm_a:2
    x1_turn:1 rope_flip:3 net_out:0 x1_norm_b:2 rope_pv:3 x2_norm_a:0 rope_out:3 x1_norm_a:3 x1_turn:2 x2_norm_b:0
    net_in:1 x1_norm_b:3 mix_norm_a:0 net_in:2 net_out:1 x2_norm_a:1 x1_turn:3 mix_norm_b:0 x2_norm_b:1 net_in:3
    mix_turn:0 net_out:2 mix_in:0 mix_norm_a:1 mix_norm_b:1 mix_out:0 dif_norm_a:0 x2_norm_a:2 net_out:3
    dif_norm_b:0 x2_norm_a:3 dif_turn:0 x2_norm_b:2 mix_turn:1 x2_norm_b:3 mix_norm_a:2 dif_qk:0 mix_in:1 dif_v:0
    mix_norm_a:3 mix_out:1 dif_norm_a:1 mix_norm_b:2 dif_norm_b:1 dif_scores:0 mix_turn:2 mix_norm_b:3 dif_turn:1
    dif_scores2:0 mix_in:2 mix_turn:3 dif_qk:1 dif_sums:0 mix_out:2 dif_norm_a:2 mix_in:3 dif_sums2:0 dif_v:1
    dif_norm_b:2 mix_out:3 dif_mix:0 dif_scores:1 dif_norm_a:3 dif_turn:2 dif_flip:0 dif_scores2:1 dif_pv:0 dif_qk:2
    dif_sums:1 gn_sum:0 gn_center:0 dif_norm_b:3 dif_v:2 dif_sums2:1 dif_turn:3 gn_var:0 dif_mix:1 dif_scores:2
    dif_flip:1 gn_rstd:0 gn_apply:0 dif_scores2:2 dif_sums:2 dif_pv:1 dif_qk:3 gn_sum:1 gn_center:1 gn_var:1 dif_v:3
    gn_rstd:1 dif_sums2:2 gn_apply:1 dif_out:0 dif_mix:2 dif_scores:3 moe_norm_a:0 dif_out:1 dif_flip:2 moe_norm_a:1
    moe_norm_b:0 dif_scores2:3 dif_sums:3 moe_turn:0 dif_pv:2 moe_qk:0 gn_sum:2 dif_sums2:3 moe_norm_b:1 gn_center:2
    moe_v:0 gn_var:2 gn_rstd:2 moe_turn:1 dif_mix:3 gn_apply:2 moe_scores:0 dif_flip:3 dif_out:2 moe_qk:1
    moe_norm_a:2 moe_sums:0 dif_pv:3 gn_sum:3 moe_norm_b:2 gn_center:3 moe_v:1 gn_var:3 gn_rstd:3 gn_apply:3
    moe_turn:2 moe_scores:1 dif_out:3 moe_flip:0 moe_norm_a:3 moe_sums:1 moe_qk:2 moe_norm_b:3 moe_pv:0 moe_v:2
    moe_turn:3 moe_out:0 rt_norm_a:0 rt_norm_b:0 moe_flip:1 moe_qk:3 moe_scores:2 moe_sums:2 moe_pv:1 moe_v:3
    moe_out:1 rt_turn:0 rt_norm_a:1 rt_norm_b:1 moe_scores:3 moe_sums:3 moe_flip:2 rt_logits:0 moe_pv:2 moe_out:2
    rt_turn:1 rt_norm_a:2 rt_logits:1 moe_flip:3 rt_gate:0 rt_gate:1 rt_norm_b:2 moe_pv:3 moe_out:3 rt_norm_a:3
    rt_count:0 rt_turn:2 rt_norm_b:3 rt_logits:2 rt_map:0 rt_count:1 rt_turn:3 rt_logits:3 rt_gate:2 rt_map:1
    rt_count:2 rt_gate:3 rt_map:2 rt_count:3 rt_map:3
"""


def plan():
    return [("patches", 0), ("patches", 1), ("prepare", 0)] + [(w.split(":")[0], int(w.split(":")[1])) for w in ORDER_FOUND.split()]


def plan0():
    stages = [line.split() for line in STAGES.split("\n") if line.strip()]
    names = [s[0] for s in stages]
    work = {s[0]: [(s[i], int(s[i + 1])) for i in range(1, len(s), 2)] for s in stages}
    must = {(name, b): set() for name in names for b in range(NB)}

    def series(*parts):
        return [(part, b) for part in parts for b in range(NB)]

    def follow(first, then, lag):
        for n in range(lag, len(then)):
            if first[n - lag] != then[n]:
                must[then[n]].add(first[n - lag])

    for i, name in enumerate(names):
        follow(series(name), series(name), 1)
        if i:
            follow(series(names[i - 1]), series(name), 0)
    kinds = {k: series(*(f"{part}_{k}" for part in ("rope", "dif", "moe"))) for k in ("qk", "v", "scores", "sums", "flip", "pv")}
    kinds["turn"] = series("src_turn", "dif_turn", "moe_turn")
    kinds["probs"] = series("rope_sums", "dif_mix", "moe_sums")
    for k in kinds.values():
        follow(k, k, 1)
    follow(kinds["v"], kinds["turn"], 2)
    follow(kinds["qk"], kinds["turn"], 2)
    follow(series("rope_scores", "dif_scores2", "moe_scores"), kinds["qk"], 2)
    follow(kinds["pv"], kinds["v"], 2)
    follow(kinds["pv"], kinds["flip"], 2)
    follow(kinds["flip"], kinds["probs"], 2)
    soft = series("rope_scores") + [(s, b) for b in range(NB) for s in ("dif_scores", "dif_scores2")] + series("moe_scores")
    used = series("rope_sums") + [("dif_mix", b) for b in range(NB) for s in range(2)] + series("moe_sums")
    follow(soft, soft, 1)
    follow(used, soft, 2)
    follow(series("net_in", "rt_logits"), series("x1_turn", "rt_turn"), 2)
    follow(series("mix_in"), series("mix_turn"), 2)
    follow(series("net_in", "mix_in"), series("net_in", "mix_in"), 1)
    follow(series("net_out", "mix_out"), series("net_in", "mix_in"), 2)
    follow(series("rt_map"), series("rt_count"), 1)
    follow(series("gn_var"), series("gn_center"), 2)

    must["rope_scores", 0].add(("tok_z", NB - 1))
    must["rope_sums", 0].add(("tok_norm_a", NB - 1))
    must["rope_flip", 0].add(("tok_turn", NB - 1))

    order = [("patches", 0), ("patches", 1), ("prepare", 0)]
    free = {"PE": 0, "ACT": 0, "DVE": 0, "POOL": 0}
    done = {}
    while len(done) < len(must):
        best = None
        for item, need in must.items():
            if item in done or any(n not in done for n in need):
                continue
            name, b = item
            i = names.index(name)
            ready = done[names[i - 1], b] if i else 0
            t, idle = ready, 0
            for eng, cost in work[name]:
                begin = max(t, free[eng])
                idle += begin - free[eng]
                t = begin + cost
            start = max(ready, free[work[name][0][0]])
            key = (start + IDLE * idle + AGE * b, -i)
            if best is None or key < best[0]:
                best = (key, item)
        item = best[1]
        i = names.index(item[0])
        t = done[names[i - 1], item[1]] if i else 0
        for eng, cost in work[item[0]]:
            t = max(t, free[eng]) + cost
            free[eng] = t
        done[item] = t
        order.append(item)
    return order


JOBS = {"prepare": (NBLOCKS + 4 + 3) // 4, "patches": 12, "tok_z": 1, "tok_shift": 1, "tok_turn": 1,
        "src_turn": 1, "rope_qk": 4, "rope_v": 2, "rope_flip": PAIRS, "rope_pv": 1, "rope_out": 1,
        "x1_turn": 1, "net_in": FC, "net_out": 1, "mix_turn": 1, "mix_in": 1, "mix_out": 1,
        "dif_turn": 1, "dif_qk": 4, "dif_v": 2, "dif_flip": PAIRS, "dif_pv": 1, "gn_sum": 1, "gn_var": 1, "dif_out": 1,
        "moe_turn": 1, "moe_qk": 2, "moe_v": 2, "moe_flip": PAIRS, "moe_pv": 1, "moe_out": 1,
        "rt_turn": 1, "rt_logits": 1, "rt_count": 1, "rt_map": 1}


def build(nc, ins, out):
    ORDER = plan()
    job_number = {}
    for stage, b in ORDER:
        for i in range(JOBS.get(stage, 0)):
            job_number[stage, b, i] = len(job_number)
    moe_order = []
    turned = 0
    returned = 0
    for e in range(E + 1):
        if e < E:
            need = min(ST, (min(e + 3, E - 1) * CAP + WIN - 1) // D + 1)
            while turned < need:
                moe_order.append(("take", turned))
                turned += 1
            moe_order.append(("hidden", e))
        if e >= 1:
            moe_order.append(("expert", e - 1))
            while (returned + 1) * D <= (e - 1) * CAP:
                moe_order.append(("give", returned))
                returned += 1
        if 8 <= e < 8 + NB:
            moe_order.append(("bias_turn", e - 8))
            moe_order.append(("bias", e - 8))
    while returned < ST:
        moe_order.append(("give", returned))
        returned += 1
    for kind, i in moe_order:
        job_number[kind, i, 0] = len(job_number)

    jobs = list(job_number)
    turned_parts = ("src", "x1", "mix", "dif", "moe", "rt")
    normed_parts = ("tok", "x2") + turned_parts
    out_count_stages = ("rope_out", "net_out", "mix_out", "dif_out", "moe_out")

    def counts(names):
        found = {}
        for stage, b in ORDER:
            if stage in names:
                found[stage, b] = len(found) + 1
        return found

    normed_count = {(s.split("_")[0], b): n for (s, b), n in counts([p + "_norm_b" for p in normed_parts]).items()}
    turned_count = {(s.split("_")[0], b): n for (s, b), n in counts([p + "_turn" for p in turned_parts]).items()}
    rstd_count = {(s.split("_")[0], b): n for (s, b), n in counts({s for s, _ in ORDER if s.endswith("norm_a")}).items()}
    out_count = counts(out_count_stages)
    base_count = counts(("mix_norm_b", "dif_norm_b"))
    square_n = counts(("gn_center", "gn_apply"))
    gn_n = counts(("gn_sum", "gn_var"))

    ctx = ExitStack()
    with ctx:
        def sb(name, shape, dt=F32):
            return ctx.enter_context(nc.sbuf_tensor(name, shape, dt))

        def sem(name):
            return ctx.enter_context(nc.semaphore(name))

        SC = PAIRS * 2 * SEQ

        scores = ctx.enter_context(nc.psum_tensor("scores", [D, QUADS, 512], F32))
        banks = [ctx.enter_context(nc.psum_tensor(f"bank{i}", [D, 512], F32)) for i in range(4)]
        bank_full = [sem(f"bank{i}_full") for i in range(4)]

        ring = sb("ring", [D, RING, 1024])
        xs = ring[:, RING - LENT:, :].rearrange("p a b -> p (a b)")[:, 0:2 * CH * PX * SIDE].rearrange(
            "p (h c y x) -> p h c y x", h=2, c=CH, y=PX)
        cst = sb("cst", [D, CONST_COLS])

        def const(name, rows=D):
            a, n = CONST[name]
            return cst[0:rows, a:a + n]

        PW = QUADS * PAIRS * 2 * HALF
        work = sb("work", [D, WORK])

        class Share:
            def __init__(self):
                self.at = 0

            def take(self, shape, dt=F32):
                n = int(np.prod(shape))
                a = work[:, self.at:self.at + n]
                self.at += n
                assert self.at <= WORK, self.at
                names = "abcdef"[:len(shape)]
                return a.rearrange(f"p ({' '.join(names)}) -> p {' '.join(names)}", **dict(zip(names, shape)))

        first = Share()
        wnat = first.take([NBLOCKS, D])
        wshift = first.take([6 * D])
        b1nat = first.take([FF])[0:E, :]
        piece = first.take([2, GRID, PX, PX])
        early = first.at
        patchT = first.take([6, T])
        zraw = first.take([T])
        tokT = first.take([T])
        second = Share()
        qT = second.take([2, 2, TB])
        kT = second.take([2, TB])
        rot_a = second.take([2, TB])
        rot_b = second.take([2, TB])
        kM = second.take([2, 2, 2, TB])
        vd = second.take([2, IB, D])
        assert second.at <= early
        second.at = early
        ex = second.take([2, QUADS, SC])
        probs = second.take([2, QUADS, PAIRS, 2, HALF])
        pT = second.take([2, QUADS, PAIRS, 2, SEQ])
        ctxT = second.take([T])
        third = Share()
        xe = third.take([SLOTS + WIN])
        yT = third.take([SLOTS])
        hT = third.take([3, FC, WIN])
        got = third.take([NG, D])
        ys = third.take([4, D])
        gmT = third.take([NB, TB])[0:E]

        wT = sb("wT", [D, NBLOCKS, D])
        wdir = sb("wdir", [D, len(DIRECT), D])
        wrot = sb("wrot", [D, 2, D])
        wr = sb("wr", [D, E])
        rows = sb("rows", [TP, len(ROWS), D])
        crows = sb("crows", [NCOLS, D])
        cols = sb("cols", [D, NCOLS])
        tok_bias = cols[:, NCOLS - 1:NCOLS]
        net_bias = cols[:, len(COLS):len(COLS) + FC]
        masked_bias = sb("masked_bias", [D, 2, 2])
        lambdas = sb("lambdas", [SROWS, 4, H])
        lam = sb("lam", [SROWS, H])
        mh = sb("mh", [D, TPB])
        b1T = sb("b1T", [D, FC, E])
        b2nat = sb("b2nat", [E, D])

        h = sb("h", [TP, NT, D])
        src = sb("src", [TP, NT, D])
        mid = sb("mid", [TP, NT, D])
        norm = sb("norm", [TP, NT, D])
        xT = sb("xT", [D, 2, 2, TB])
        hid = sb("hid", [D, FC, 2, TB])
        xTp = sb("xTp", [D, 2, IB + 1, HALF])
        res = norm
        stats = sb("stats", [TP, 2, TPB, 6])
        mv = sb("mv", [TP, NT, 2])
        rstd = sb("rstd", [TP, NT, 3])
        mx = sb("mx", [SROWS, 2, QUADS * PAIRS * 2])
        sm = sb("sm", [SROWS, 2, QUADS * PAIRS * 2])
        gn_s = sb("gn_s", [D, 4, IMG])
        gn_q = sb("gn_q", [D, 2, TB])
        lg = sb("lg", [TP, NT, E])
        top = sb("top", [TP, NT, 8])
        top_i = sb("top_i", [TP, NT, 8], U32)
        top_f = sb("top_f", [TP, NT, 2])
        gate = sb("gate", [TP, NT, 4])
        oh = sb("oh", [TP, NT, 2, E])
        oh_both = sb("oh_both", [TP, NT, E], BF16)
        run = sb("run", [TP, NB + 1, E], BF16)
        before16 = sb("before16", [TP, TP], BF16)
        ones16 = sb("ones16", [TP, TP], BF16)
        cum = sb("cum", [TP, TPB, 2, E])
        pos = sb("pos", [TP, NT, 2])
        flat = sb("flat", [TP, NT, 2])
        far = sb("far", [TP, NT, 2])
        flat_u = sb("flat_u", [TP, 3, NT, 2], U32)
        flat_f = sb("flat_f", [TP, 2, NT, 2])
        kept = sb("kept", [TP, NT, 2])
        kept_gate = sb("kept_gate", [TP, NT, 2])
        lo1 = sb("lo1", [TP, TPB, 2, D])
        hi1 = sb("hi1", [TP, TPB, 2, ST])
        pay = sb("pay", [TP, TPB, 2, 2 * ST])
        gm = sb("gm", [TP, NT, E])
        smap = sb("smap", [D, 2 * ST])
        smap2 = sb("smap2", [D, 2, ST])
        put_u = sb("put_u", [D, ST], U32)
        get_u = sb("get_u", [D, 2, ST], U32)

        x2d = nc.dram_tensor("x2_rows", [T, D], F32, kind="Internal").ap()
        ytok = nc.dram_tensor("expert_rows", [2 * T, D], F32, kind="Internal").ap()

        names = """piece_even piece_odd w_in const_in small_in zero_in zeros16 tok_back v_pads probs_pads scores_zero w_made blocks_turned b1_turned
            tri_made rot_made patches_turned patches_turned2 z_raw z_biased tok_added h_norm var rstd_ready
            normed x_turned rot_parts q_ready k_full k_ready v_ready s_full exp_in exp_done sums_ready
            probs_ready map_scaled ctx_ready gn_stat gn_back gn_ready out_added affine_ready hid_ready
            mask_ready x2_stored logits_ready picked mapped map_added run_ready hi_ready paid split map_ready xe_ready h_full yT_ready ys_ready
            back_in x2_ready base_ready h_summed src_ready stored gm_ready gmT_ready bias_added lam_ready square_ready pT_ready gn_mean_back gn_centred
            gn_scaled logits_back placed gate_exp dve_step act_step pool_step final_ready
           """.split()
        S = {n: sem(n) for n in names}
        x_in = [[sem(f"x_in{half}_{c}") for c in range(CH)] for half in range(2)]
        w_here = [sem(f"expert_here{i}") for i in range(RING)]
        got_here = [sem(f"got{i}") for i in range(NG)]
        ys_gone = [sem(f"ys_gone{i}") for i in range(4)]

        def bank(job):
            n = job_number[job]
            return banks[n % 4]

        def fill(pe, job):
            n = job_number[job]
            if n >= 4:
                name, count = taken(jobs[n - 4])
                pe.wait_ge(S[name], count)
            return banks[n % 4]

        def filled(job):
            return bank_full[job_number[job] % 4]

        def read(eng, job):
            n = job_number[job]
            eng.wait_ge(bank_full[n % 4], n // 4 + 1)
            return banks[n % 4]

        def taken(job):
            stage, b, i = job
            part = stage.split("_")[0]
            at = {"rope": 0, "dif": 1, "moe": 2}.get(part, 0) * NB + b
            if stage == "prepare":
                return ("b1_turned", 1) if i == JOBS[stage] - 1 else ("blocks_turned", i + 1)
            if stage == "patches":
                return ("patches_turned2" if i % 2 else "patches_turned"), 6 * b + i // 2 + 1
            if stage.endswith("_turn") and part in turned_parts:
                return "x_turned", turned_count[part, b]
            if stage in ("rope_v", "dif_v", "moe_v"):
                return "v_ready", 4 * at + 2 * i + 2
            if stage in ("rope_flip", "dif_flip", "moe_flip"):
                return "pT_ready", PAIRS * at + i + 1
            if stage in ("rope_pv", "dif_pv", "moe_pv"):
                return "ctx_ready", at + 1
            if stage in out_count_stages:
                return "out_added", out_count[stage, b]
            return {
                "tok_z": ("z_biased", b + 1), "tok_shift": ("tok_added", b + 1), "tok_turn": ("tok_back", b + 1),
                "rope_qk": ("rot_parts", 4 * b + i + 1),
                "net_in": ("hid_ready", FC * b + i + 1), "mix_in": ("hid_ready", FC * NB + b + 1),
                "dif_qk": ("k_ready", 2 * NB + 4 * b + i + 1) if i % 2 else ("q_ready", NB + 2 * b + i // 2 + 1),
                "moe_qk": ("k_ready", 6 * NB + 2 * b + 2) if i % 2 else ("q_ready", 3 * NB + b + 1),
                "gn_sum": ("gn_mean_back", b + 1), "gn_var": ("gn_back", b + 1),
                "rt_logits": ("logits_back", b + 1), "rt_count": ("placed", b + 1),
                "rt_map": ("map_added", b + 1),
                "take": ("xe_ready", b + 1), "hidden": ("h_full", b + 1), "expert": ("yT_ready", b + 1),
                "give": ("ys_ready", b + 1), "bias_turn": ("gmT_ready", b + 1), "bias": ("bias_added", b + 1),
            }[stage]

        class Steps:

            def __init__(self, eng, s):
                self.eng, self.s, self.n = eng, s, 0

            def step(self, ins):
                ins.then_inc(self.s, 1)
                self.n += 1

            def link(self, ins):
                self.step(ins)
                self.eng.wait_ge(self.s, self.n)

            def settle(self):
                self.eng.wait_ge(self.s, self.n)

        def block_of(name, i=0):
            return wT[:, BLOCKS[name][0] + i, :]

        def row(name):
            return rows[:, ROWS.index(name), :].unsqueeze(1).broadcast_to([TP, TPB, D])

        def col(name):
            i = COLS.index(name)
            return cols[:, i:i + 1]

        def tiles(t, b):
            return t[:, TPB * b:TPB * b + TPB, :]

        def x_of(stage, b):
            return xT[:, 1 if stage.startswith("mix") else 0, b % 2, :]

        def grid(ap):
            return ap.rearrange("p (i r c) -> p i r c", r=GRID, c=GRID)

        NDMA = {}
        def back_of(b):
            return ring[0:TP, b, 0:TPB * 2 * D].rearrange("p (n c) -> p n c", n=TPB)

        def cut(eng, k, copy, done):
            half, c, y = k // (2 * CH), k // 2 % CH, PX // 2 * (k % 2)
            eng.wait_ge(x_in[half][c], 16)
            if k >= 4:
                eng.wait_ge(S["patches_turned"], k - 3)
                eng.wait_ge(S["patches_turned2"], k - 3)
            copy(piece[0:TP, k // 2 % 2, :, y:y + PX // 2, :],
                 xs[0:TP, half, c, y:y + PX // 2, :].rearrange("p y (w x) -> p w y x", x=PX)).then_inc(done, 1)

        block = ctx.enter_context(nc.Block())

        def load_patch_weights(eng, s):
            n = 0

            def go(dst, source):
                nonlocal n
                eng.dma_start(dst, source).then_inc(s, 16)
                n += 16

            wn = wnat[:, 0:6, :].rearrange("p k f -> p (k f)")
            for q in range(QUADS):
                go(wn[32 * q + 16:32 * q + 32, :], ins["L0_tok_W_main"][16 * q:16 * q + 16, :])
                go(wshift[32 * q:32 * q + 16, :], ins["L0_tok_W_sx" if q < 2 else "L0_tok_W_sy"])
            bias = crows[NCOLS - 1:NCOLS, :].rearrange("a (q s d) -> a q s d", q=QUADS, s=2)
            go(bias[:, :, 1, :], ins["L0_tok_b_main"].rearrange("(a q d) -> a q d", a=1, q=QUADS))
            for q in range(QUADS):
                go(bias[:, q, 0, :], ins["L0_tok_b_sx" if q < 2 else "L0_tok_b_sy"].rearrange("(a d) -> a d", a=1))
            return n

        PATCH_WEIGHTS = 16 * (2 * QUADS + 1 + QUADS)

        def load_small(eng, s):
            n = 0

            def go(dst, source):
                nonlocal n
                eng.dma_start(dst, source).then_inc(s, 16)
                n += 16

            for name in ("L0_attn_Wq", "L0_attn_Wk", "L0_attn_Wv", "L0_attn_Wo", "L0_ffn_W1", "L0_ffn_W2", "L1_attn_Q1_w",
                         "L1_attn_K1_w", "L1_attn_Q2_w", "L1_attn_K2_w", "L1_attn_V_w", "L1_attn_out_w"):
                go(wnat[:, BLOCKS[name][0], :], ins[name])
            a = BLOCKS["L0_attn_W1"][0]
            go(wnat[:, a:a + FC, :], ins["L0_attn_W1"].rearrange("(m p) i -> p m i", p=D))
            a = BLOCKS["L0_attn_W2"][0]
            go(wnat[:, a:a + FC, :], ins["L0_attn_W2"].rearrange("o (m f) -> o m f", f=D))
            for i, name in enumerate(DIRECT):
                go(wdir[:, i, :], ins[name])
            go(wr[:, :], ins["L1_ffn_wr"])
            for i, name in enumerate(ROWS):
                go(rows[:, i, :], ins[name].partition_broadcast(TP))
            for i, name in enumerate(COLS):
                go(crows[i:i + 1, :], ins[name].rearrange("(a p) -> a p", a=1))
            go(crows[len(COLS):len(COLS) + FC, :], ins["L0_attn_b1"].rearrange("(m p) -> m p", p=D))
            for i, name in enumerate(LAMBDAS):
                go(lambdas[:, i, :], ins[name].rearrange("h a -> (h a)").partition_broadcast(SROWS))
            go(b1nat[:, :], ins["L1_ffn_b1"])
            go(b2nat[:, :], ins["L1_ffn_b2"])
            return n

        SMALL = 16 * (12 + 2 + 4 + 1 + len(ROWS) + len(COLS) + 1 + 4 + 2)

        @block.sync
        def _(sp):
            sp.dma_start(cst[:, :], ins["const"]).then_inc(S["const_in"], 16)
            for half in range(2):
                for c in range(CH):
                    a = IMG // 2 * half
                    sp.dma_start(xs[0:TP, half, c, :, :].rearrange("p y x -> p (y x)"),
                                 ins["x"][a:a + IMG // 2, c].rearrange("i (r y) x -> i r (y x)", y=PX)).then_inc(x_in[half][c], 16)
                if half == 0:
                    sp.wait_ge(S["zeros16"], 1)
                    assert load_patch_weights(sp, S["w_in"]) == PATCH_WEIGHTS
            assert load_small(sp, S["small_in"]) == SMALL
            for e in range(E):
                s = e % RING
                if e == RING - LENT:
                    sp.wait_ge(S["patches_turned"], 12)
                    sp.wait_ge(S["patches_turned2"], 12)
                if e >= RING:
                    sp.wait_ge(S["yT_ready"], e - RING + 1)
                sp.dma_start(ring[:, s, 0:FF], ins["L1_ffn_w1"][e]).then_inc(w_here[s], 16)
                sp.dma_start(ring[:, s, FF:2 * FF].rearrange("p (c n) -> p c n", n=D),
                             ins["L1_ffn_w2"][e].rearrange("(c p) n -> p c n", p=D)).then_inc(w_here[s], 16)
            sp.wait_ge(S["yT_ready"], E)
            for i in range(4):
                sp.wait_ge(ys_gone[i], 16 * (ST // 4))
            for b in range(NB):
                sp.dma_start(back_of(b), ytok.rearrange("(n p k) c -> p n (k c)", p=TP, k=2)[:, TPB * b:TPB * b + TPB, :]
                             ).then_inc(S["back_in"], 16)
            for b in range(NB):
                sp.wait_ge(S["final_ready"], b + 1)
                sp.dma_start(out.rearrange("i s c -> (i s) c").rearrange("(n p) c -> p n c", p=TP)[:, TPB * b:TPB * b + TPB, :],
                             tiles(res, b)).then_inc(S["stored"], 16)
            sp.wait_ge(S["stored"], 16 * NB)

        @block.gpsimd
        def _(pool):
            st = Steps(pool, S["pool_step"])
            pool.memset(wnat[:, 0:6, :], 0.0).then_inc(S["zeros16"], 1)
            st.step(pool.memset(mh[:, :], -0.5))
            st.step(pool.memset(xTp[:, :, :, :], 0.0))
            pool.memset(run[:, 0, :], 0.0).then_inc(S["run_ready"], 1)
            st.step(pool.memset(ones16[:, :], 1.0))
            pool.wait_ge(S["w_in"], PATCH_WEIGHTS)
            st.settle()
            wn = wnat[:, 0:6, :].rearrange("p k f -> p (k f)")
            w5 = wn.rearrange("p (c y x) -> p c y x", c=CH, y=PX)
            s5 = wshift[:, :].rearrange("p (c y x) -> p c y x", c=CH, y=PX)
            hp = PX // 2
            pool.tensor_copy(w5[0:16, :, :, hp:PX], s5[0:16, :, :, 0:hp]).then_inc(S["w_made"], 1)
            pool.tensor_copy(w5[32:48, :, :, 0:hp], s5[32:48, :, :, hp:PX]).then_inc(S["w_made"], 1)
            pool.tensor_copy(w5[64:80, :, hp:PX, :], s5[64:80, :, 0:hp, :]).then_inc(S["w_made"], 1)
            pool.tensor_copy(w5[96:112, :, 0:hp, :], s5[96:112, :, hp:PX, :]).then_inc(S["w_made"], 1)
            pool.wait_ge(S["w_made"], 4)
            pool.wait_ge(S["const_in"], 16)
            pool.tensor_copy(before16[:, :], const("before", TP)).then_inc(S["tri_made"], 1)
            pool.wait_ge(S["tri_made"], 1)
            st.link(pool.memset(mid[:, :, :], 0.0))
            for k in range(2):
                pool.dma_start(ytok.rearrange("(k p n) c -> k p (n c)", k=2, p=TP)[k], mid[:, :, :].rearrange("p n c -> p (n c)")
                               ).then_inc(S["zero_in"], 16)
            pool.wait_ge(S["zero_in"], 32)
            pool.wait_ge(S["b1_turned"], 1)
            for n, name in enumerate(("L1_attn_K1_b", "L1_attn_K2_b")):
                for a in range(2):
                    pool.tensor_tensor(masked_bias[:, n, a:a + 1], col(name), const("parity")[:, a:a + 1], ALU.mult
                                       ).then_inc(S["mask_ready"], 1)
            pool.wait_ge(S["blocks_turned"], (NBLOCKS + 3) // 4)
            for name in ("L0_ffn_W1", "L0_ffn_W2"):
                w = block_of(name)
                pool.affine_select(out=w, in_=w, compare_op=ALU.is_ge, fill=0.0, base=0, pattern=[[1, D]],
                                   channel_multiplier=-1).then_inc(S["tri_made"], 1)
            for n, name in enumerate(("L0_attn_Wq", "L0_attn_Wk")):
                w = block_of(name).rearrange("p (h a d) -> p h a d", h=H, a=2)
                r = wrot[:, n, :].rearrange("p (h a d) -> p h a d", h=H, a=2)
                for a in range(2):
                    pool.tensor_copy(r[:, :, a, :], w[:, :, 1 - a, :]).then_inc(S["rot_made"], 1)

            var_n = 0

            def rsqrt(b, twice=False):
                nonlocal var_n
                var_n += 1
                pool.wait_ge(S["var"], var_n)
                v = mv[:, TPB * b:TPB * b + TPB, 1]
                r = rstd[:, TPB * b:TPB * b + TPB, 0]
                r2 = rstd[:, TPB * b:TPB * b + TPB, 1]
                m = mv[:, TPB * b:TPB * b + TPB, 0]
                n = rstd[:, TPB * b:TPB * b + TPB, 2]
                st.link(pool.tensor_scalar(r2, v, EPS, None, ALU.add))
                if not twice:
                    st.link(pool.tensor_tensor(r, r2, mh[0:TP, 0:TPB], ALU.pow))
                    st.link(pool.tensor_tensor(n, m, r, ALU.mult))
                    pool.tensor_scalar(n, n, -1.0, None, ALU.mult).then_inc(S["rstd_ready"], 1)
                    return
                st.link(pool.tensor_tensor(r, r2, mh[0:TP, 0:TPB], ALU.pow))
                st.link(pool.tensor_tensor(n, m, r, ALU.mult))
                st.step(pool.tensor_scalar(n, n, -1.0, None, ALU.mult))
                st.link(pool.tensor_tensor(r2, r, r, ALU.mult))
                st.link(pool.tensor_tensor(r2, r2, v, ALU.mult))
                st.link(pool.tensor_scalar(r2, r2, EPS, None, ALU.add))
                pool.tensor_tensor(r2, r2, mh[0:TP, 0:TPB], ALU.pow).then_inc(S["rstd_ready"], 1)

            sums_n = flips = 0
            for stage, b in ORDER:
                tok = slice(TB * b, TB * b + TB)
                if stage == "tok_z" and b == 0:
                    pool.wait_ge(S["patches_turned"], 12)
                    pool.wait_ge(S["patches_turned2"], 12)
                    pool.memset(vd[:, :, :, :], 0.0).then_inc(S["v_pads"], 1)
                if stage.endswith("norm_a"):
                    rsqrt(b, twice=stage.startswith("moe"))
                if stage == "tok_norm_a" and b == NB - 1:
                    pool.wait_ge(S["z_biased"], NB)
                    pool.memset(probs[:, :, :, :, :, SEQ:HALF], 0.0).then_inc(S["probs_pads"], 1)
                if stage == "tok_norm_b":
                    pool.wait_ge(S["normed"], normed_count["tok", b])
                    st.link(pool.tensor_tensor(tiles(h, b), tiles(h, b), row("L0_tok_ln_g"), ALU.mult))
                    pool.tensor_tensor(tiles(h, b), tiles(h, b), row("L0_tok_ln_b"), ALU.add).then_inc(S["h_norm"], 1)
                if stage == "x2_norm_b":
                    pool.wait_ge(S["normed"], normed_count["x2", b])
                    st.link(pool.tensor_tensor(tiles(norm, b), tiles(norm, b), row("L0_attn_g2"), ALU.mult))
                    pool.tensor_tensor(tiles(norm, b), tiles(norm, b), row("L0_attn_be2"), ALU.add).then_inc(S["x2_ready"], 1)
                if stage in ("mix_norm_b", "dif_norm_b"):
                    pool.tensor_tensor(tiles(mid, b), tiles(h, b), row("L0_ffn_b2" if stage[0] == "m" else "L1_attn_out_b"), ALU.add
                                       ).then_inc(S["base_ready"], 1)
                if stage == "rt_gate":
                    pool.wait_ge(S["picked"], b + 1)
                    pool.wait_ge(S["run_ready"], b + 1)
                    g = TPB * b
                    st.link(pool.tensor_tensor(run[:, b + 1, :], run[:, b, :], oh_both[:, g, :], ALU.add))
                    for i in range(1, TPB):
                        last = pool.tensor_tensor(run[:, b + 1, :], run[:, b + 1, :], oh_both[:, g + i, :], ALU.add)
                        if i < TPB - 1:
                            st.link(last)
                    last.then_inc(S["run_ready"], 1)
                if stage == "rt_count":
                    t = slice(TPB * b, TPB * b + TPB)
                    pool.wait_ge(S["hi_ready"], b + 1)
                    ids = const("ids", TP).rearrange("p (n k) -> p n k", k=2)[:, t, :].unsqueeze(3).broadcast_to([TP, TPB, 2, ST])
                    st.step(pool.tensor_tensor(pay[:, :, :, 0:ST], hi1[:, :, :, :], ids, ALU.mult))
                    pool.tensor_tensor(pay[:, :, :, ST:2 * ST], hi1[:, :, :, :], gate[:, t, 0:2].unsqueeze(3).broadcast_to([TP, TPB, 2, ST]),
                                       ALU.mult).then_inc(S["paid"], 1)
                if stage == "rt_map":
                    t = slice(TPB * b, TPB * b + TPB)
                    st.link(pool.tensor_tensor(kept_gate[:, t, :], gate[:, t, 0:2], kept[:, t, :], ALU.mult))
                    st.link(pool.tensor_tensor(oh[:, t, :, :], oh[:, t, :, :], kept_gate[:, t, :].unsqueeze(3).broadcast_to([TP, TPB, 2, E]), ALU.mult))
                    pool.tensor_tensor(gm[:, t, :], oh[:, t, 0, :], oh[:, t, 1, :], ALU.add).then_inc(S["gm_ready"], 1)
                if stage == "rt_norm_b":
                    pool.wait_ge(S["out_added"], out_count["moe_out", b])
                    pool.tensor_tensor(tiles(h, b), tiles(h, b), tiles(src, b), ALU.add).then_inc(S["h_summed"], 1)
                if stage == "rope_qk":
                    pool.wait_ge(S["rot_parts"], 4 * b + 2)
                    pool.tensor_tensor(qT[:, b % 2, 0, :], rot_a[:, 0, :], rot_b[:, 0, :], ALU.add).then_inc(S["q_ready"], 1)
                    pool.wait_ge(S["rot_parts"], 4 * b + 4)
                    pool.tensor_tensor(kT[:, b % 2, :], rot_a[:, 1, :], rot_b[:, 1, :], ALU.add).then_inc(S["k_full"], 1)
                if stage in ("rope_sums", "moe_sums", "dif_sums", "dif_sums2"):
                    if sums_n == 0:
                        pool.wait_ge(S["probs_pads"], 1)
                    pool.wait_ge(S["sums_ready"], sums_n + 1)
                    if stage[:3] != "dif" and flips >= 2:
                        pool.wait_ge(S["pT_ready"], PAIRS * (flips - 1))
                    s = sums_n % 2
                    for q in range(QUADS):
                        e3 = ex[0:SROWS, s, q, :].rearrange("p (a k) -> p a k", k=SEQ)
                        to = e3 if stage[:3] == "dif" else probs[0:SROWS, flips % 2, q, :, :, 0:SEQ].rearrange("p a b k -> p (a b) k")
                        last = pool.tensor_tensor(
                            to, e3, sm[:, s, 2 * PAIRS * q:2 * PAIRS * (q + 1)].unsqueeze(2).broadcast_to([SROWS, 2 * PAIRS, SEQ]), ALU.mult)
                    last.then_inc(S["map_scaled" if stage[:3] == "dif" else "probs_ready"], 1)
                    sums_n += 1
                    flips += stage != "dif_sums"
                if stage == "gn_rstd":
                    pool.wait_ge(S["gn_back"], b + 1)
                    im = slice(IB * b, IB * b + IB)
                    st.link(pool.tensor_scalar(gn_s[:, 3, im], gn_s[:, 3, im], EPS, None, ALU.add))
                    st.link(pool.tensor_tensor(gn_s[:, 3, im], gn_s[:, 3, im], mh[:, 0:1].broadcast_to([D, IB]), ALU.pow))
                    pool.tensor_scalar(gn_s[:, 3, im], gn_s[:, 3, im], col("L1_attn_gn_w"), 0.0, ALU.mult, ALU.add
                                       ).then_inc(S["gn_ready"], 1)
                if stage == "x1_norm_b":
                    pool.wait_ge(S["normed"], normed_count["x1", b])
                    st.link(pool.tensor_tensor(tiles(mid, b), tiles(norm, b), row("L0_attn_g1"), ALU.mult))
                    st.link(pool.tensor_tensor(tiles(mid, b), tiles(mid, b), row("L0_attn_be1"), ALU.add))
                    pool.tensor_tensor(tiles(mid, b), tiles(mid, b), row("L0_attn_b2"), ALU.add).then_inc(S["affine_ready"], 1)
                if stage == "rt_norm_b":
                    pool.wait_ge(S["normed"], normed_count["rt", b])
                    st.link(pool.tensor_tensor(tiles(mid, b), tiles(norm, b), row("L1_ffn_ln2_g"), ALU.mult))
                    st.link(pool.tensor_tensor(tiles(mid, b), tiles(mid, b), row("L1_ffn_ln2_b"), ALU.add))
                    pool.dma_start(x2d.rearrange("(n p) c -> p n c", p=TP)[:, TPB * b:TPB * b + TPB, :], tiles(mid, b)
                                   ).then_inc(S["x2_stored"], 16)

            pool.wait_ge(S["map_ready"], 1)
            pool.wait_ge(S["x2_stored"], 16 * NB)
            gathered = 0

            def gather(i):
                if i >= NG:
                    pool.wait_ge(S["xe_ready"], i - NG + 1)
                pool.indirect_dma_start(out=got[:, i % NG, :], out_offset=None, in_=x2d[:, :],
                                        in_offset=bass.IndirectOffsetOnAxis(ap=get_u[:, 1, i:i + 1], axis=0)
                                        ).then_inc(got_here[i % NG], 16)

            for kind, i in moe_order:
                if kind == "take":
                    while gathered < min(ST, i + 3):
                        gather(gathered)
                        gathered += 1
                if kind == "give":
                    pool.wait_ge(S["ys_ready"], i + 1)
                    pool.indirect_dma_start(out=ytok[:, :], out_offset=bass.IndirectOffsetOnAxis(ap=put_u[:, i:i + 1], axis=0),
                                            in_=ys[:, i % 4, :], in_offset=None, bounds_check=2 * T - 1, oob_is_err=False
                                            ).then_inc(ys_gone[i % 4], 16)

        @block.tensor
        def _(pe):
            def mm(o, a, b, start=True, stop=True):
                return nc.tensor.matmul(o, a, b, start=start, stop=stop)

            x_turned = {"n": 0}

            def turn(stage, b):
                job = (stage, b, 0)
                o = fill(pe, job)
                source = src if stage == "src_turn" else norm
                pe.wait_ge(S["normed"], normed_count[stage.split("_")[0], b])
                for i in range(TPB):
                    last = nc.tensor.transpose(o[:, TP * i:TP * i + TP], source[:, TPB * b + i, :], const("ident")[0:TP, 0:TP])
                last.then_inc(filled(job), 1)

            def features(job, w, b, n=None):
                o = fill(pe, job)
                x = x_of(job[0], b) if job[0] in ("net_in", "mix_in") else xTp[:, b % 2, 0:IB, 0:SEQ]
                mm(o[:, 0:TB], w, x).then_inc(filled(job), 1)

            def tokens(job, lhs, rhs_list, width=D):
                o = fill(pe, job)
                for i in range(TPB):
                    for k, rhs in enumerate(rhs_list):
                        last = mm(o[0:TP, width * i:width * i + width], lhs(k, i), rhs, start=(k == 0), stop=(k == len(rhs_list) - 1))
                last.then_inc(filled(job), 1)

            def values(stage, b, w):
                for half in range(2):
                    job = (stage, b, half)
                    o = fill(pe, job)
                    for i in range(IB // 2):
                        at = IB // 2 * half + i
                        last = mm(o[:, D * i:D * i + D], xTp[:, b % 2, at:at + 2, :].rearrange("p i s -> p (i s)"), w)
                    last.then_inc(filled(job), 1)

            def score(n, b, s):
                if n >= 1:
                    pe.wait_ge(S["exp_in"], n)
                else:
                    pe.wait_ge(S["scores_zero"], 1)
                for p in range(PAIRS):
                    for a in range(2):
                        t = SEQ * (2 * p + a)
                        for q in range(QUADS):
                            last = mm(scores[HALF * a:HALF * a + SEQ, q, 2 * SEQ * p:2 * SEQ * (p + 1)],
                                      qT[32 * q:32 * q + 32, b % 2, s, t:t + SEQ], kM[32 * q:32 * q + 32, b % 2, s, :, t:t + SEQ])
                last.then_inc(S["s_full"], 1)

            def flip(stage, b, n):
                pe.wait_ge(S["probs_ready"], n + 1)
                for p in range(PAIRS):
                    job = (stage, b, p)
                    o = fill(pe, job)
                    for q in range(QUADS):
                        last = nc.tensor.transpose(o[:, SROWS * q:SROWS * (q + 1)],
                                                   probs[0:SROWS, n % 2, q, p, :, :].rearrange("p a k -> p (a k)"),
                                                   const("ident")[0:SROWS, 0:SROWS])
                    last.then_inc(filled(job), 1)

            def weigh(stage, b, n):
                job = (stage, b, 0)
                o = fill(pe, job)
                pe.wait_ge(S["v_ready"], 4 * (n + 1))
                pe.wait_ge(S["pT_ready"], PAIRS * (n + 1))
                for p in range(PAIRS):
                    for a in range(2):
                        i = 2 * p + a
                        for q in range(QUADS):
                            last = mm(o[32 * q:32 * q + 32, SEQ * i:SEQ * i + SEQ], vd[:, b % 2, i, 32 * q:32 * q + 32],
                                      pT[:, n % 2, q, p, a, :])
                last.then_inc(filled(job), 1)

            score_n = 0
            flip_n = 0
            pv_n = 0
            pe.wait_ge(S["const_in"], 16)
            for stage, b in ORDER:
                def ctx_tile(k, i):
                    return ctxT[:, TB * b + TP * i:TB * b + TP * i + TP]

                if stage == "prepare":
                    pe.wait_ge(S["w_made"], 4)
                    pe.wait_ge(S["small_in"], SMALL)
                    for j in range(JOBS["prepare"] - 1):
                        o = fill(pe, (stage, 0, j))
                        for i in range(4 * j, min(4 * j + 4, NBLOCKS)):
                            last = nc.tensor.transpose(o[:, D * (i % 4):D * (i % 4) + D], wnat[:, i, :], const("ident"))
                        last.then_inc(filled((stage, 0, j)), 1)
                    job = (stage, 0, JOBS["prepare"] - 1)
                    o = fill(pe, job)
                    for c in range(FC):
                        last = nc.tensor.transpose(o[:, E * c:E * c + E], b1nat[:, D * c:D * c + D], const("ident")[0:E, 0:E])
                    pe.wait_ge(S["w_in"], PATCH_WEIGHTS)
                    last = nc.tensor.transpose(o[:, FC * E:FC * E + NCOLS], crows[:, :], const("ident")[0:NCOLS, 0:NCOLS])
                    last.then_inc(filled(job), 1)
                elif stage == "patches":
                    for k in range(6):
                        pe.wait_ge(S["piece_odd" if k % 2 else "piece_even"], (6 * b + k) // 2 + 1)
                        for g in range(2):
                            job = (stage, b, 2 * k + g)
                            o = fill(pe, job)
                            for w in range(3):
                                last = nc.tensor.transpose(o[:, TP * w:TP * w + TP],
                                                           piece[0:TP, (CH * b + k // 2) % 2, 3 * g + w, 8 * (k % 2):8 * (k % 2) + 8, :]
                                                           .rearrange("p y x -> p (y x)"),
                                                           const("ident")[0:TP, 0:TP])
                            last.then_inc(filled(job), 1)
                elif stage == "tok_z":
                    pe.wait_ge(S["patches_turned"], 6 * (b // 2 + 1))
                    pe.wait_ge(S["patches_turned2"], 6 * (b // 2 + 1))
                    if b == 0:
                        pe.wait_ge(S["blocks_turned"], (NBLOCKS + 3) // 4)
                    job = (stage, b, 0)
                    o = fill(pe, job)
                    for k in range(6):
                        last = mm(o[:, 0:TB], wT[:, k, :], patchT[:, k, TB * b:TB * b + TB], start=(k == 0), stop=(k == 5))
                    last.then_inc(filled(job), 1)
                elif stage == "tok_shift":
                    pe.wait_ge(S["z_raw"], b + 1)
                    job = (stage, b, 0)
                    o = fill(pe, job)
                    mm(o[:, 0:TB], const("swap"), zraw[:, TB * b:TB * b + TB]).then_inc(filled(job), 1)
                elif stage == "tok_turn":
                    pe.wait_ge(S["tok_added"], b + 1)
                    tokens((stage, b, 0), lambda k, i: tokT[:, TB * b + TP * i:TB * b + TP * i + TP], [const("order")])
                elif stage in ("src_turn", "x1_turn", "mix_turn", "dif_turn", "moe_turn", "rt_turn"):
                    turn(stage, b)
                elif stage == "rope_qk":
                    pe.wait_ge(S["x_turned"], turned_count["src", b])
                    if b == 0:
                        pe.wait_ge(S["rot_made"], 4)
                    for j, w in enumerate((block_of("L0_attn_Wq"), wrot[:, 0, :], block_of("L0_attn_Wk"), wrot[:, 1, :])):
                        features((stage, b, j), w, b)
                elif stage == "rope_v":
                    if b == 0:
                        pe.wait_ge(S["v_pads"], 1)
                    values(stage, b, block_of("L0_attn_Wv"))
                elif stage == "rope_scores":
                    pe.wait_ge(S["q_ready"], b + 1)
                    pe.wait_ge(S["k_ready"], 2 * (b + 1))
                    score(score_n, b, 0)
                    score_n += 1
                elif stage in ("rope_flip", "dif_flip", "moe_flip"):
                    flip(stage, b, flip_n)
                    flip_n += 1
                elif stage in ("rope_pv", "dif_pv", "moe_pv"):
                    weigh(stage, b, pv_n)
                    pv_n += 1
                elif stage in ("rope_out", "moe_out"):
                    pe.wait_ge(S["ctx_ready"], NB * (2 if stage == "moe_out" else 0) + b + 1)
                    tokens((stage, b, 0), ctx_tile, [block_of("L0_attn_Wo") if stage == "rope_out" else wdir[:, 3, :]])
                elif stage == "net_in":
                    pe.wait_ge(S["x_turned"], turned_count["x1", b])
                    for m in range(FC):
                        features((stage, b, m), block_of("L0_attn_W1", m), b)
                elif stage == "net_out":
                    pe.wait_ge(S["hid_ready"], 4 * (b + 1))
                    tokens((stage, b, 0), lambda k, i: hid[:, k, b % 2, TP * i:TP * i + TP],
                           [block_of("L0_attn_W2", m) for m in range(FC)])
                elif stage == "mix_in":
                    pe.wait_ge(S["x_turned"], turned_count["mix", b])
                    if b == 0:
                        pe.wait_ge(S["tri_made"], 3)
                    features((stage, b, 0), block_of("L0_ffn_W1"), b)
                elif stage == "mix_out":
                    pe.wait_ge(S["hid_ready"], 4 * NB + b + 1)
                    tokens((stage, b, 0), lambda k, i: hid[:, 0, b % 2, TP * i:TP * i + TP], [block_of("L0_ffn_W2")])
                elif stage == "dif_qk":
                    pe.wait_ge(S["x_turned"], turned_count["dif", b])
                    for j, w in enumerate(("L1_attn_Q1_w", "L1_attn_K1_w", "L1_attn_Q2_w", "L1_attn_K2_w")):
                        features((stage, b, j), block_of(w), b)
                elif stage == "dif_v":
                    values(stage, b, block_of("L1_attn_V_w"))
                elif stage in ("dif_scores", "dif_scores2"):
                    s = int(stage == "dif_scores2")
                    pe.wait_ge(S["q_ready"], NB + 2 * b + s + 1)
                    pe.wait_ge(S["k_ready"], 2 * NB + 4 * b + 2 * s + 2)
                    score(score_n, b, s)
                    score_n += 1
                elif stage == "gn_sum":
                    job = (stage, b, 0)
                    o = fill(pe, job)
                    pe.wait_ge(S["gn_stat"], gn_n[stage, b])
                    mm(o[:, 0:IB], const("group"), gn_s[:, 0, IB * b:IB * b + IB]).then_inc(filled(job), 1)
                elif stage == "gn_var":
                    job = (stage, b, 0)
                    o = fill(pe, job)
                    pe.wait_ge(S["gn_stat"], gn_n[stage, b])
                    mm(o[:, 0:IB], const("group"), gn_s[:, 2, IB * b:IB * b + IB]).then_inc(filled(job), 1)
                elif stage == "dif_out":
                    pe.wait_ge(S["square_ready"], square_n["gn_apply", b])
                    tokens((stage, b, 0), ctx_tile, [block_of("L1_attn_out_w")])
                elif stage == "moe_qk":
                    pe.wait_ge(S["x_turned"], turned_count["moe", b])
                    for j in range(2):
                        features((stage, b, j), wdir[:, j, :], b)
                elif stage == "moe_v":
                    values(stage, b, wdir[:, 2, :])
                elif stage == "moe_scores":
                    pe.wait_ge(S["q_ready"], 3 * NB + b + 1)
                    pe.wait_ge(S["k_ready"], 6 * NB + 2 * (b + 1))
                    score(score_n, b, 0)
                    score_n += 1
                elif stage == "rt_logits":
                    pe.wait_ge(S["x_turned"], turned_count["rt", b])
                    tokens((stage, b, 0), lambda k, i: x_of(stage, b)[:, TP * i:TP * i + TP], [wr[:, :]], width=E)
                elif stage == "rt_count":
                    pe.wait_ge(S["picked"], b + 1)
                    pe.wait_ge(S["run_ready"], b + 1)
                    job = (stage, b, 0)
                    o = fill(pe, job)
                    for i in range(TPB):
                        to = o[0:TP, E * i:E * i + E]
                        mm(to, before16[:, :], oh_both[:, TPB * b + i, :], start=True, stop=False)
                        for j in range(i):
                            mm(to, ones16[:, :], oh_both[:, TPB * b + j, :], start=False, stop=False)
                        last = mm(to, ones16[:, :], run[:, b, :], start=False, stop=True)
                    last.then_inc(filled(job), 1)
                elif stage == "rt_map":
                    pe.wait_ge(S["mapped"], b + 1)
                    pe.wait_ge(S["paid"], b + 1)
                    job = (stage, b, 0)
                    o = fill(pe, job)
                    for i in range(TPB):
                        for k in range(2):
                            last = mm(o[:, 0:2 * ST], lo1[:, i, k, :], pay[:, i, k, :],
                                      start=(i == 0 and k == 0), stop=(i == TPB - 1 and k == 1))
                    last.then_inc(filled(job), 1)

            for kind, i in moe_order:
                job = (kind, i, 0)
                o = fill(pe, job)
                if kind == "take":
                    pe.wait_ge(got_here[i % NG], 16 * (i // NG + 1))
                    nc.tensor.transpose(o[:, 0:D], got[:, i % NG, :], const("ident")).then_inc(filled(job), 1)
                elif kind == "hidden":
                    e, s = i, i % RING
                    pe.wait_ge(S["xe_ready"], min(ST, (e * CAP + WIN - 1) // D + 1))
                    pe.wait_ge(w_here[s], 32 * (e // RING + 1))
                    for c in range(FC):
                        last = mm(o[:, WIN * c:WIN * c + WIN], ring[:, s, D * c:D * c + D], xe[:, CAP * e:CAP * e + WIN])
                    last.then_inc(filled(job), 1)
                elif kind == "expert":
                    e, s = i, i % RING
                    pe.wait_ge(S["h_full"], e + 1)
                    for c in range(FC):
                        last = mm(o[:, 0:WIN], ring[:, s, FF + D * c:FF + D * c + D], hT[:, e % 3, c, :], start=(c == 0), stop=(c == FC - 1))
                    last.then_inc(filled(job), 1)
                elif kind == "give":
                    pe.wait_ge(S["yT_ready"], min(E, -(-(i + 1) * D // CAP)))
                    nc.tensor.transpose(o[:, 0:D], yT[:, D * i:D * i + D], const("ident")).then_inc(filled(job), 1)
                elif kind == "bias_turn":
                    pe.wait_ge(S["gm_ready"], NB)
                    for t in range(TPB):
                        last = nc.tensor.transpose(o[0:E, TP * t:TP * t + TP], gm[:, TPB * i + t, :], const("ident")[0:TP, 0:TP])
                    last.then_inc(filled(job), 1)
                elif kind == "bias":
                    pe.wait_ge(S["gmT_ready"], i + 1)
                    for t in range(TPB):
                        last = mm(o[0:TP, D * t:D * t + D], gmT[:, i, TP * t:TP * t + TP], b2nat[:, :])
                    last.then_inc(filled(job), 1)

        @block.scalar
        def _(act):
            def go(o, i, f=ACT.Copy, **kw):
                return nc.scalar.activation(o, i, f, **kw)

            flip_n = 0
            soft_n = 0
            v_n = 0
            st = Steps(act, S["act_step"])
            for stage, b in ORDER:
                name = stage.split("_")[0]
                tok = slice(TB * b, TB * b + TB)
                if stage == "prepare":
                    for j in range(JOBS["prepare"] - 1):
                        n = min(4 * j + 4, NBLOCKS) - 4 * j
                        o = read(act, (stage, 0, j))
                        go(wT[:, 4 * j:4 * j + n, :], o[:, 0:D * n].rearrange("p (k f) -> p k f", f=D)).then_inc(S["blocks_turned"], 1)
                    job = (stage, 0, JOBS["prepare"] - 1)
                    o = read(act, job)
                    go(cols[:, :], o[:, FC * E:FC * E + NCOLS])
                    go(b1T[:, :, :], o[:, 0:FC * E].rearrange("p (c e) -> p c e", e=E)).then_inc(S["b1_turned"], 1)
                    act.wait_ge(S["lam_ready"], 1)
                    go(lambdas[:, 0:2, :], lambdas[:, 0:2, :], ACT.Exp).then_inc(S["lam_ready"], 1)
                elif stage == "patches":
                    if b == 0:
                        cut(act, 1, go, S["piece_odd"])
                    for k in range(6):
                        if k % 2 and 6 * b + k + 2 < 12:
                            cut(act, 6 * b + k + 2, go, S["piece_odd"])
                        job = (stage, b, 2 * k)
                        o = read(act, job)
                        dst = patchT[:, k, T // 2 * b:T // 2 * (b + 1)].rearrange("p (r w) -> p w r", w=GRID)[:, 0:3, :]
                        go(dst, o[:, 0:3 * TP].rearrange("p (w r) -> p w r", w=3)).then_inc(S["patches_turned"], 1)
                elif stage == "tok_z":
                    if b == 0:
                        act.wait_ge(S["b1_turned"], 1)
                    job = (stage, b, 0)
                    o = read(act, job)
                    go(zraw[:, tok], o[:, 0:TB]).then_inc(S["z_raw"], 1)
                    go(tokT[:, tok], o[:, 0:TB], ACT.Identity, bias=tok_bias[:, 0:1]).then_inc(S["z_biased"], 1)
                elif stage == "tok_turn":
                    o = read(act, (stage, b, 0))
                    go(tiles(h, b), o[0:TP, 0:TPB * D].rearrange("p (n c) -> p n c", c=D)).then_inc(S["tok_back"], 1)
                elif stage.endswith("_norm_b"):
                    source = {"tok": h, "src": h, "x1": src, "x2": src, "mix": h, "dif": h, "moe": h, "rt": src}[name]
                    dst = {"tok": h, "src": src, "moe": src}.get(name, norm)
                    act.wait_ge(S["rstd_ready"], rstd_count[name, b])
                    for g in range(TPB * b, TPB * b + TPB):
                        last = go(dst[:, g, :], source[:, g, :], ACT.Identity, scale=rstd[:, g, 0:1], bias=rstd[:, g, 2:3])
                    if name == "moe":
                        last.then_inc(S["src_ready"], 1)
                        act.wait_ge(S["src_ready"], b + 1)
                        for g in range(TPB * b, TPB * b + TPB):
                            last = go(norm[:, g, :], src[:, g, :], ACT.Identity, scale=rstd[:, g, 1:2])
                    last.then_inc(S["normed"], 1)
                elif stage in ("src_turn", "mix_turn", "dif_turn"):
                    job = (stage, b, 0)
                    o = read(act, job)
                    dst, again, u = x_of(stage, b), None, o[:, 0:TB]
                    if stage != "mix_turn":
                        dst, again, u = xTp[:, b % 2, 0:IB, 0:SEQ], xTp[:, b % 2, IB, 0:SEQ], u.rearrange("p (i s) -> p i s", s=SEQ)
                        go(again, o[:, 0:SEQ])
                    go(dst, u).then_inc(S["x_turned"], 1)
                elif stage in ("x1_turn", "moe_turn", "rt_turn"):
                    g, be = {"x1": ("L0_attn_g1", "L0_attn_be1"), "moe": ("L1_ffn_ln1_g", "L1_ffn_ln1_b"),
                             "rt": ("L1_ffn_ln2_g", "L1_ffn_ln2_b")}[stage.split("_")[0]]
                    job = (stage, b, 0)
                    o = read(act, job)
                    dst, u = x_of(stage, b), o[:, 0:TB]
                    if stage == "moe_turn":
                        dst, u = xTp[:, b % 2, 0:IB, 0:SEQ], u.rearrange("p (i s) -> p i s", s=SEQ)
                        go(xTp[:, b % 2, IB, 0:SEQ], o[:, 0:SEQ], ACT.Identity, bias=col(be), scale=col(g))
                    go(dst, u, ACT.Identity, bias=col(be), scale=col(g)).then_inc(S["x_turned"], 1)
                elif stage == "rope_qk":
                    act.wait_ge(S["k_full"], b + 1)
                    for a in range(2):
                        go(kM[:, b % 2, 0, a, :], kT[:, b % 2, :], ACT.Identity, scale=const("parity")[:, a:a + 1]).then_inc(S["k_ready"], 1)
                elif stage in ("rope_v", "dif_v", "moe_v"):
                    if v_n == 0:
                        act.wait_ge(S["v_pads"], 1)
                    for half in range(2):
                        job = (stage, b, half)
                        o = read(act, job)
                        i0 = IB // 2 * half
                        for a in range(2):
                            r = slice(HALF * a, HALF * a + HALF)
                            v5 = vd[r, b % 2, :, :].rearrange("p i (q a d) -> p i q a d", q=QUADS, a=2)[:, :, :, a, :]
                            o5 = o[r, :].rearrange("p (i q a d) -> p i q a d", i=IB // 2, q=QUADS, a=2)[:, :, :, a, :]
                            n = IB // 2 - (1 if a and half else 0)
                            ins_ = go(v5[:, i0 + a:i0 + a + n], o5[:, 0:n])
                            if a and half:
                                ins_ = go(v5[:, 0], o5[:, n])
                            ins_.then_inc(S["v_ready"], 1)
                            v_n += 1
                elif stage in ("dif_qk", "moe_qk"):
                    for j in range(JOBS[stage]):
                        job = (stage, b, j)
                        o = read(act, job)
                        s = j // 2
                        if j % 2 == 0:
                            ins_ = go(qT[:, b % 2, s, :], o[:, 0:TB])
                            ins_.then_inc(S["q_ready"], 1)
                        else:
                            for a in range(2):
                                if stage == "dif_qk":
                                    ins_ = go(kM[:, b % 2, s, a, :], o[:, 0:TB], ACT.Identity, scale=const("parity")[:, a:a + 1],
                                              bias=masked_bias[:, s, a:a + 1])
                                else:
                                    ins_ = go(kM[:, b % 2, s, a, :], o[:, 0:TB], ACT.Identity, scale=const("parity")[:, a:a + 1])
                                ins_.then_inc(S["k_ready"], 1)
                elif stage in ("rope_scores", "dif_scores", "dif_scores2", "moe_scores"):
                    act.wait_ge(S["exp_in"], soft_n + 1)
                    v = ex[0:SROWS, soft_n % 2, :, :]
                    go(v, v, ACT.Exp, scale=HD ** -0.5).then_inc(S["exp_done"], 1)
                    soft_n += 1
                elif stage in ("rope_flip", "dif_flip", "moe_flip"):
                    for p in range(PAIRS):
                        job = (stage, b, p)
                        o = read(act, job)
                        both = bass.AP(o[:, :].tensor, o[:, :].offset, [list(o[:, :].ap[0]), [SROWS, QUADS], [HALF, 2], [1, SEQ]])
                        go(pT[:, flip_n % 2, :, p, :, :], both).then_inc(S["pT_ready"], 1)
                    flip_n += 1
                elif stage in ("rope_pv", "dif_pv", "moe_pv"):
                    o = read(act, (stage, b, 0))
                    go(ctxT[:, tok], o[:, 0:TB]).then_inc(S["ctx_ready"], 1)
                elif stage == "gn_center":
                    act.wait_ge(S["gn_centred"], b + 1)
                    go(gn_q[:, b % 2, :], ctxT[:, tok], ACT.Square).then_inc(S["square_ready"], 1)
                elif stage == "gn_apply":
                    act.wait_ge(S["gn_scaled"], b + 1)
                    go(ctxT[:, tok], ctxT[:, tok], ACT.Identity, bias=col("L1_attn_gn_b")).then_inc(S["square_ready"], 1)
                elif stage == "net_in":
                    for m in range(0, FC):
                        job = (stage, b, m)
                        o = read(act, job)
                        go(hid[:, m, b % 2, :], o[:, 0:TB], ACT.Relu, bias=net_bias[:, m:m + 1]).then_inc(S["hid_ready"], 1)
                elif stage == "mix_in":
                    job = (stage, b, 0)
                    o = read(act, job)
                    go(hid[:, 0, b % 2, :], o[:, 0:TB], ACT.Gelu, bias=col("L0_ffn_b1")).then_inc(S["hid_ready"], 1)
                elif stage == "rt_logits":
                    o = read(act, (stage, b, 0))
                    go(tiles(lg, b), o[0:TP, 0:TPB * E].rearrange("p (n e) -> p n e", e=E)).then_inc(S["logits_back"], 1)
                elif stage == "rt_gate":
                    act.wait_ge(S["logits_ready"], b + 1)
                    t = slice(TPB * b, TPB * b + TPB)
                    go(gate[:, t, 2], gate[:, t, 3], ACT.Exp).then_inc(S["gate_exp"], 1)

            for kind, i in moe_order:
                job = (kind, i, 0)
                if kind == "hidden":
                    if i >= 3:
                        act.wait_ge(S["yT_ready"], i - 2)
                    o = read(act, job)
                    for c in range(FC):
                        ins_ = go(hT[:, i % 3, c, 0:CAP], o[:, WIN * c:WIN * c + CAP], ACT.Gelu_apprx_tanh, bias=b1T[:, c, i:i + 1])
                    ins_.then_inc(S["h_full"], 1)
                elif kind == "give":
                    if i >= 4:
                        act.wait_ge(ys_gone[i % 4], 16 * (i // 4))
                    o = read(act, job)
                    go(ys[:, i % 4, :], o[:, 0:D], ACT.Identity, scale=smap[:, ST + i:ST + i + 1]).then_inc(S["ys_ready"], 1)

        @block.vector
        def _(dve):
            v = nc.vector
            st = Steps(dve, S["dve_step"])
            v.memset(scores[:, :, :], 0.0).then_inc(S["scores_zero"], 1)
            moments_n = 0

            def moments(b, source):
                nonlocal moments_n
                if moments_n >= 2:
                    dve.wait_ge(S["var"], moments_n - 1)
                u = moments_n % 2
                moments_n += 1
                for i in range(TPB):
                    st.step(v.bn_stats(stats[:, u, i, :], source(i)))
                st.settle()
                for i in range(TPB):
                    last = v.bn_aggr(mv[:, TPB * b + i, :], stats[:, u, i, :])
                return last

            def of(t, b):
                return lambda i: t[:, TPB * b + i, :]

            soft_n = 0
            sums_n = 0
            flip_of = list(range(NB)) + [NB + b for b in range(NB) for _ in range(2)] + list(range(2 * NB, 3 * NB))
            for stage, b in ORDER:
                tok = slice(TB * b, TB * b + TB)
                name = stage.split("_")[0]
                t = slice(TPB * b, TPB * b + TPB)
                im = slice(IB * b, IB * b + IB)
                if stage == "prepare":
                    dve.wait_ge(S["small_in"], SMALL)
                    st.link(v.tensor_tensor(lambdas[:, 0, :], lambdas[:, 0, :], lambdas[:, 1, :], ALU.mult))
                    v.tensor_tensor(lambdas[:, 1, :], lambdas[:, 2, :], lambdas[:, 3, :], ALU.mult).then_inc(S["lam_ready"], 1)
                elif stage == "patches":
                    if b == 0:
                        cut(dve, 0, v.tensor_copy, S["piece_even"])
                    for k in range(6):
                        if k % 2 == 0 and 6 * b + k + 2 < 12:
                            cut(dve, 6 * b + k + 2, v.tensor_copy, S["piece_even"])
                        job = (stage, b, 2 * k + 1)
                        o = read(dve, job)
                        dst = patchT[:, k, T // 2 * b:T // 2 * (b + 1)].rearrange("p (r w) -> p w r", w=GRID)[:, 3:6, :]
                        v.tensor_copy(dst, o[:, 0:3 * TP].rearrange("p (w r) -> p w r", w=3)).then_inc(S["patches_turned2"], 1)
                elif stage == "tok_shift":
                    job = (stage, b, 0)
                    dve.wait_ge(S["z_biased"], b + 1)
                    o = read(dve, job)
                    z, x = grid(o[:, 0:TB]), grid(tokT[:, tok])
                    n = GRID - 1
                    for q, (to, frm) in enumerate((((slice(0, GRID), slice(0, n)), (slice(0, GRID), slice(1, GRID))),
                                                   ((slice(0, GRID), slice(1, GRID)), (slice(0, GRID), slice(0, n))),
                                                   ((slice(0, n), slice(0, GRID)), (slice(1, GRID), slice(0, GRID))),
                                                   ((slice(1, GRID), slice(0, GRID)), (slice(0, n), slice(0, GRID))))):
                        p = slice(32 * q, 32 * q + 16)
                        last = v.tensor_tensor(x[p, :, to[0], to[1]], x[p, :, to[0], to[1]], z[p, :, frm[0], frm[1]], ALU.add)
                    last.then_inc(S["tok_added"], 1)
                elif stage == "tok_norm_a":
                    dve.wait_ge(S["tok_back"], b + 1)
                    moments(b, of(h, b)).then_inc(S["var"], 1)
                elif stage == "src_norm_a":
                    dve.wait_ge(S["h_norm"], b + 1)
                    moments(b, of(h, b)).then_inc(S["var"], 1)
                elif stage == "rope_qk":
                    if b >= 1:
                        dve.wait_ge(S["q_ready"], b)
                        dve.wait_ge(S["k_full"], b)
                    for n in range(2):
                        for dst, table, j in ((rot_a, "cos", 2 * n), (rot_b, "sin", 2 * n + 1)):
                            job = (stage, b, j)
                            o = read(dve, job)
                            v.tensor_tensor(dst[:, n, :].rearrange("p (i s) -> p i s", s=SEQ), o[:, 0:TB].rearrange("p (i s) -> p i s", s=SEQ),
                                            const(table).unsqueeze(1).broadcast_to([D, IB, SEQ]), ALU.mult).then_inc(S["rot_parts"], 1)
                elif stage in ("rope_scores", "dif_scores", "dif_scores2", "moe_scores"):
                    u = soft_n % 2
                    dve.wait_ge(S["s_full"], soft_n + 1)
                    sc = scores[0:SROWS, :, 0:SC].rearrange("p q (a k) -> p q a k", k=SEQ)
                    m3 = mx[:, u, :].rearrange("p (q a) -> p q a", q=QUADS)
                    st.link(v.tensor_reduce(m3, sc, AX_X, ALU.max))
                    if soft_n >= 2:
                        dve.wait_ge(S["probs_ready"], flip_of[soft_n - 2] + 1)
                    e4 = ex[0:SROWS, u, :, :].rearrange("p q (a k) -> p q a k", k=SEQ)
                    v.tensor_tensor(e4, sc, m3.unsqueeze(3).broadcast_to([SROWS, QUADS, 2 * PAIRS, SEQ]), ALU.subtract
                                    ).then_inc(S["exp_in"], 1)
                    soft_n += 1
                elif stage in ("rope_sums", "dif_sums", "dif_sums2", "moe_sums"):
                    u = sums_n % 2
                    dve.wait_ge(S["exp_done"], sums_n + 1)
                    e4 = ex[0:SROWS, u, :, :].rearrange("p q (a k) -> p q a k", k=SEQ)
                    s3 = sm[:, u, :].rearrange("p (q a) -> p q a", q=QUADS)
                    st.link(v.tensor_reduce(s3, e4, AX_X, ALU.add))
                    if stage == "dif_sums2":
                        st.link(v.reciprocal(s3, s3))
                        s4 = sm[:, u, :].rearrange("p (q i a) -> p q i a", q=QUADS, a=2)
                        l4 = lam[:, :].rearrange("p (q a) -> p q a", a=2).unsqueeze(2).broadcast_to([SROWS, QUADS, PAIRS, 2])
                        v.tensor_tensor(s4, s4, l4, ALU.mult).then_inc(S["sums_ready"], 1)
                    else:
                        v.reciprocal(s3, s3).then_inc(S["sums_ready"], 1)
                    sums_n += 1
                    if stage == "rope_sums" and b == 0:
                        dve.wait_ge(S["lam_ready"], 2)
                        st.link(v.tensor_tensor(lam[:, :], lambdas[:, 0, :], lambdas[:, 1, :], ALU.subtract))
                        st.link(v.tensor_scalar(lam[:, :], lam[:, :], 0.2, None, ALU.add))
                elif stage == "dif_mix":
                    f = NB + b
                    dve.wait_ge(S["map_scaled"], 2 * (b + 1))
                    dve.wait_ge(S["pT_ready"], PAIRS * (f - 1))
                    for q in range(QUADS):
                        last = v.tensor_tensor(probs[0:SROWS, f % 2, q, :, :, 0:SEQ].rearrange("p a b k -> p (a b) k"),
                                               ex[0:SROWS, 0, q, :].rearrange("p (a k) -> p a k", k=SEQ),
                                               ex[0:SROWS, 1, q, :].rearrange("p (a k) -> p a k", k=SEQ), ALU.subtract)
                    last.then_inc(S["probs_ready"], 1)
                elif stage in ("rope_out", "net_out", "mix_out", "dif_out", "moe_out"):
                    job = (stage, b, 0)
                    if stage == "net_out":
                        dve.wait_ge(S["affine_ready"], b + 1)
                    if name in ("mix", "dif"):
                        dve.wait_ge(S["base_ready"], base_count[name + "_norm_b", b])
                    o = read(dve, job)
                    base = {"rope": src, "net": mid, "mix": mid, "dif": mid, "moe": src}[name]
                    dst = {"rope": src, "net": src, "mix": h, "dif": h, "moe": src}[name]
                    last = v.tensor_tensor(dst[:, t, :], o[0:TP, 0:TPB * D].rearrange("p (n c) -> p n c", c=D), base[:, t, :], ALU.add)
                    last.then_inc(S["out_added"], 1)
                    dve.wait_ge(S["out_added"], out_count[stage, b])
                elif stage in ("x1_norm_a", "x2_norm_a", "rt_norm_a"):
                    moments(b, of(src, b)).then_inc(S["var"], 1)
                elif stage in ("mix_norm_a", "dif_norm_a", "moe_norm_a"):
                    moments(b, of(h, b)).then_inc(S["var"], 1)
                elif stage == "x2_norm_b":
                    dve.wait_ge(S["x2_ready"], b + 1)
                    st.link(v.tensor_tensor(h[:, t, :], h[:, t, :], norm[:, t, :], ALU.add))
                elif stage == "gn_sum":
                    dve.wait_ge(S["ctx_ready"], NB + b + 1)
                    v.tensor_reduce(gn_s[:, 0, im], ctxT[:, tok].rearrange("p (i s) -> p i s", s=SEQ), AX_X, ALU.add
                                    ).then_inc(S["gn_stat"], 1)
                elif stage == "gn_center":
                    c3 = ctxT[:, tok].rearrange("p (i s) -> p i s", s=SEQ)
                    o = read(dve, ("gn_sum", b, 0))
                    v.tensor_scalar(gn_s[:, 1, im], o[:, 0:IB], 1.0 / GSIZE, None, ALU.mult).then_inc(S["gn_mean_back"], 1)
                    dve.wait_ge(S["gn_mean_back"], b + 1)
                    v.tensor_tensor(c3, c3, gn_s[:, 1, im].unsqueeze(2).broadcast_to([D, IB, SEQ]), ALU.subtract
                                    ).then_inc(S["gn_centred"], 1)
                elif stage == "gn_var":
                    dve.wait_ge(S["square_ready"], square_n["gn_center", b])
                    v.tensor_reduce(gn_s[:, 2, im], gn_q[:, b % 2, :].rearrange("p (i s) -> p i s", s=SEQ), AX_X, ALU.add
                                    ).then_inc(S["gn_stat"], 1)
                elif stage == "gn_rstd":
                    o = read(dve, ("gn_var", b, 0))
                    v.tensor_scalar(gn_s[:, 3, im], o[:, 0:IB], 1.0 / GSIZE, None, ALU.mult).then_inc(S["gn_back"], 1)
                elif stage == "gn_apply":
                    dve.wait_ge(S["gn_ready"], b + 1)
                    c3 = ctxT[:, tok].rearrange("p (i s) -> p i s", s=SEQ)
                    v.tensor_tensor(c3, c3, gn_s[:, 3, im].unsqueeze(2).broadcast_to([D, IB, SEQ]), ALU.mult
                                    ).then_inc(S["gn_scaled"], 1)
                elif stage == "rt_logits":
                    dve.wait_ge(S["logits_back"], b + 1)
                    for g in range(TPB * b, TPB * b + TPB):
                        st.step(v.max(top[:, g, :], lg[:, g, :]))
                    st.settle()
                    v.tensor_tensor(gate[:, t, 3], top[:, t, 1], top[:, t, 0], ALU.subtract).then_inc(S["logits_ready"], 1)
                    for g in range(TPB * b, TPB * b + TPB):
                        st.step(v.max_index(top_i[:, g, :], top[:, g, :], lg[:, g, :]))
                    st.settle()
                    st.link(v.tensor_copy(top_f[:, t, :], top_i[:, t, 0:2]))
                    st.link(v.tensor_tensor(oh[:, t, :, :], const("iota_e", TP).unsqueeze(1).unsqueeze(1).broadcast_to([TP, TPB, 2, E]),
                                            top_f[:, t, :].unsqueeze(3).broadcast_to([TP, TPB, 2, E]), ALU.is_equal))
                    v.tensor_tensor(oh_both[:, t, :], oh[:, t, 0, :], oh[:, t, 1, :], ALU.add).then_inc(S["picked"], 1)
                elif stage == "rt_gate":
                    dve.wait_ge(S["gate_exp"], b + 1)
                    st.link(v.tensor_scalar(gate[:, t, 3], gate[:, t, 2], 1.0, None, ALU.add))
                    st.step(v.tensor_scalar(flat[:, t, :], top_f[:, t, :], float(CAP), None, ALU.mult))
                    st.link(v.reciprocal(gate[:, t, 0], gate[:, t, 3]))
                    st.link(v.tensor_tensor(gate[:, t, 1], gate[:, t, 2], gate[:, t, 0], ALU.mult))
                elif stage == "rt_count":
                    o = read(dve, (stage, b, 0))
                    cnt = o[0:TP, 0:TPB * E].rearrange("p (n e) -> p n e", e=E).unsqueeze(2).broadcast_to([TP, TPB, 2, E])
                    st.link(v.tensor_tensor(cum[:, :, :, :], cnt, oh[:, t, :, :], ALU.mult))
                    v.tensor_reduce(pos[:, t, :], cum[:, :, :, :], AX_X, ALU.add).then_inc(S["placed"], 1)
                    dve.wait_ge(S["placed"], b + 1)
                    st.step(v.tensor_scalar(far[:, t, :], pos[:, t, :], float(CAP), BEYOND, ALU.is_ge, ALU.mult))
                    st.step(v.tensor_scalar(kept[:, t, :], pos[:, t, :], float(CAP), None, ALU.is_lt))
                    st.link(v.tensor_tensor(flat[:, t, :], flat[:, t, :], pos[:, t, :], ALU.add))
                    st.link(v.tensor_tensor(flat_u[:, 0, t, :], flat[:, t, :], far[:, t, :], ALU.add))
                    st.step(v.tensor_scalar(flat_u[:, 1, t, :], flat_u[:, 0, t, :], 127, None, ALU.bitwise_and))
                    st.link(v.tensor_scalar(flat_u[:, 2, t, :], flat_u[:, 0, t, :], 7, None, ALU.logical_shift_right))
                    v.tensor_copy(flat_f[:, :, t, :], flat_u[:, 1:3, t, :]).then_inc(S["split"], 1)
                    dve.wait_ge(S["split"], b + 1)
                    if b >= 1:
                        dve.wait_ge(S["map_added"], b)
                    v.tensor_tensor(hi1[:, :, :, :], const("iota_hi", TP).unsqueeze(1).unsqueeze(1).broadcast_to([TP, TPB, 2, ST]),
                                    flat_f[:, 1, t, :].unsqueeze(3).broadcast_to([TP, TPB, 2, ST]), ALU.is_equal).then_inc(S["hi_ready"], 1)
                    v.tensor_tensor(lo1[:, :, :, :], const("iota_lo", TP).unsqueeze(1).unsqueeze(1).broadcast_to([TP, TPB, 2, D]),
                                    flat_f[:, 0, t, :].unsqueeze(3).broadcast_to([TP, TPB, 2, D]), ALU.is_equal).then_inc(S["mapped"], 1)
                elif stage == "rt_map":
                    o = read(dve, (stage, b, 0))
                    if b == 0:
                        last = v.tensor_copy(smap[:, :], o[:, 0:2 * ST])
                    else:
                        last = v.tensor_tensor(smap[:, :], smap[:, :], o[:, 0:2 * ST], ALU.add)
                    last.then_inc(S["map_added"], 1)

            dve.wait_ge(S["map_added"], NB)
            st.step(v.memset(xe[:, SLOTS:SLOTS + WIN], 0.0))
            st.step(v.memset(hT[:, :, :, CAP:WIN], 0.0))
            st.settle()
            st.step(v.tensor_scalar(smap2[:, 0, :], smap[:, 0:ST], 0.0, NOWHERE, ALU.is_equal, ALU.mult))
            st.step(v.tensor_scalar(get_u[:, 0, :], smap[:, 0:ST], 1.0, 1.0, ALU.max, ALU.subtract))
            st.settle()
            st.step(v.tensor_tensor(smap2[:, 1, :], smap2[:, 0, :], smap[:, 0:ST], ALU.add))
            st.step(v.tensor_scalar(get_u[:, 1, :], get_u[:, 0, :], 1, None, ALU.logical_shift_right))
            st.settle()
            v.tensor_scalar(put_u[:, :], smap2[:, 1, :], 1.0, None, ALU.subtract).then_inc(S["map_ready"], 1)
            for kind, i in moe_order:
                job = (kind, i, 0)
                if kind == "take":
                    o = read(dve, job)
                    v.tensor_copy(xe[:, D * i:D * i + D], o[:, 0:D]).then_inc(S["xe_ready"], 1)
                elif kind == "expert":
                    o = read(dve, job)
                    v.tensor_copy(yT[:, CAP * i:CAP * i + CAP], o[:, 0:CAP]).then_inc(S["yT_ready"], 1)
                elif kind == "bias_turn":
                    o = read(dve, job)
                    v.tensor_copy(gmT[:, i, :], o[0:E, 0:TB]).then_inc(S["gmT_ready"], 1)
                elif kind == "bias":
                    dve.wait_ge(S["h_summed"], NB)
                    o = read(dve, job)
                    t = slice(TPB * i, TPB * i + TPB)
                    v.tensor_tensor(h[:, t, :], o[0:TP, 0:TPB * D].rearrange("p (n c) -> p n c", c=D), h[:, t, :], ALU.add
                                    ).then_inc(S["bias_added"], 1)
            for b in range(NB):
                t = slice(TPB * b, TPB * b + TPB)
                dve.wait_ge(S["back_in"], 16 * NB)
                y = back_of(b)
                st.link(v.tensor_tensor(res[:, t, :], h[:, t, :], y[:, :, 0:D], ALU.add))
                v.tensor_tensor(res[:, t, :], res[:, t, :], y[:, :, D:2 * D], ALU.add).then_inc(S["final_ready"], 1)


def kernel(**inputs):
    import numpy as _np
    import concourse.bacc as _bacc
    from concourse import mybir as _mybir
    from concourse.bass_utils import run_bass_kernel_spmd as _run

    nc = _bacc.Bacc("TRN2", target_bir_lowering=False, num_devices=1)
    arrays, args = {}, {}
    for name, value in list(inputs.items()) + [("const", constants())]:
        a = _np.ascontiguousarray(value)
        arrays[f"in_{name}"] = a
        args[name] = nc.dram_tensor(f"in_{name}", a.shape, _mybir.dt.from_np(a.dtype), kind="ExternalInput").ap()
    out = nc.dram_tensor("out_0", (IMG, SEQ, D), F32, kind="ExternalOutput").ap()
    build(nc, args, out)
    r = _run(nc, [arrays], core_ids=[0])
    return r.results[0]["out_0"]
```

```python
from contextlib import ExitStack

import numpy as np

import concourse.bass as bass
from concourse import mybir

ALU = mybir.AluOpType
ACT = mybir.ActivationFunctionType
F32 = mybir.dt.float32
BF16 = mybir.dt.bfloat16
U32 = mybir.dt.uint32
AX_X = mybir.AxisListType.X

D = 128
H = 8
HD = D // H
QUADS = 4
IMG = 32
CH, PX, GRID = 3, 16, 6
SEQ = GRID * GRID
T = IMG * SEQ
NB = 4
IB = IMG // NB
TB = T // NB
TP = 96
TPB = TB // TP
NT = T // TP
PAIRS = IB // 2
HALF = 64
SROWS = HALF + SEQ
F0 = 512
FC = F0 // D
E, FF = 64, 512
CAP = 2 * (T * 2 // E)
SLOTS = E * CAP
ST = SLOTS // D
WIN = 96
RING = 11
NG = 6
WORK = 17088
EPS = 1e-5
BEYOND = 8192.0
NOWHERE = 1.0e6
GSIZE = D // 4 * SEQ

CONST = {}
_at = 0
for _name, _n in (("ident", D), ("swap", D), ("order", D), ("group", D), ("parity", 2), ("cos", SEQ), ("sin", SEQ),
                  ("iota_e", E), ("iota_lo", D), ("iota_hi", ST), ("before", TP), ("ids", 2 * NT)):
    CONST[_name] = (_at, _n)
    _at += _n
CONST_COLS = _at

BLOCKS = {}
_at = 0
for _name, _n in (("tok", 6), ("L0_attn_Wq", 1), ("L0_attn_Wq_rot", 1), ("L0_attn_Wk", 1), ("L0_attn_Wk_rot", 1),
                  ("L0_attn_Wv", 1), ("L0_attn_Wo", 1), ("L0_attn_W1", FC), ("L0_attn_W2", FC),
                  ("L0_ffn_W1", 1), ("L0_ffn_W2", 1), ("L1_attn_Q1_w", 1), ("L1_attn_K1_w", 1), ("L1_attn_Q2_w", 1),
                  ("L1_attn_K2_w", 1), ("L1_attn_V_w", 1), ("L1_attn_out_w", 1), ("L1_ffn_wq", 1), ("L1_ffn_wk", 1),
                  ("L1_ffn_wv", 1), ("L1_ffn_wo", 1)):
    BLOCKS[_name] = (_at, _n)
    _at += _n
NBLOCKS = _at
ROWS = ["L0_tok_ln_g", "L0_tok_ln_b", "L0_attn_g1", "L0_attn_be1", "L0_attn_b2", "L0_attn_g2", "L0_attn_be2",
        "L0_ffn_b2", "L1_attn_out_b", "L1_ffn_ln2_g", "L1_ffn_ln2_b"]
COLS = ["L0_attn_g1", "L0_attn_be1", "L0_ffn_b1", "L1_attn_K1_b", "L1_attn_K2_b", "L1_attn_gn_w", "L1_attn_gn_b",
        "L1_ffn_ln1_g", "L1_ffn_ln1_b", "L1_ffn_ln2_g", "L1_ffn_ln2_b"]
NCOLS = len(COLS) + FC + 1
LAMBDAS = ["L1_attn_lambda_q1", "L1_attn_lambda_k1", "L1_attn_lambda_q2", "L1_attn_lambda_k2"]


def constants():
    c = np.zeros((D, CONST_COLS), np.float32)

    def put(name, value):
        a, n = CONST[name]
        value = np.asarray(value, np.float32)
        c[:value.shape[0], a:a + n] = value

    put("ident", np.eye(D))
    f = np.arange(D)
    q, r = f // 32, f % 32
    partner = np.where(r < 16, f ^ 32, -1)
    swap = np.zeros((D, D))
    swap[partner[r < 16], f[r < 16]] = 1
    put("swap", swap)
    order = np.zeros((D, D))
    order[f, np.where(r < 16, 64 + 16 * q + r, 16 * q + r - 16)] = 1
    put("order", order)
    put("group", (f[:, None] // 32 == f[None, :] // 32))
    put("parity", np.stack([(f // HD) % 2 == 0, (f // HD) % 2 == 1], 1))
    half = HD // 2
    inv = (np.float32(1.0) / np.float32(10000.0) ** (np.arange(0, HD, 2, dtype=np.float32) / np.float32(HD)))
    angle = (np.arange(SEQ, dtype=np.float32)[:, None] * inv.astype(np.float32)[None, :]).astype(np.float32)
    d = f % HD
    put("cos", np.cos(angle)[:, d % half].T)
    put("sin", (np.sin(angle)[:, d % half] * np.where(d < half, -1.0, 1.0)).T)
    put("iota_e", np.tile(np.arange(E), (D, 1)))
    put("iota_lo", np.tile(np.arange(D), (D, 1)))
    put("iota_hi", np.tile(np.arange(ST), (D, 1)))
    t = np.arange(TP)
    put("before", t[:, None] < t[None, :])
    ids = np.zeros((TP, NT, 2))
    for k in range(2):
        ids[:, :, k] = 2 * (np.arange(NT)[None, :] * TP + t[:, None]) + k + 1
    put("ids", ids.reshape(TP, -1))
    return c


def packed(ins):
    put = {"const": constants()}
    x = ins["x"].reshape(NB, IB, CH, GRID, PX, GRID, PX).transpose(2, 4, 6, 0, 1, 3, 5)
    put["patches"] = x.reshape(6, D, NB, TB).transpose(1, 2, 0, 3)
    hp = PX // 2
    w = np.zeros((QUADS, 2, PX, CH, PX, PX), ins["x"].dtype)
    sx, sy = (ins[f"L0_tok_W_{n}"].reshape(PX, CH, PX, PX) for n in ("sx", "sy"))
    w[0, 0, :, :, :, hp:], w[1, 0, :, :, :, :hp] = sx[..., :hp], sx[..., hp:]
    w[2, 0, :, :, hp:, :], w[3, 0, :, :, :hp, :] = sy[:, :, :hp], sy[:, :, hp:]
    w[:, 1] = ins["L0_tok_W_main"].reshape(QUADS, PX, CH, PX, PX)
    blocks = {"tok": w.reshape(D, 6 * D).T.reshape(6, D, D)}
    for name in BLOCKS:
        if name in ("L0_attn_Wq_rot", "L0_attn_Wk_rot"):
            blocks[name] = ins[name[:-4]].reshape(H, 2, HD // 2, D)[:, ::-1].reshape(D, D).T
        elif name.startswith("L1_ffn_"):
            blocks[name] = ins[name]
        elif name == "L0_attn_W1":
            blocks[name] = ins[name].reshape(FC, D, D).transpose(0, 2, 1)
        elif name != "tok":
            blocks[name] = ins[name].T.reshape(BLOCKS[name][1], D, D)
    put["weights"] = np.concatenate([blocks[name].reshape(-1, D, D) for name in BLOCKS]).transpose(1, 0, 2)
    bias = np.stack([np.stack([ins["L0_tok_b_sx" if q < 2 else "L0_tok_b_sy"], ins["L0_tok_b_main"][PX * q:PX * q + PX]])
                     for q in range(QUADS)]).reshape(1, D)
    put["cols"] = np.concatenate([ins[name].reshape(1, D) for name in COLS] + [ins["L0_attn_b1"].reshape(FC, D), bias]).T
    put["rows"] = np.concatenate([ins[name].reshape(D) for name in ROWS])
    put["lambdas"] = np.concatenate([ins[name].reshape(H) for name in LAMBDAS])
    put["router"] = ins["L1_ffn_wr"]
    put["b1"] = ins["L1_ffn_b1"].reshape(E, FC, D).transpose(2, 1, 0)
    put["b2"] = ins["L1_ffn_b2"]
    w2 = ins["L1_ffn_w2"].reshape(E, FC, D, D).transpose(0, 2, 1, 3).reshape(E, D, FF)
    put["experts"] = np.concatenate([ins["L1_ffn_w1"], w2], 2)
    return put


ORDER_FOUND = """
    tok_z:0 tok_shift:0 tok_z:1 tok_turn:0 tok_norm_a:0 tok_norm_b:0 tok_shift:1 tok_z:2 tok_turn:1 tok_norm_a:1
    src_norm_a:0 tok_norm_b:1 src_norm_b:0 tok_shift:2 tok_z:3 src_norm_a:1 src_turn:0 tok_turn:2 src_norm_b:1
    tok_norm_a:2 rope_qk:0 tok_shift:3 tok_norm_b:2 src_norm_a:2 src_turn:1 tok_turn:3 rope_v:0 src_norm_b:2
    rope_qk:1 tok_norm_a:3 tok_norm_b:3 rope_scores:0 rope_sums:0 src_norm_a:3 src_turn:2 rope_v:1 src_norm_b:3
    rope_scores:1 rope_flip:0 src_turn:3 rope_qk:2 rope_sums:1 rope_pv:0 rope_qk:3 rope_out:0 x1_norm_a:0
    rope_flip:1 x1_norm_b:0 rope_v:2 rope_pv:1 x1_turn:0 rope_scores:2 rope_out:1 rope_sums:2 x1_norm_a:1 rope_v:3
    net_in:0 x1_affine:0 x1_norm_b:1 x1_affine:1 rope_scores:3 rope_sums:3 rope_flip:2 net_out:0 x2_norm_a:0
    rope_pv:2 rope_out:2 x1_turn:1 x1_norm_a:2 x2_norm_b:0 rope_flip:3 x1_norm_b:2 net_in:1 x1_affine:2 rope_pv:3
    rope_out:3 x1_turn:2 x1_norm_a:3 mix_norm_a:0 net_out:1 x1_norm_b:3 net_in:2 x1_turn:3 mix_norm_b:0 x1_affine:3
    mix_turn:0 mix_base:0 x2_norm_a:1 net_out:2 x2_norm_b:1 mix_norm_a:1 net_in:3 mix_in:0 mix_base:1 mix_out:0
    dif_norm_a:0 x2_norm_a:2 net_out:3 mix_norm_b:1 x2_norm_a:3 dif_norm_b:0 dif_turn:0 x2_norm_b:2 x2_norm_b:3
    mix_turn:1 mix_norm_a:2 mix_base:2 dif_qk:0 mix_in:1 dif_v:0 mix_out:1 dif_norm_a:1 mix_norm_b:2 dif_norm_b:1
    mix_norm_a:3 dif_scores:0 mix_base:3 mix_norm_b:3 mix_turn:2 dif_turn:1 dif_scores2:0 mix_in:2 dif_sums:0
    dif_base:0 mix_turn:3 dif_sums2:0 dif_qk:1 mix_out:2 dif_mix:0 dif_v:1 dif_norm_a:2 dif_norm_b:2 mix_in:3
    dif_scores:1 dif_base:1 mix_out:3 dif_turn:2 dif_norm_a:3 dif_flip:0 dif_scores2:1 dif_sums:1 dif_pv:0 dif_qk:2
    gn_sum:0 dif_sums2:1 gn_center:0 dif_v:2 dif_norm_b:3 gn_var:0 gn_rstd:0 dif_mix:1 gn_apply:0 dif_scores:2
    dif_out:0 dif_flip:1 dif_base:2 dif_turn:3 moe_norm_a:0 moe_norm_b:0 dif_scores2:2 dif_qk:3 dif_sums:2 dif_pv:1
    dif_sums2:2 gn_sum:1 moe_turn:0 dif_mix:2 gn_center:1 dif_v:3 gn_var:1 gn_rstd:1 gn_apply:1 dif_scores:3
    dif_out:1 moe_norm_a:1 dif_flip:2 moe_norm_b:1 dif_scores2:3 dif_pv:2 moe_qk:0 dif_sums:3 moe_turn:1 gn_sum:2
    dif_sums2:3 gn_center:2 moe_qk:1 dif_mix:3 moe_v:0 dif_flip:3 gn_var:2 gn_rstd:2 gn_apply:2 moe_scores:0
    dif_pv:3 dif_out:2 moe_v:1 gn_sum:3 moe_norm_a:2 moe_sums:0 gn_center:3 moe_norm_b:2 moe_scores:1 dif_base:3
    moe_flip:0 gn_var:3 gn_rstd:3 moe_sums:1 moe_pv:0 gn_apply:3 moe_out:0 moe_turn:2 rt_norm_a:0 rt_norm_b:0
    dif_out:3 moe_norm_a:3 moe_flip:1 moe_qk:2 rt_turn:0 moe_pv:1 rt_store:0 moe_norm_b:3 moe_v:2 moe_out:1
    moe_turn:3 rt_norm_a:1 rt_logits:0 rt_gate:0 moe_qk:3 rt_norm_b:1 rt_store:1 moe_scores:2 rt_count:0 rt_gm:0
    rt_turn:1 moe_v:3 moe_sums:2 moe_scores:3 rt_map:0 moe_flip:2 moe_sums:3 rt_logits:1 rt_gate:1 moe_pv:2
    moe_out:2 moe_flip:3 rt_norm_a:2 rt_count:1 rt_norm_b:2 moe_pv:3 moe_out:3 rt_gm:1 rt_norm_a:3 rt_turn:2
    rt_logits:2 rt_store:2 rt_map:1 rt_gate:2 rt_count:2 rt_norm_b:3 rt_turn:3 rt_gm:2 rt_logits:3 rt_gate:3
    rt_map:2 rt_count:3 rt_gm:3 rt_map:3 rt_store:3
"""


def plan():
    return [tuple((w.split(":")[0], int(w.split(":")[1]))) for w in ORDER_FOUND.split()]


JOBS = {"tok_z": 1, "tok_shift": 1, "tok_turn": 1,
        "src_turn": 1, "rope_qk": 4, "rope_v": 2, "rope_flip": PAIRS, "rope_pv": 1, "rope_out": 1,
        "x1_turn": 1, "net_in": FC, "net_out": 1, "mix_turn": 1, "mix_in": 1, "mix_out": 1,
        "dif_turn": 1, "dif_qk": 4, "dif_v": 2, "dif_flip": PAIRS, "dif_pv": 1, "gn_sum": 1, "gn_var": 1, "dif_out": 1,
        "moe_turn": 1, "moe_qk": 2, "moe_v": 2, "moe_flip": PAIRS, "moe_pv": 1, "moe_out": 1,
        "rt_turn": 1, "rt_logits": 1, "rt_count": 1, "rt_map": 1}


def build(nc, ins, out):
    ORDER = plan()
    job_number = {}
    for stage, b in ORDER:
        for i in range(JOBS.get(stage, 0)):
            job_number[stage, b, i] = len(job_number)
    moe_order = []
    turned = 0
    returned = 0
    for b in range(NB + 1):
        moe_order += [("bias_turn", b)] * (b < NB) + [("bias", b - 1)] * (b > 0)
    for e in range(E + 1):
        if e < E:
            need = min(ST, (min(e + 3, E - 1) * CAP + WIN - 1) // D + 1)
            while turned < need:
                moe_order.append(("take", turned))
                turned += 1
            moe_order.append(("hidden", e))
        if e >= 1:
            moe_order.append(("expert", e - 1))
            while (returned + 1) * D <= (e - 1) * CAP:
                moe_order.append(("give", returned))
                returned += 1
    while returned < ST:
        moe_order.append(("give", returned))
        returned += 1
    for kind, i in moe_order:
        job_number[kind, i, 0] = len(job_number)

    jobs = list(job_number)
    turned_parts = ("src", "x1", "mix", "dif", "moe", "rt")
    normed_parts = ("tok", "x2") + turned_parts
    out_count_stages = ("rope_out", "net_out", "mix_out", "dif_out", "moe_out")

    def counts(names):
        found = {}
        for stage, b in ORDER:
            if stage in names:
                found[stage, b] = len(found) + 1
        return found

    normed_count = {(s.split("_")[0], b): n for (s, b), n in counts([p + "_norm_b" for p in normed_parts]).items()}
    turned_count = {(s.split("_")[0], b): n for (s, b), n in counts([p + "_turn" for p in turned_parts]).items()}
    rstd_count = {(s.split("_")[0], b): n for (s, b), n in counts({s for s, _ in ORDER if s.endswith("norm_a")}).items()}
    out_count = counts(out_count_stages)
    base_count = counts(("mix_base", "dif_base"))
    var_of = counts({s for s, _ in ORDER if s.endswith("norm_a")})
    square_n = counts(("gn_center", "gn_apply"))
    gn_n = counts(("gn_sum", "gn_var"))

    ctx = ExitStack()
    with ctx:
        def sb(name, shape, dt=F32):
            return ctx.enter_context(nc.sbuf_tensor(name, shape, dt))

        def sem(name):
            return ctx.enter_context(nc.semaphore(name))

        SC = PAIRS * 2 * SEQ

        scores = ctx.enter_context(nc.psum_tensor("scores", [D, QUADS, 512], F32))
        banks = [ctx.enter_context(nc.psum_tensor(f"bank{i}", [D, 512], F32)) for i in range(4)]
        bank_full = [sem(f"bank{i}_full") for i in range(4)]

        ring = sb("ring", [D, RING, 1024])
        cst = sb("cst", [D, CONST_COLS])

        def const(name, rows=D):
            a, n = CONST[name]
            return cst[0:rows, a:a + n]

        work = sb("work", [D, WORK])

        class Share:
            def __init__(self):
                self.at = 0

            def take(self, shape, dt=F32):
                n = int(np.prod(shape))
                a = work[:, self.at:self.at + n]
                self.at += n
                assert self.at <= WORK, self.at
                names = "abcdef"[:len(shape)]
                return a.rearrange(f"p ({' '.join(names)}) -> p {' '.join(names)}", **dict(zip(names, shape)))

        first = Share()
        patchT = first.take([NB, 6, TB])
        zraw = first.take([T])
        tokT = first.take([T])
        second = Share()
        ex = second.take([2, QUADS, SC])
        probs = second.take([2, QUADS, PAIRS, 2, HALF])
        pT = second.take([2, QUADS, PAIRS, 2, SEQ])
        ctxT = second.take([T])
        second.at = max(second.at, first.at)
        qT = second.take([2, 2, TB])
        kT = second.take([2, TB])
        rot_a = second.take([2, TB])
        rot_b = second.take([2, TB])
        kM = second.take([2, 2, 2, TB])
        vd = second.take([2, IB, D])
        third = Share()
        xe = third.take([SLOTS + WIN])
        yT = third.take([SLOTS])
        hT = third.take([3, FC, WIN])
        got = third.take([NG, D])
        ys = third.take([4, D])
        gmT = third.take([NB, TB])[0:E]

        wT = sb("wT", [D, NBLOCKS, D])
        wr = sb("wr", [D, E])
        rows = sb("rows", [TP, len(ROWS), D])
        cols = sb("cols", [D, NCOLS])
        tok_bias = cols[:, NCOLS - 1:NCOLS]
        net_bias = cols[:, len(COLS):len(COLS) + FC]
        masked_bias = sb("masked_bias", [D, 2, 2])
        lambdas = sb("lambdas", [SROWS, 4, H])
        lam = sb("lam", [SROWS, H])
        minus_half = sb("minus_half", [D, TPB])
        b1T = sb("b1T", [D, FC, E])
        b2nat = sb("b2nat", [E, D])

        h = sb("h", [TP, NT, D])
        src = sb("src", [TP, NT, D])
        mid = sb("mid", [TP, NT, D])
        norm = sb("norm", [TP, NT, D])
        xT = sb("xT", [D, 2, 2, TB])
        hid = sb("hid", [D, FC, 2, TB])
        xTp = sb("xTp", [D, 2, IB + 1, HALF])
        res = norm
        stats = sb("stats", [TP, 2, TPB, 6])
        mv = sb("mv", [TP, NT, 2])
        rstd = sb("rstd", [TP, NT, 3])
        mx = sb("mx", [SROWS, 2, QUADS * PAIRS * 2])
        sm = sb("sm", [SROWS, 2, QUADS * PAIRS * 2])
        gn_s = sb("gn_s", [D, 4, IMG])
        gn_q = rot_a
        lg = sb("lg", [TP, NT, E])
        top = sb("top", [TP, NT, 8])
        top_i = sb("top_i", [TP, NT, 8], U32)
        top_f = sb("top_f", [TP, NT, 2])
        gate = sb("gate", [TP, NT, 4])
        oh = sb("oh", [TP, NT, 2, E])
        oh_both = sb("oh_both", [TP, NT, E], BF16)
        run = sb("run", [TP, NB + 1, E], BF16)
        before16 = sb("before16", [TP, TP], BF16)
        ones16 = sb("ones16", [TP, TP], BF16)
        cum = sb("cum", [TP, TPB, 2, E])
        pos = sb("pos", [TP, NT, 2])
        flat = sb("flat", [TP, NT, 2])
        far = sb("far", [TP, NT, 2])
        flat_u = sb("flat_u", [TP, 3, NT, 2], U32)
        flat_f = sb("flat_f", [TP, 2, NT, 2])
        kept = sb("kept", [TP, NT, 2])
        kept_gate = sb("kept_gate", [TP, NT, 2])
        lo1 = sb("lo1", [TP, TPB, 2, D])
        hi1 = sb("hi1", [TP, TPB, 2, ST])
        pay = sb("pay", [TP, TPB, 2, 2 * ST])
        gm = sb("gm", [TP, NT, E])
        smap = sb("smap", [D, 2 * ST])
        smap2 = sb("smap2", [D, 2, ST])
        put_u = sb("put_u", [D, ST], U32)
        get_u = sb("get_u", [D, 2, ST], U32)

        x2d = nc.dram_tensor("x2_rows", [T, D], F32, kind="Internal").ap()
        ytok = nc.dram_tensor("expert_rows", [2 * T, D], F32, kind="Internal").ap()

        names = """const_in patch_weights_in rows_in weights_in lambdas_in late_in zero_in tok_back v_pads probs_pads scores_zero 
            tri_made before_made z_raw z_biased tok_added h_norm var rstd_ready
            normed x_turned rot_parts q_ready k_full k_ready v_ready s_full exp_in exp_done sums_ready
            probs_ready map_scaled ctx_ready gn_stat gn_back gn_ready out_added affine_ready hid_ready
            mask_ready x2_stored logits_ready picked mapped map_added run_ready hi_ready paid split map_ready xe_ready h_full yT_ready ys_ready
            x2_ready base_ready h_summed src_ready stored gm_ready gmT_ready bias_added lam_ready square_ready pT_ready gn_mean_back gn_centred
            gn_scaled half_scaled logits_back placed gate_exp dve_step pool_step final_ready
           """.split()
        S = {n: sem(n) for n in names}
        back_in = [sem(f"back_in{b}") for b in range(NB)]
        x_in = [sem(f"x_in{b}") for b in range(NB)]
        w_here = [sem(f"expert_here{i}") for i in range(RING)]
        got_here = [sem(f"got{i}") for i in range(NG)]
        ys_gone = [sem(f"ys_gone{i}") for i in range(4)]

        def bank(job):
            n = job_number[job]
            return banks[n % 4]

        def fill(pe, job):
            n = job_number[job]
            if n >= 4:
                name, count = taken(jobs[n - 4])
                pe.wait_ge(S[name], count)
            return banks[n % 4]

        def filled(job):
            return bank_full[job_number[job] % 4]

        def read(eng, job):
            n = job_number[job]
            eng.wait_ge(bank_full[n % 4], n // 4 + 1)
            return banks[n % 4]

        def taken(job):
            stage, b, i = job
            part = stage.split("_")[0]
            at = {"rope": 0, "dif": 1, "moe": 2}.get(part, 0) * NB + b
            if stage.endswith("_turn") and part in turned_parts:
                return "x_turned", turned_count[part, b]
            if stage in ("rope_v", "dif_v", "moe_v"):
                return "v_ready", 4 * at + 2 * i + 2
            if stage in ("rope_flip", "dif_flip", "moe_flip"):
                return "pT_ready", PAIRS * at + i + 1
            if stage in ("rope_pv", "dif_pv", "moe_pv"):
                return "ctx_ready", at + 1
            if stage in out_count_stages:
                return "out_added", out_count[stage, b]
            return {
                "tok_z": ("z_biased", b + 1), "tok_shift": ("tok_added", b + 1), "tok_turn": ("tok_back", b + 1),
                "rope_qk": ("rot_parts", 4 * b + i + 1),
                "net_in": ("hid_ready", FC * b + i + 1), "mix_in": ("hid_ready", FC * NB + b + 1),
                "dif_qk": ("k_ready", 2 * NB + 4 * b + i + 1) if i % 2 else ("q_ready", NB + 2 * b + i // 2 + 1),
                "moe_qk": ("k_ready", 6 * NB + 2 * b + 2) if i % 2 else ("q_ready", 3 * NB + b + 1),
                "gn_sum": ("gn_mean_back", b + 1), "gn_var": ("gn_back", b + 1),
                "rt_logits": ("logits_back", b + 1), "rt_count": ("placed", b + 1),
                "rt_map": ("map_added", b + 1),
                "take": ("xe_ready", b + 1), "hidden": ("h_full", b + 1), "expert": ("yT_ready", b + 1),
                "give": ("ys_ready", b + 1), "bias_turn": ("gmT_ready", b + 1), "bias": ("bias_added", b + 1),
            }[stage]

        class Steps:

            def __init__(self, eng, s):
                self.eng, self.s, self.n = eng, s, 0

            def step(self, ins):
                ins.then_inc(self.s, 1)
                self.n += 1

            def link(self, ins):
                self.step(ins)
                self.eng.wait_ge(self.s, self.n)

            def settle(self):
                self.eng.wait_ge(self.s, self.n)

        def block_of(name, i=0):
            return wT[:, BLOCKS[name][0] + i, :]

        def row(name):
            return rows[:, ROWS.index(name), :].unsqueeze(1).broadcast_to([TP, TPB, D])

        def col(name):
            i = COLS.index(name)
            return cols[:, i:i + 1]

        def tiles(t, b):
            return t[:, TPB * b:TPB * b + TPB, :]

        def x_of(stage, b):
            return xT[:, 1 if stage.startswith("mix") else 0, b % 2, :]

        def grid(ap):
            return ap.rearrange("p (i r c) -> p i r c", r=GRID, c=GRID)

        def back_of(b):
            return ring[0:TP, b, 0:TPB * 2 * D].rearrange("p (n c) -> p n c", n=TPB)

        block = ctx.enter_context(nc.Block())

        @block.sync
        def _(sp):
            sp.dma_start(cst[:, :], ins["const"]).then_inc(S["const_in"], 16)
            sp.dma_start(wT[:, 0:6, :], ins["weights"][:, 0:6, :]).then_inc(S["patch_weights_in"], 16)
            sp.dma_start(cols[:, :], ins["cols"]).then_inc(S["patch_weights_in"], 16)
            for b in range(NB):
                sp.dma_start(patchT[:, b, :, :], ins["patches"][:, b, :, :]).then_inc(x_in[b], 16)
                if b == 1:
                    sp.dma_start(rows[:, :, :], ins["rows"].partition_broadcast(TP).rearrange("p (n c) -> p n c", c=D)).then_inc(S["rows_in"], 16)
                if b == 2:
                    sp.dma_start(wT[:, 6:NBLOCKS, :], ins["weights"][:, 6:NBLOCKS, :]).then_inc(S["weights_in"], 16)
            sp.dma_start(lambdas[:, :, :], ins["lambdas"].partition_broadcast(SROWS).rearrange("p (n h) -> p n h", h=H)
                         ).then_inc(S["lambdas_in"], 16)
            sp.dma_start(wr[:, :], ins["router"]).then_inc(S["late_in"], 16)
            sp.dma_start(b1T[:, :, :], ins["b1"]).then_inc(S["late_in"], 16)
            sp.dma_start(b2nat[:, :], ins["b2"]).then_inc(S["late_in"], 16)
            for e in range(E):
                s = e % RING
                if e >= RING:
                    sp.wait_ge(S["yT_ready"], e - RING + 1)
                sp.dma_start(ring[:, s, :], ins["experts"][e]).then_inc(w_here[s], 16)
            sp.wait_ge(S["yT_ready"], E)
            for i in range(4):
                sp.wait_ge(ys_gone[i], 16 * (ST // 4))
            for b in range(NB):
                sp.dma_start(back_of(b), ytok.rearrange("(n p k) c -> p n (k c)", p=TP, k=2)[:, TPB * b:TPB * b + TPB, :]
                             ).then_inc(back_in[b], 16)
            for b in range(NB):
                sp.wait_ge(S["final_ready"], b + 1)
                sp.dma_start(out.rearrange("i s c -> (i s) c").rearrange("(n p) c -> p n c", p=TP)[:, TPB * b:TPB * b + TPB, :],
                             tiles(res, b)).then_inc(S["stored"], 16)
            sp.wait_ge(S["stored"], 16 * NB)

        @block.gpsimd
        def _(pool):
            st = Steps(pool, S["pool_step"])
            st.step(pool.memset(minus_half[:, :], -0.5))
            st.step(pool.memset(xTp[:, :, :, :], 0.0))
            pool.memset(run[:, 0, :], 0.0).then_inc(S["run_ready"], 1)
            st.step(pool.memset(ones16[:, :], 1.0))
            pool.memset(vd[:, :, :, :], 0.0).then_inc(S["v_pads"], 1)
            pool.wait_ge(S["const_in"], 16)
            pool.tensor_copy(before16[:, :], const("before", TP)).then_inc(S["before_made"], 1)
            pool.wait_ge(S["before_made"], 1)
            st.link(pool.memset(mid[:, :, :], 0.0))
            for k in range(2):
                pool.dma_start(ytok.rearrange("(k p n) c -> k p (n c)", k=2, p=TP)[k], mid[:, :, :].rearrange("p n c -> p (n c)")
                               ).then_inc(S["zero_in"], 16)
            var_n = 0

            def rsqrt(b, twice=False):
                nonlocal var_n
                var_n += 1
                pool.wait_ge(S["var"], var_n)
                v = mv[:, TPB * b:TPB * b + TPB, 1]
                r = rstd[:, TPB * b:TPB * b + TPB, 0]
                r2 = rstd[:, TPB * b:TPB * b + TPB, 1]
                m = mv[:, TPB * b:TPB * b + TPB, 0]
                n = rstd[:, TPB * b:TPB * b + TPB, 2]
                st.step(pool.tensor_scalar(n, m, -1.0, None, ALU.mult))
                st.link(pool.tensor_scalar(r, v, EPS, None, ALU.add))
                st.link(pool.tensor_tensor(r, r, minus_half[0:TP, 0:TPB], ALU.pow))
                if not twice:
                    pool.tensor_tensor(n, n, r, ALU.mult).then_inc(S["rstd_ready"], 1)
                    return
                st.step(pool.tensor_tensor(n, n, r, ALU.mult))
                st.link(pool.tensor_tensor(r2, r, r, ALU.mult))
                st.link(pool.tensor_tensor(r2, r2, v, ALU.mult))
                st.link(pool.tensor_scalar(r2, r2, EPS, None, ALU.add))
                pool.tensor_tensor(r2, r2, minus_half[0:TP, 0:TPB], ALU.pow).then_inc(S["rstd_ready"], 1)

            sums_n = flips = 0
            for stage, b in ORDER:
                name = stage.split("_")[0]
                tok = slice(TB * b, TB * b + TB)
                if stage == "rope_v" and b == 0:
                    pool.wait_ge(S["patch_weights_in"], 32)
                    for n, name in enumerate(("L1_attn_K1_b", "L1_attn_K2_b")):
                        for a in range(2):
                            pool.tensor_tensor(masked_bias[:, n, a:a + 1], col(name), const("parity")[:, a:a + 1], ALU.mult
                                               ).then_inc(S["mask_ready"], 1)
                    pool.wait_ge(S["mask_ready"], 4)
                    pool.wait_ge(S["weights_in"], 16)
                    for name in ("L0_ffn_W1", "L0_ffn_W2"):
                        w = block_of(name)
                        pool.affine_select(out=w, in_=w, compare_op=ALU.is_ge, fill=0.0, base=0, pattern=[[1, D]],
                                           channel_multiplier=-1).then_inc(S["tri_made"], 1)
                if stage.endswith("norm_a"):
                    rsqrt(b, twice=stage.startswith("moe"))
                if stage == "tok_norm_a" and b == NB - 1:
                    pool.wait_ge(S["z_biased"], NB)
                    pool.memset(probs[:, :, :, :, :, SEQ:HALF], 0.0).then_inc(S["probs_pads"], 1)
                if stage == "tok_norm_b":
                    pool.wait_ge(S["normed"], normed_count["tok", b])
                    if b == 0:
                        pool.wait_ge(S["rows_in"], 16)
                    st.link(pool.tensor_tensor(tiles(h, b), tiles(h, b), row("L0_tok_ln_g"), ALU.mult))
                    pool.tensor_tensor(tiles(h, b), tiles(h, b), row("L0_tok_ln_b"), ALU.add).then_inc(S["h_norm"], 1)
                if stage == "x2_norm_b":
                    pool.wait_ge(S["normed"], normed_count["x2", b])
                    st.link(pool.tensor_tensor(tiles(norm, b), tiles(norm, b), row("L0_attn_g2"), ALU.mult))
                    pool.tensor_tensor(tiles(norm, b), tiles(norm, b), row("L0_attn_be2"), ALU.add).then_inc(S["x2_ready"], 1)
                if stage in ("mix_base", "dif_base"):
                    pool.wait_ge(S["var"], var_of[name + "_norm_a", b])
                    pool.tensor_tensor(tiles(mid, b), tiles(h, b), row("L0_ffn_b2" if stage[0] == "m" else "L1_attn_out_b"), ALU.add
                                       ).then_inc(S["base_ready"], 1)
                if stage == "rt_gate":
                    pool.wait_ge(S["picked"], b + 1)
                    pool.wait_ge(S["run_ready"], b + 1)
                    g = TPB * b
                    st.link(pool.tensor_tensor(run[:, b + 1, :], run[:, b, :], oh_both[:, g, :], ALU.add))
                    for i in range(1, TPB):
                        last = pool.tensor_tensor(run[:, b + 1, :], run[:, b + 1, :], oh_both[:, g + i, :], ALU.add)
                        if i < TPB - 1:
                            st.link(last)
                    last.then_inc(S["run_ready"], 1)
                if stage == "rt_count":
                    t = slice(TPB * b, TPB * b + TPB)
                    pool.wait_ge(S["hi_ready"], b + 1)
                    ids = const("ids", TP).rearrange("p (n k) -> p n k", k=2)[:, t, :].unsqueeze(3).broadcast_to([TP, TPB, 2, ST])
                    st.step(pool.tensor_tensor(pay[:, :, :, 0:ST], hi1[:, :, :, :], ids, ALU.mult))
                    pool.tensor_tensor(pay[:, :, :, ST:2 * ST], hi1[:, :, :, :], gate[:, t, 0:2].unsqueeze(3).broadcast_to([TP, TPB, 2, ST]),
                                       ALU.mult).then_inc(S["paid"], 1)
                if stage == "rt_gm":
                    t = slice(TPB * b, TPB * b + TPB)
                    pool.wait_ge(S["hi_ready"], b + 1)
                    st.link(pool.tensor_tensor(kept_gate[:, t, :], gate[:, t, 0:2], kept[:, t, :], ALU.mult))
                    st.link(pool.tensor_tensor(oh[:, t, :, :], oh[:, t, :, :], kept_gate[:, t, :].unsqueeze(3).broadcast_to([TP, TPB, 2, E]), ALU.mult))
                    pool.tensor_tensor(gm[:, t, :], oh[:, t, 0, :], oh[:, t, 1, :], ALU.add).then_inc(S["gm_ready"], 1)
                if stage == "rt_store":
                    pool.wait_ge(S["out_added"], out_count["moe_out", b])
                    pool.tensor_tensor(tiles(h, b), tiles(h, b), tiles(src, b), ALU.add).then_inc(S["h_summed"], 1)
                if stage == "rope_qk":
                    pool.wait_ge(S["rot_parts"], 4 * b + 2)
                    pool.tensor_tensor(qT[:, b % 2, 0, :], rot_a[:, 0, :], rot_b[:, 0, :], ALU.add).then_inc(S["q_ready"], 1)
                    pool.wait_ge(S["rot_parts"], 4 * b + 4)
                    pool.tensor_tensor(kT[:, b % 2, :], rot_a[:, 1, :], rot_b[:, 1, :], ALU.add).then_inc(S["k_full"], 1)
                if stage in ("rope_sums", "moe_sums", "dif_sums", "dif_sums2"):
                    if sums_n == 0:
                        pool.wait_ge(S["probs_pads"], 1)
                    pool.wait_ge(S["sums_ready"], sums_n + 1)
                    if stage[:3] != "dif" and flips >= 2:
                        pool.wait_ge(S["pT_ready"], PAIRS * (flips - 1))
                    s = sums_n % 2
                    for q in range(QUADS // 2):
                        e3 = ex[0:SROWS, s, q, :].rearrange("p (a k) -> p a k", k=SEQ)
                        to = e3 if stage[:3] == "dif" else probs[0:SROWS, flips % 2, q, :, :, 0:SEQ].rearrange("p a b k -> p (a b) k")
                        last = pool.tensor_tensor(
                            to, e3, sm[:, s, 2 * PAIRS * q:2 * PAIRS * (q + 1)].unsqueeze(2).broadcast_to([SROWS, 2 * PAIRS, SEQ]), ALU.mult)
                    last.then_inc(S["map_scaled" if stage[:3] == "dif" else "probs_ready"], 1)
                    sums_n += 1
                    flips += stage != "dif_sums"
                if stage == "gn_rstd":
                    pool.wait_ge(S["gn_back"], b + 1)
                    im = slice(IB * b, IB * b + IB)
                    st.link(pool.tensor_scalar(gn_s[:, 3, im], gn_s[:, 3, im], EPS, None, ALU.add))
                    st.link(pool.tensor_tensor(gn_s[:, 3, im], gn_s[:, 3, im], minus_half[:, 0:1].broadcast_to([D, IB]), ALU.pow))
                    pool.tensor_scalar(gn_s[:, 3, im], gn_s[:, 3, im], col("L1_attn_gn_w"), 0.0, ALU.mult, ALU.add
                                       ).then_inc(S["gn_ready"], 1)
                if stage == "x1_affine":
                    if b == 0:
                        pool.wait_ge(S["zero_in"], 32)
                    pool.wait_ge(S["normed"], normed_count["x1", b])
                    st.link(pool.tensor_tensor(tiles(mid, b), tiles(norm, b), row("L0_attn_g1"), ALU.mult))
                    st.link(pool.tensor_tensor(tiles(mid, b), tiles(mid, b), row("L0_attn_be1"), ALU.add))
                    pool.tensor_tensor(tiles(mid, b), tiles(mid, b), row("L0_attn_b2"), ALU.add).then_inc(S["affine_ready"], 1)
                if stage == "rt_store":
                    pool.wait_ge(S["normed"], normed_count["rt", b])
                    st.link(pool.tensor_tensor(tiles(mid, b), tiles(norm, b), row("L1_ffn_ln2_g"), ALU.mult))
                    st.link(pool.tensor_tensor(tiles(mid, b), tiles(mid, b), row("L1_ffn_ln2_b"), ALU.add))
                    pool.dma_start(x2d.rearrange("(n p) c -> p n c", p=TP)[:, TPB * b:TPB * b + TPB, :], tiles(mid, b)
                                   ).then_inc(S["x2_stored"], 16)

            pool.wait_ge(S["map_ready"], 1)
            pool.wait_ge(S["x2_stored"], 16 * NB)
            gathered = 0

            def gather(i):
                if i >= NG:
                    pool.wait_ge(S["xe_ready"], i - NG + 1)
                pool.indirect_dma_start(out=got[:, i % NG, :], out_offset=None, in_=x2d[:, :],
                                        in_offset=bass.IndirectOffsetOnAxis(ap=get_u[:, 1, i:i + 1], axis=0)
                                        ).then_inc(got_here[i % NG], 16)

            for kind, i in moe_order:
                if kind == "take":
                    while gathered < min(ST, i + 3):
                        gather(gathered)
                        gathered += 1
                if kind == "give":
                    pool.wait_ge(S["ys_ready"], i + 1)
                    pool.indirect_dma_start(out=ytok[:, :], out_offset=bass.IndirectOffsetOnAxis(ap=put_u[:, i:i + 1], axis=0),
                                            in_=ys[:, i % 4, :], in_offset=None, bounds_check=2 * T - 1, oob_is_err=False
                                            ).then_inc(ys_gone[i % 4], 16)

        @block.tensor
        def _(pe):
            def mm(o, a, b, start=True, stop=True):
                return nc.tensor.matmul(o, a, b, start=start, stop=stop)

            def turn(stage, b):
                job = (stage, b, 0)
                o = fill(pe, job)
                source = src if stage == "src_turn" else norm
                pe.wait_ge(S["normed"], normed_count[stage.split("_")[0], b])
                for i in range(TPB):
                    last = nc.tensor.transpose(o[:, TP * i:TP * i + TP], source[:, TPB * b + i, :], const("ident")[0:TP, 0:TP])
                last.then_inc(filled(job), 1)

            def features(job, w, b, n=None):
                o = fill(pe, job)
                x = x_of(job[0], b) if job[0] in ("net_in", "mix_in") else xTp[:, b % 2, 0:IB, 0:SEQ]
                mm(o[:, 0:TB], w, x).then_inc(filled(job), 1)

            def tokens(job, lhs, rhs_list, width=D):
                o = fill(pe, job)
                for i in range(TPB):
                    for k, rhs in enumerate(rhs_list):
                        last = mm(o[0:TP, width * i:width * i + width], lhs(k, i), rhs, start=(k == 0), stop=(k == len(rhs_list) - 1))
                last.then_inc(filled(job), 1)

            def values(stage, b, w):
                for half in range(2):
                    job = (stage, b, half)
                    o = fill(pe, job)
                    for i in range(IB // 2):
                        at = IB // 2 * half + i
                        last = mm(o[:, D * i:D * i + D], xTp[:, b % 2, at:at + 2, :].rearrange("p i s -> p (i s)"), w)
                    last.then_inc(filled(job), 1)

            def score(n, b, s):
                if n >= 1:
                    pe.wait_ge(S["exp_in"], n)
                else:
                    pe.wait_ge(S["scores_zero"], 1)
                for p in range(PAIRS):
                    for a in range(2):
                        t = SEQ * (2 * p + a)
                        for q in range(QUADS):
                            last = mm(scores[HALF * a:HALF * a + SEQ, q, 2 * SEQ * p:2 * SEQ * (p + 1)],
                                      qT[32 * q:32 * q + 32, b % 2, s, t:t + SEQ], kM[32 * q:32 * q + 32, b % 2, s, :, t:t + SEQ])
                last.then_inc(S["s_full"], 1)

            def flip(stage, b, n):
                pe.wait_ge(S["probs_ready"], n + 1)
                if not stage.startswith("dif"):
                    pe.wait_ge(S["half_scaled"], n + 1 if n < NB else n + NB + 1)
                for p in range(PAIRS):
                    job = (stage, b, p)
                    o = fill(pe, job)
                    for q in range(QUADS):
                        last = nc.tensor.transpose(o[:, SROWS * q:SROWS * (q + 1)],
                                                   probs[0:SROWS, n % 2, q, p, :, :].rearrange("p a k -> p (a k)"),
                                                   const("ident")[0:SROWS, 0:SROWS])
                    last.then_inc(filled(job), 1)

            def weigh(stage, b, n):
                job = (stage, b, 0)
                o = fill(pe, job)
                pe.wait_ge(S["v_ready"], 4 * (n + 1))
                pe.wait_ge(S["pT_ready"], PAIRS * (n + 1))
                for p in range(PAIRS):
                    for a in range(2):
                        i = 2 * p + a
                        for q in range(QUADS):
                            last = mm(o[32 * q:32 * q + 32, SEQ * i:SEQ * i + SEQ], vd[:, b % 2, i, 32 * q:32 * q + 32],
                                      pT[:, n % 2, q, p, a, :])
                last.then_inc(filled(job), 1)

            score_n = 0
            flip_n = 0
            pv_n = 0
            pe.wait_ge(S["const_in"], 16)
            for stage, b in ORDER:
                def ctx_tile(k, i):
                    return ctxT[:, TB * b + TP * i:TB * b + TP * i + TP]

                if stage == "tok_z":
                    if b == 0:
                        pe.wait_ge(S["patch_weights_in"], 32)
                    pe.wait_ge(x_in[b], 16)
                    job = (stage, b, 0)
                    o = fill(pe, job)
                    for k in range(6):
                        last = mm(o[:, 0:TB], wT[:, k, :], patchT[:, b, k, :], start=(k == 0), stop=(k == 5))
                    last.then_inc(filled(job), 1)
                elif stage == "tok_shift":
                    pe.wait_ge(S["z_raw"], b + 1)
                    job = (stage, b, 0)
                    o = fill(pe, job)
                    mm(o[:, 0:TB], const("swap"), zraw[:, TB * b:TB * b + TB]).then_inc(filled(job), 1)
                elif stage == "tok_turn":
                    pe.wait_ge(S["tok_added"], b + 1)
                    tokens((stage, b, 0), lambda k, i: tokT[:, TB * b + TP * i:TB * b + TP * i + TP], [const("order")])
                elif stage in ("src_turn", "x1_turn", "mix_turn", "dif_turn", "moe_turn", "rt_turn"):
                    turn(stage, b)
                elif stage == "rope_qk":
                    pe.wait_ge(S["x_turned"], turned_count["src", b])
                    if b == 0:
                        pe.wait_ge(S["weights_in"], 16)
                    for j, w in enumerate(("L0_attn_Wq", "L0_attn_Wq_rot", "L0_attn_Wk", "L0_attn_Wk_rot")):
                        features((stage, b, j), block_of(w), b)
                elif stage == "rope_v":
                    if b == 0:
                        pe.wait_ge(S["v_pads"], 1)
                    values(stage, b, block_of("L0_attn_Wv"))
                elif stage == "rope_scores":
                    pe.wait_ge(S["q_ready"], b + 1)
                    pe.wait_ge(S["k_ready"], 2 * (b + 1))
                    score(score_n, b, 0)
                    score_n += 1
                elif stage in ("rope_flip", "dif_flip", "moe_flip"):
                    flip(stage, b, flip_n)
                    flip_n += 1
                elif stage in ("rope_pv", "dif_pv", "moe_pv"):
                    weigh(stage, b, pv_n)
                    pv_n += 1
                elif stage in ("rope_out", "moe_out"):
                    pe.wait_ge(S["ctx_ready"], NB * (2 if stage == "moe_out" else 0) + b + 1)
                    tokens((stage, b, 0), ctx_tile, [block_of("L0_attn_Wo") if stage == "rope_out" else block_of("L1_ffn_wo")])
                elif stage == "net_in":
                    pe.wait_ge(S["x_turned"], turned_count["x1", b])
                    for m in range(FC):
                        features((stage, b, m), block_of("L0_attn_W1", m), b)
                elif stage == "net_out":
                    pe.wait_ge(S["hid_ready"], 4 * (b + 1))
                    tokens((stage, b, 0), lambda k, i: hid[:, k, b % 2, TP * i:TP * i + TP],
                           [block_of("L0_attn_W2", m) for m in range(FC)])
                elif stage == "mix_in":
                    pe.wait_ge(S["x_turned"], turned_count["mix", b])
                    if b == 0:
                        pe.wait_ge(S["tri_made"], 2)
                    features((stage, b, 0), block_of("L0_ffn_W1"), b)
                elif stage == "mix_out":
                    pe.wait_ge(S["hid_ready"], 4 * NB + b + 1)
                    tokens((stage, b, 0), lambda k, i: hid[:, 0, b % 2, TP * i:TP * i + TP], [block_of("L0_ffn_W2")])
                elif stage == "dif_qk":
                    pe.wait_ge(S["x_turned"], turned_count["dif", b])
                    for j, w in enumerate(("L1_attn_Q1_w", "L1_attn_K1_w", "L1_attn_Q2_w", "L1_attn_K2_w")):
                        features((stage, b, j), block_of(w), b)
                elif stage == "dif_v":
                    values(stage, b, block_of("L1_attn_V_w"))
                elif stage in ("dif_scores", "dif_scores2"):
                    s = int(stage == "dif_scores2")
                    pe.wait_ge(S["q_ready"], NB + 2 * b + s + 1)
                    pe.wait_ge(S["k_ready"], 2 * NB + 4 * b + 2 * s + 2)
                    score(score_n, b, s)
                    score_n += 1
                elif stage == "gn_sum":
                    job = (stage, b, 0)
                    o = fill(pe, job)
                    pe.wait_ge(S["gn_stat"], gn_n[stage, b])
                    mm(o[:, 0:IB], const("group"), gn_s[:, 0, IB * b:IB * b + IB]).then_inc(filled(job), 1)
                elif stage == "gn_var":
                    job = (stage, b, 0)
                    o = fill(pe, job)
                    pe.wait_ge(S["gn_stat"], gn_n[stage, b])
                    mm(o[:, 0:IB], const("group"), gn_s[:, 2, IB * b:IB * b + IB]).then_inc(filled(job), 1)
                elif stage == "dif_out":
                    pe.wait_ge(S["square_ready"], square_n["gn_apply", b])
                    tokens((stage, b, 0), ctx_tile, [block_of("L1_attn_out_w")])
                elif stage == "moe_qk":
                    pe.wait_ge(S["x_turned"], turned_count["moe", b])
                    for j in range(2):
                        features((stage, b, j), block_of(("L1_ffn_wq", "L1_ffn_wk")[j]), b)
                elif stage == "moe_v":
                    values(stage, b, block_of("L1_ffn_wv"))
                elif stage == "moe_scores":
                    pe.wait_ge(S["q_ready"], 3 * NB + b + 1)
                    pe.wait_ge(S["k_ready"], 6 * NB + 2 * (b + 1))
                    score(score_n, b, 0)
                    score_n += 1
                elif stage == "rt_logits":
                    if b == 0:
                        pe.wait_ge(S["late_in"], 48)
                        pe.wait_ge(S["before_made"], 1)
                    pe.wait_ge(S["x_turned"], turned_count["rt", b])
                    tokens((stage, b, 0), lambda k, i: x_of(stage, b)[:, TP * i:TP * i + TP], [wr[:, :]], width=E)
                elif stage == "rt_count":
                    pe.wait_ge(S["picked"], b + 1)
                    pe.wait_ge(S["run_ready"], b + 1)
                    job = (stage, b, 0)
                    o = fill(pe, job)
                    for i in range(TPB):
                        to = o[0:TP, E * i:E * i + E]
                        mm(to, before16[:, :], oh_both[:, TPB * b + i, :], start=True, stop=False)
                        for j in range(i):
                            mm(to, ones16[:, :], oh_both[:, TPB * b + j, :], start=False, stop=False)
                        last = mm(to, ones16[:, :], run[:, b, :], start=False, stop=True)
                    last.then_inc(filled(job), 1)
                elif stage == "rt_map":
                    pe.wait_ge(S["mapped"], b + 1)
                    pe.wait_ge(S["paid"], b + 1)
                    job = (stage, b, 0)
                    o = fill(pe, job)
                    for i in range(TPB):
                        for k in range(2):
                            last = mm(o[:, 0:2 * ST], lo1[:, i, k, :], pay[:, i, k, :],
                                      start=(i == 0 and k == 0), stop=(i == TPB - 1 and k == 1))
                    last.then_inc(filled(job), 1)

            for kind, i in moe_order:
                job = (kind, i, 0)
                o = fill(pe, job)
                if kind == "take":
                    pe.wait_ge(got_here[i % NG], 16 * (i // NG + 1))
                    nc.tensor.transpose(o[:, 0:D], got[:, i % NG, :], const("ident")).then_inc(filled(job), 1)
                elif kind == "hidden":
                    e, s = i, i % RING
                    pe.wait_ge(S["xe_ready"], min(ST, (e * CAP + WIN - 1) // D + 1))
                    pe.wait_ge(w_here[s], 16 * (e // RING + 1))
                    for c in range(FC):
                        last = mm(o[:, WIN * c:WIN * c + WIN], ring[:, s, D * c:D * c + D], xe[:, CAP * e:CAP * e + WIN])
                    last.then_inc(filled(job), 1)
                elif kind == "expert":
                    e, s = i, i % RING
                    pe.wait_ge(S["h_full"], e + 1)
                    for c in range(FC):
                        last = mm(o[:, 0:WIN], ring[:, s, FF + D * c:FF + D * c + D], hT[:, e % 3, c, :], start=(c == 0), stop=(c == FC - 1))
                    last.then_inc(filled(job), 1)
                elif kind == "give":
                    pe.wait_ge(S["yT_ready"], min(E, -(-(i + 1) * D // CAP)))
                    nc.tensor.transpose(o[:, 0:D], yT[:, D * i:D * i + D], const("ident")).then_inc(filled(job), 1)
                elif kind == "bias_turn":
                    pe.wait_ge(S["gm_ready"], NB)
                    for t in range(TPB):
                        last = nc.tensor.transpose(o[0:E, TP * t:TP * t + TP], gm[:, TPB * i + t, :], const("ident")[0:TP, 0:TP])
                    last.then_inc(filled(job), 1)
                elif kind == "bias":
                    pe.wait_ge(S["gmT_ready"], i + 1)
                    for t in range(TPB):
                        last = mm(o[0:TP, D * t:D * t + D], gmT[:, i, TP * t:TP * t + TP], b2nat[:, :])
                    last.then_inc(filled(job), 1)

        @block.scalar
        def _(act):
            def go(o, i, f=ACT.Copy, **kw):
                return nc.scalar.activation(o, i, f, **kw)

            flip_n = 0
            soft_n = 0
            v_n = 0
            for stage, b in ORDER:
                name = stage.split("_")[0]
                tok = slice(TB * b, TB * b + TB)
                if stage == "rope_v" and b == NB - 1:
                    act.wait_ge(S["lam_ready"], 1)
                    go(lambdas[:, 0:2, :], lambdas[:, 0:2, :], ACT.Exp).then_inc(S["lam_ready"], 1)
                if stage == "tok_z":
                    if b == 0:
                        act.wait_ge(S["patch_weights_in"], 32)
                    job = (stage, b, 0)
                    o = read(act, job)
                    go(zraw[:, tok], o[:, 0:TB]).then_inc(S["z_raw"], 1)
                    go(tokT[:, tok], o[:, 0:TB], ACT.Identity, bias=tok_bias[:, 0:1]).then_inc(S["z_biased"], 1)
                elif stage == "tok_turn":
                    o = read(act, (stage, b, 0))
                    go(tiles(h, b), o[0:TP, 0:TPB * D].rearrange("p (n c) -> p n c", c=D)).then_inc(S["tok_back"], 1)
                elif stage.endswith("_norm_b"):
                    source = {"tok": h, "src": h, "x1": src, "x2": src, "mix": h, "dif": h, "moe": h, "rt": src}[name]
                    dst = {"tok": h, "src": src, "moe": src}.get(name, norm)
                    act.wait_ge(S["rstd_ready"], rstd_count[name, b])
                    for g in range(TPB * b, TPB * b + TPB):
                        last = go(dst[:, g, :], source[:, g, :], ACT.Identity, scale=rstd[:, g, 0:1], bias=rstd[:, g, 2:3])
                    if name == "moe":
                        last.then_inc(S["src_ready"], 1)
                        act.wait_ge(S["src_ready"], b + 1)
                        for g in range(TPB * b, TPB * b + TPB):
                            last = go(norm[:, g, :], src[:, g, :], ACT.Identity, scale=rstd[:, g, 1:2])
                    last.then_inc(S["normed"], 1)
                elif stage in ("src_turn", "mix_turn", "dif_turn"):
                    job = (stage, b, 0)
                    o = read(act, job)
                    dst, again, u = x_of(stage, b), None, o[:, 0:TB]
                    if stage != "mix_turn":
                        dst, again, u = xTp[:, b % 2, 0:IB, 0:SEQ], xTp[:, b % 2, IB, 0:SEQ], u.rearrange("p (i s) -> p i s", s=SEQ)
                        go(again, o[:, 0:SEQ])
                    go(dst, u).then_inc(S["x_turned"], 1)
                elif stage in ("x1_turn", "moe_turn", "rt_turn"):
                    g, be = {"x1": ("L0_attn_g1", "L0_attn_be1"), "moe": ("L1_ffn_ln1_g", "L1_ffn_ln1_b"),
                             "rt": ("L1_ffn_ln2_g", "L1_ffn_ln2_b")}[stage.split("_")[0]]
                    job = (stage, b, 0)
                    o = read(act, job)
                    dst, u = x_of(stage, b), o[:, 0:TB]
                    if stage == "moe_turn":
                        dst, u = xTp[:, b % 2, 0:IB, 0:SEQ], u.rearrange("p (i s) -> p i s", s=SEQ)
                        go(xTp[:, b % 2, IB, 0:SEQ], o[:, 0:SEQ], ACT.Identity, bias=col(be), scale=col(g))
                    go(dst, u, ACT.Identity, bias=col(be), scale=col(g)).then_inc(S["x_turned"], 1)
                elif stage == "rope_qk":
                    act.wait_ge(S["k_full"], b + 1)
                    for a in range(2):
                        go(kM[:, b % 2, 0, a, :], kT[:, b % 2, :], ACT.Identity, scale=const("parity")[:, a:a + 1]).then_inc(S["k_ready"], 1)
                elif stage in ("rope_v", "dif_v", "moe_v"):
                    if v_n == 0:
                        act.wait_ge(S["v_pads"], 1)
                    for half in range(2):
                        job = (stage, b, half)
                        o = read(act, job)
                        i0 = IB // 2 * half
                        for a in range(2):
                            r = slice(HALF * a, HALF * a + HALF)
                            v5 = vd[r, b % 2, :, :].rearrange("p i (q a d) -> p i q a d", q=QUADS, a=2)[:, :, :, a, :]
                            o5 = o[r, :].rearrange("p (i q a d) -> p i q a d", i=IB // 2, q=QUADS, a=2)[:, :, :, a, :]
                            n = IB // 2 - (1 if a and half else 0)
                            ins_ = go(v5[:, i0 + a:i0 + a + n], o5[:, 0:n])
                            if a and half:
                                ins_ = go(v5[:, 0], o5[:, n])
                            ins_.then_inc(S["v_ready"], 1)
                            v_n += 1
                elif stage in ("dif_qk", "moe_qk"):
                    if stage == "dif_qk" and b == 0:
                        act.wait_ge(S["mask_ready"], 4)
                    for j in range(JOBS[stage]):
                        job = (stage, b, j)
                        o = read(act, job)
                        s = j // 2
                        if j % 2 == 0:
                            ins_ = go(qT[:, b % 2, s, :], o[:, 0:TB])
                            ins_.then_inc(S["q_ready"], 1)
                        else:
                            for a in range(2):
                                if stage == "dif_qk":
                                    ins_ = go(kM[:, b % 2, s, a, :], o[:, 0:TB], ACT.Identity, scale=const("parity")[:, a:a + 1],
                                              bias=masked_bias[:, s, a:a + 1])
                                else:
                                    ins_ = go(kM[:, b % 2, s, a, :], o[:, 0:TB], ACT.Identity, scale=const("parity")[:, a:a + 1])
                                ins_.then_inc(S["k_ready"], 1)
                elif stage in ("rope_scores", "dif_scores", "dif_scores2", "moe_scores"):
                    act.wait_ge(S["exp_in"], soft_n + 1)
                    v = ex[0:SROWS, soft_n % 2, :, :]
                    go(v, v, ACT.Exp, scale=HD ** -0.5).then_inc(S["exp_done"], 1)
                    soft_n += 1
                elif stage in ("rope_flip", "dif_flip", "moe_flip"):
                    for p in range(PAIRS):
                        job = (stage, b, p)
                        o = read(act, job)
                        both = bass.AP(o[:, :].tensor, o[:, :].offset, [list(o[:, :].ap[0]), [SROWS, QUADS], [HALF, 2], [1, SEQ]])
                        go(pT[:, flip_n % 2, :, p, :, :], both).then_inc(S["pT_ready"], 1)
                    flip_n += 1
                elif stage in ("rope_pv", "dif_pv", "moe_pv"):
                    o = read(act, (stage, b, 0))
                    go(ctxT[:, tok], o[:, 0:TB]).then_inc(S["ctx_ready"], 1)
                elif stage == "gn_center":
                    act.wait_ge(S["gn_centred"], b + 1)
                    go(gn_q[:, b % 2, :], ctxT[:, tok], ACT.Square).then_inc(S["square_ready"], 1)
                elif stage == "gn_apply":
                    act.wait_ge(S["gn_scaled"], b + 1)
                    go(ctxT[:, tok], ctxT[:, tok], ACT.Identity, bias=col("L1_attn_gn_b")).then_inc(S["square_ready"], 1)
                elif stage == "net_in":
                    for m in range(0, FC):
                        job = (stage, b, m)
                        o = read(act, job)
                        go(hid[:, m, b % 2, :], o[:, 0:TB], ACT.Relu, bias=net_bias[:, m:m + 1]).then_inc(S["hid_ready"], 1)
                elif stage == "mix_in":
                    job = (stage, b, 0)
                    o = read(act, job)
                    go(hid[:, 0, b % 2, :], o[:, 0:TB], ACT.Gelu, bias=col("L0_ffn_b1")).then_inc(S["hid_ready"], 1)
                elif stage == "rt_logits":
                    o = read(act, (stage, b, 0))
                    go(tiles(lg, b), o[0:TP, 0:TPB * E].rearrange("p (n e) -> p n e", e=E)).then_inc(S["logits_back"], 1)
                elif stage == "rt_gate":
                    act.wait_ge(S["logits_ready"], b + 1)
                    t = slice(TPB * b, TPB * b + TPB)
                    go(gate[:, t, 2], gate[:, t, 3], ACT.Exp).then_inc(S["gate_exp"], 1)

            for kind, i in moe_order:
                job = (kind, i, 0)
                if kind == "hidden":
                    if i >= 3:
                        act.wait_ge(S["yT_ready"], i - 2)
                    o = read(act, job)
                    for c in range(FC):
                        ins_ = go(hT[:, i % 3, c, 0:CAP], o[:, WIN * c:WIN * c + CAP], ACT.Gelu_apprx_tanh, bias=b1T[:, c, i:i + 1])
                    ins_.then_inc(S["h_full"], 1)
                elif kind == "give":
                    if i >= 4:
                        act.wait_ge(ys_gone[i % 4], 16 * (i // 4))
                    o = read(act, job)
                    go(ys[:, i % 4, :], o[:, 0:D], ACT.Identity, scale=smap[:, ST + i:ST + i + 1]).then_inc(S["ys_ready"], 1)

        @block.vector
        def _(dve):
            v = nc.vector
            st = Steps(dve, S["dve_step"])
            v.memset(scores[:, :, :], 0.0).then_inc(S["scores_zero"], 1)
            moments_n = 0

            def moments(b, source):
                nonlocal moments_n
                if moments_n >= 2:
                    dve.wait_ge(S["var"], moments_n - 1)
                u = moments_n % 2
                moments_n += 1
                for i in range(TPB):
                    st.step(v.bn_stats(stats[:, u, i, :], source(i)))
                st.settle()
                for i in range(TPB):
                    last = v.bn_aggr(mv[:, TPB * b + i, :], stats[:, u, i, :])
                return last

            def of(t, b):
                return lambda i: t[:, TPB * b + i, :]

            soft_n = 0
            sums_n = 0
            flip_of = list(range(NB)) + [NB + b for b in range(NB) for _ in range(2)] + list(range(2 * NB, 3 * NB))
            for stage, b in ORDER:
                tok = slice(TB * b, TB * b + TB)
                name = stage.split("_")[0]
                t = slice(TPB * b, TPB * b + TPB)
                im = slice(IB * b, IB * b + IB)
                if stage == "tok_norm_a" and b == 1:
                    dve.wait_ge(S["lambdas_in"], 16)
                    st.link(v.tensor_tensor(lambdas[:, 0, :], lambdas[:, 0, :], lambdas[:, 1, :], ALU.mult))
                    v.tensor_tensor(lambdas[:, 1, :], lambdas[:, 2, :], lambdas[:, 3, :], ALU.mult).then_inc(S["lam_ready"], 1)
                if stage == "tok_shift":
                    job = (stage, b, 0)
                    dve.wait_ge(S["z_biased"], b + 1)
                    o = read(dve, job)
                    z, x = grid(o[:, 0:TB]), grid(tokT[:, tok])
                    n = GRID - 1
                    for q, (to, frm) in enumerate((((slice(0, GRID), slice(0, n)), (slice(0, GRID), slice(1, GRID))),
                                                   ((slice(0, GRID), slice(1, GRID)), (slice(0, GRID), slice(0, n))),
                                                   ((slice(0, n), slice(0, GRID)), (slice(1, GRID), slice(0, GRID))),
                                                   ((slice(1, GRID), slice(0, GRID)), (slice(0, n), slice(0, GRID))))):
                        p = slice(32 * q, 32 * q + 16)
                        last = v.tensor_tensor(x[p, :, to[0], to[1]], x[p, :, to[0], to[1]], z[p, :, frm[0], frm[1]], ALU.add)
                    last.then_inc(S["tok_added"], 1)
                elif stage == "tok_norm_a":
                    dve.wait_ge(S["tok_back"], b + 1)
                    moments(b, of(h, b)).then_inc(S["var"], 1)
                elif stage == "src_norm_a":
                    dve.wait_ge(S["h_norm"], b + 1)
                    moments(b, of(h, b)).then_inc(S["var"], 1)
                elif stage == "rope_qk":
                    if b >= 1:
                        dve.wait_ge(S["q_ready"], b)
                        dve.wait_ge(S["k_full"], b)
                    for n in range(2):
                        for dst, table, j in ((rot_a, "cos", 2 * n), (rot_b, "sin", 2 * n + 1)):
                            job = (stage, b, j)
                            o = read(dve, job)
                            v.tensor_tensor(dst[:, n, :].rearrange("p (i s) -> p i s", s=SEQ), o[:, 0:TB].rearrange("p (i s) -> p i s", s=SEQ),
                                            const(table).unsqueeze(1).broadcast_to([D, IB, SEQ]), ALU.mult).then_inc(S["rot_parts"], 1)
                elif stage in ("rope_scores", "dif_scores", "dif_scores2", "moe_scores"):
                    if stage == "dif_scores" and b == 0:
                        dve.wait_ge(S["lam_ready"], 2)
                        st.link(v.tensor_tensor(lam[:, :], lambdas[:, 0, :], lambdas[:, 1, :], ALU.subtract))
                        st.link(v.tensor_scalar(lam[:, :], lam[:, :], 0.2, None, ALU.add))
                    u = soft_n % 2
                    dve.wait_ge(S["s_full"], soft_n + 1)
                    sc = scores[0:SROWS, :, 0:SC].rearrange("p q (a k) -> p q a k", k=SEQ)
                    m3 = mx[:, u, :].rearrange("p (q a) -> p q a", q=QUADS)
                    st.link(v.tensor_reduce(m3, sc, AX_X, ALU.max))
                    if soft_n >= 2:
                        dve.wait_ge(S["probs_ready"], flip_of[soft_n - 2] + 1)
                        dve.wait_ge(S["half_scaled"], soft_n - 1)
                    e4 = ex[0:SROWS, u, :, :].rearrange("p q (a k) -> p q a k", k=SEQ)
                    v.tensor_tensor(e4, sc, m3.unsqueeze(3).broadcast_to([SROWS, QUADS, 2 * PAIRS, SEQ]), ALU.subtract
                                    ).then_inc(S["exp_in"], 1)
                    soft_n += 1
                elif stage in ("rope_sums", "dif_sums", "dif_sums2", "moe_sums"):
                    u = sums_n % 2
                    dve.wait_ge(S["exp_done"], sums_n + 1)
                    e4 = ex[0:SROWS, u, :, :].rearrange("p q (a k) -> p q a k", k=SEQ)
                    s3 = sm[:, u, :].rearrange("p (q a) -> p q a", q=QUADS)
                    st.link(v.tensor_reduce(s3, e4, AX_X, ALU.add))
                    if stage == "dif_sums2":
                        st.link(v.reciprocal(s3, s3))
                        s4 = sm[:, u, :].rearrange("p (q i a) -> p q i a", q=QUADS, a=2)
                        l4 = lam[:, :].rearrange("p (q a) -> p q a", a=2).unsqueeze(2).broadcast_to([SROWS, QUADS, PAIRS, 2])
                        v.tensor_tensor(s4, s4, l4, ALU.mult).then_inc(S["sums_ready"], 1)
                    else:
                        v.reciprocal(s3, s3).then_inc(S["sums_ready"], 1)
                    dve.wait_ge(S["sums_ready"], sums_n + 1)
                    f = flip_of[sums_n]
                    if stage[:3] != "dif" and f >= 2:
                        dve.wait_ge(S["pT_ready"], PAIRS * (f - 1))
                    for q in range(QUADS // 2, QUADS):
                        e3 = ex[0:SROWS, u, q, :].rearrange("p (a k) -> p a k", k=SEQ)
                        to = e3 if stage[:3] == "dif" else probs[0:SROWS, f % 2, q, :, :, 0:SEQ].rearrange("p a b k -> p (a b) k")
                        last = v.tensor_tensor(
                            to, e3, sm[:, u, 2 * PAIRS * q:2 * PAIRS * (q + 1)].unsqueeze(2).broadcast_to([SROWS, 2 * PAIRS, SEQ]), ALU.mult)
                    last.then_inc(S["half_scaled"], 1)
                    sums_n += 1
                elif stage == "dif_mix":
                    f = NB + b
                    dve.wait_ge(S["map_scaled"], 2 * (b + 1))
                    dve.wait_ge(S["half_scaled"], sums_n)
                    dve.wait_ge(S["pT_ready"], PAIRS * (f - 1))
                    for q in range(QUADS):
                        last = v.tensor_tensor(probs[0:SROWS, f % 2, q, :, :, 0:SEQ].rearrange("p a b k -> p (a b) k"),
                                               ex[0:SROWS, 0, q, :].rearrange("p (a k) -> p a k", k=SEQ),
                                               ex[0:SROWS, 1, q, :].rearrange("p (a k) -> p a k", k=SEQ), ALU.subtract)
                    last.then_inc(S["probs_ready"], 1)
                elif stage in ("rope_out", "net_out", "mix_out", "dif_out", "moe_out"):
                    job = (stage, b, 0)
                    if stage == "net_out":
                        dve.wait_ge(S["affine_ready"], b + 1)
                    if name in ("mix", "dif"):
                        dve.wait_ge(S["base_ready"], base_count[name + "_base", b])
                    o = read(dve, job)
                    base = {"rope": src, "net": mid, "mix": mid, "dif": mid, "moe": src}[name]
                    dst = {"rope": src, "net": src, "mix": h, "dif": h, "moe": src}[name]
                    last = v.tensor_tensor(dst[:, t, :], o[0:TP, 0:TPB * D].rearrange("p (n c) -> p n c", c=D), base[:, t, :], ALU.add)
                    last.then_inc(S["out_added"], 1)
                    dve.wait_ge(S["out_added"], out_count[stage, b])
                elif stage in ("x1_norm_a", "x2_norm_a", "rt_norm_a"):
                    moments(b, of(src, b)).then_inc(S["var"], 1)
                elif stage in ("mix_norm_a", "dif_norm_a", "moe_norm_a"):
                    moments(b, of(h, b)).then_inc(S["var"], 1)
                elif stage == "x2_norm_b":
                    dve.wait_ge(S["x2_ready"], b + 1)
                    st.link(v.tensor_tensor(h[:, t, :], h[:, t, :], norm[:, t, :], ALU.add))
                elif stage == "gn_sum":
                    dve.wait_ge(S["ctx_ready"], NB + b + 1)
                    v.tensor_reduce(gn_s[:, 0, im], ctxT[:, tok].rearrange("p (i s) -> p i s", s=SEQ), AX_X, ALU.add
                                    ).then_inc(S["gn_stat"], 1)
                elif stage == "gn_center":
                    c3 = ctxT[:, tok].rearrange("p (i s) -> p i s", s=SEQ)
                    o = read(dve, ("gn_sum", b, 0))
                    v.tensor_scalar(gn_s[:, 1, im], o[:, 0:IB], 1.0 / GSIZE, None, ALU.mult).then_inc(S["gn_mean_back"], 1)
                    dve.wait_ge(S["gn_mean_back"], b + 1)
                    v.tensor_tensor(c3, c3, gn_s[:, 1, im].unsqueeze(2).broadcast_to([D, IB, SEQ]), ALU.subtract
                                    ).then_inc(S["gn_centred"], 1)
                elif stage == "gn_var":
                    dve.wait_ge(S["square_ready"], square_n["gn_center", b])
                    v.tensor_reduce(gn_s[:, 2, im], gn_q[:, b % 2, :].rearrange("p (i s) -> p i s", s=SEQ), AX_X, ALU.add
                                    ).then_inc(S["gn_stat"], 1)
                elif stage == "gn_rstd":
                    o = read(dve, ("gn_var", b, 0))
                    v.tensor_scalar(gn_s[:, 3, im], o[:, 0:IB], 1.0 / GSIZE, None, ALU.mult).then_inc(S["gn_back"], 1)
                elif stage == "gn_apply":
                    dve.wait_ge(S["gn_ready"], b + 1)
                    c3 = ctxT[:, tok].rearrange("p (i s) -> p i s", s=SEQ)
                    v.tensor_tensor(c3, c3, gn_s[:, 3, im].unsqueeze(2).broadcast_to([D, IB, SEQ]), ALU.mult
                                    ).then_inc(S["gn_scaled"], 1)
                elif stage == "rt_logits":
                    dve.wait_ge(S["logits_back"], b + 1)
                    for g in range(TPB * b, TPB * b + TPB):
                        st.step(v.max(top[:, g, :], lg[:, g, :]))
                    st.settle()
                    v.tensor_tensor(gate[:, t, 3], top[:, t, 1], top[:, t, 0], ALU.subtract).then_inc(S["logits_ready"], 1)
                    for g in range(TPB * b, TPB * b + TPB):
                        st.step(v.max_index(top_i[:, g, :], top[:, g, :], lg[:, g, :]))
                    st.settle()
                    st.link(v.tensor_copy(top_f[:, t, :], top_i[:, t, 0:2]))
                    st.link(v.tensor_tensor(oh[:, t, :, :], const("iota_e", TP).unsqueeze(1).unsqueeze(1).broadcast_to([TP, TPB, 2, E]),
                                            top_f[:, t, :].unsqueeze(3).broadcast_to([TP, TPB, 2, E]), ALU.is_equal))
                    v.tensor_tensor(oh_both[:, t, :], oh[:, t, 0, :], oh[:, t, 1, :], ALU.add).then_inc(S["picked"], 1)
                elif stage == "rt_gate":
                    dve.wait_ge(S["gate_exp"], b + 1)
                    st.link(v.tensor_scalar(gate[:, t, 3], gate[:, t, 2], 1.0, None, ALU.add))
                    st.step(v.tensor_scalar(flat[:, t, :], top_f[:, t, :], float(CAP), None, ALU.mult))
                    st.link(v.reciprocal(gate[:, t, 0], gate[:, t, 3]))
                    st.link(v.tensor_tensor(gate[:, t, 1], gate[:, t, 2], gate[:, t, 0], ALU.mult))
                elif stage == "rt_count":
                    o = read(dve, (stage, b, 0))
                    cnt = o[0:TP, 0:TPB * E].rearrange("p (n e) -> p n e", e=E).unsqueeze(2).broadcast_to([TP, TPB, 2, E])
                    st.link(v.tensor_tensor(cum[:, :, :, :], cnt, oh[:, t, :, :], ALU.mult))
                    v.tensor_reduce(pos[:, t, :], cum[:, :, :, :], AX_X, ALU.add).then_inc(S["placed"], 1)
                    dve.wait_ge(S["placed"], b + 1)
                    st.step(v.tensor_scalar(far[:, t, :], pos[:, t, :], float(CAP), BEYOND, ALU.is_ge, ALU.mult))
                    st.step(v.tensor_scalar(kept[:, t, :], pos[:, t, :], float(CAP), None, ALU.is_lt))
                    st.link(v.tensor_tensor(flat[:, t, :], flat[:, t, :], pos[:, t, :], ALU.add))
                    st.link(v.tensor_tensor(flat_u[:, 0, t, :], flat[:, t, :], far[:, t, :], ALU.add))
                    st.step(v.tensor_scalar(flat_u[:, 1, t, :], flat_u[:, 0, t, :], 127, None, ALU.bitwise_and))
                    st.link(v.tensor_scalar(flat_u[:, 2, t, :], flat_u[:, 0, t, :], 7, None, ALU.logical_shift_right))
                    v.tensor_copy(flat_f[:, :, t, :], flat_u[:, 1:3, t, :]).then_inc(S["split"], 1)
                    dve.wait_ge(S["split"], b + 1)
                    if b >= 1:
                        dve.wait_ge(S["map_added"], b)
                    v.tensor_tensor(hi1[:, :, :, :], const("iota_hi", TP).unsqueeze(1).unsqueeze(1).broadcast_to([TP, TPB, 2, ST]),
                                    flat_f[:, 1, t, :].unsqueeze(3).broadcast_to([TP, TPB, 2, ST]), ALU.is_equal).then_inc(S["hi_ready"], 1)
                    v.tensor_tensor(lo1[:, :, :, :], const("iota_lo", TP).unsqueeze(1).unsqueeze(1).broadcast_to([TP, TPB, 2, D]),
                                    flat_f[:, 0, t, :].unsqueeze(3).broadcast_to([TP, TPB, 2, D]), ALU.is_equal).then_inc(S["mapped"], 1)
                elif stage == "rt_map":
                    o = read(dve, (stage, b, 0))
                    if b == 0:
                        last = v.tensor_copy(smap[:, :], o[:, 0:2 * ST])
                    else:
                        last = v.tensor_tensor(smap[:, :], smap[:, :], o[:, 0:2 * ST], ALU.add)
                    last.then_inc(S["map_added"], 1)

            dve.wait_ge(S["map_added"], NB)
            st.step(v.memset(xe[:, SLOTS:SLOTS + WIN], 0.0))
            st.step(v.memset(hT[:, :, :, CAP:WIN], 0.0))
            st.settle()
            st.step(v.tensor_scalar(smap2[:, 0, :], smap[:, 0:ST], 0.0, NOWHERE, ALU.is_equal, ALU.mult))
            st.step(v.tensor_scalar(get_u[:, 0, :], smap[:, 0:ST], 1.0, 1.0, ALU.max, ALU.subtract))
            st.settle()
            st.step(v.tensor_tensor(smap2[:, 1, :], smap2[:, 0, :], smap[:, 0:ST], ALU.add))
            st.step(v.tensor_scalar(get_u[:, 1, :], get_u[:, 0, :], 1, None, ALU.logical_shift_right))
            st.settle()
            v.tensor_scalar(put_u[:, :], smap2[:, 1, :], 1.0, None, ALU.subtract).then_inc(S["map_ready"], 1)
            for kind, i in moe_order:
                job = (kind, i, 0)
                if kind == "take":
                    o = read(dve, job)
                    v.tensor_copy(xe[:, D * i:D * i + D], o[:, 0:D]).then_inc(S["xe_ready"], 1)
                elif kind == "expert":
                    o = read(dve, job)
                    v.tensor_copy(yT[:, CAP * i:CAP * i + CAP], o[:, 0:CAP]).then_inc(S["yT_ready"], 1)
                elif kind == "bias_turn":
                    o = read(dve, job)
                    v.tensor_copy(gmT[:, i, :], o[0:E, 0:TB]).then_inc(S["gmT_ready"], 1)
                elif kind == "bias":
                    dve.wait_ge(S["h_summed"], NB)
                    o = read(dve, job)
                    t = slice(TPB * i, TPB * i + TPB)
                    v.tensor_tensor(h[:, t, :], o[0:TP, 0:TPB * D].rearrange("p (n c) -> p n c", c=D), h[:, t, :], ALU.add
                                    ).then_inc(S["bias_added"], 1)
            for b in range(NB):
                t = slice(TPB * b, TPB * b + TPB)
                dve.wait_ge(back_in[b], 16)
                y = back_of(b)
                st.link(v.tensor_tensor(res[:, t, :], h[:, t, :], y[:, :, 0:D], ALU.add))
                v.tensor_tensor(res[:, t, :], res[:, t, :], y[:, :, D:2 * D], ALU.add).then_inc(S["final_ready"], 1)


def kernel(**inputs):
    import numpy as _np
    import concourse.bacc as _bacc
    from concourse import mybir as _mybir
    from concourse.bass_utils import run_bass_kernel_spmd as _run

    nc = _bacc.Bacc("TRN2", target_bir_lowering=False, num_devices=1)
    arrays, args = {}, {}
    for name, value in packed({name: _np.asarray(a) for name, a in inputs.items()}).items():
        a = _np.ascontiguousarray(value)
        arrays[f"in_{name}"] = a
        args[name] = nc.dram_tensor(f"in_{name}", a.shape, _mybir.dt.from_np(a.dtype), kind="ExternalInput").ap()
    out = nc.dram_tensor("out_0", (IMG, SEQ, D), F32, kind="ExternalOutput").ap()
    build(nc, args, out)
    r = _run(nc, [arrays], core_ids=[0])
    return r.results[0]["out_0"]
```
